# Optimizing a Trainium2 kernel written in Bass

```python
import numpy as np
import jax
import jax.numpy as jnp

def _softmax(x, axis=-1):
    return jax.nn.softmax(x, axis=axis)

def _gelu(x):
    return jax.nn.gelu(x, approximate=True)

def _silu(x):
    return jax.nn.silu(x)

def _sigmoid(x):
    return jax.nn.sigmoid(x)

def _layernorm(x, axis=-1, eps=1e-05):
    m = jnp.mean(x, axis=axis, keepdims=True)
    v = jnp.var(x, axis=axis, keepdims=True)
    return (x - m) / jnp.sqrt(v + eps)

def _scatter_add(tgt, idx, src, axis=0):
    return tgt.at[idx].add(src)

def _segment_sum(src, seg, n):
    return jax.ops.segment_sum(src, seg, n)
kernel_name = 'mk_gnn_resnorm_d2_gnn_r8_7e2000'

def setup_inputs(seed: int=0):
    np.random.seed(seed)
    _w = jnp.asarray

    def _rec_inputs():
        import jax
        import jax.numpy as jnp
        _gk = jax.random.key(seed)
        x = -0.0003713 + 1 * jax.random.normal(jax.random.fold_in(_gk, 1), (12500, 256), jnp.float32)
        src = jax.random.randint(jax.random.fold_in(_gk, 2), (200000,), 0, 12500, jnp.int32)
        dst = jax.random.randint(jax.random.fold_in(_gk, 3), (200000,), 0, 12500, jnp.int32)
        _o = jnp.argsort(dst, stable=True)
        src = src[_o]
        dst = dst[_o]
        edge_attr_4 = 0.000126197 + 0.999763 * jax.random.normal(jax.random.fold_in(_gk, 11), (200000, 4), jnp.float32)
        edge_attr_8 = jax.random.uniform(jax.random.fold_in(_gk, 12), (200000, 8), jnp.float32, 0.0, 1)
        return (x, src, dst, edge_attr_4, edge_attr_8)
    x, src, dst, edge_attr_4, edge_attr_8 = _rec_inputs()

    def _L0_gnn_setup():
        import jax, jax.numpy as jnp
        import numpy as np
        N_NODES = 6250
        N_EDGES = 100000
        IN_DIM = 256
        HEADS = 4
        OUT_DIM = 64
        NEG_SLOPE = 0.2
        EPS = 1e-16
        key = jax.random.key(seed)
        ks = jax.random.split(key, 6)
        x = jax.random.normal(ks[0], (N_NODES, IN_DIM), dtype=jnp.float32)
        edge_index = jax.random.randint(ks[1], (2, N_EDGES), 0, N_NODES, dtype=jnp.int64)
        W = jax.random.normal(ks[2], (IN_DIM, HEADS * OUT_DIM), dtype=jnp.float32) * 0.05
        att_src = jax.random.normal(ks[3], (HEADS, OUT_DIM), dtype=jnp.float32) * 0.05
        att_dst = jax.random.normal(ks[4], (HEADS, OUT_DIM), dtype=jnp.float32) * 0.05
        bias = jnp.zeros((HEADS * OUT_DIM,), dtype=jnp.float32)
        skip_W = jax.random.normal(ks[5], (IN_DIM, HEADS * OUT_DIM), dtype=jnp.float32) * 0.05
        return {'x': x, 'edge_index': edge_index, 'W': W, 'att_src': att_src, 'att_dst': att_dst, 'bias': bias, 'skip_W': skip_W}
    _L0_gnn_all = _L0_gnn_setup()
    _L0_gnn_in = {k: v for k, v in _L0_gnn_all.items() if k in ('W', 'att_src', 'att_dst', 'bias', 'skip_W')}
    del _L0_gnn_all

    def _L1_gnn_setup():
        import jax, jax.numpy as jnp
        import numpy as np
        N_NODES = 2500
        N_EDGES = 40000
        MUL = 64
        NUM_BASIS = 8
        INV_SQRT3 = 0.5773502691896258
        EPS = 1e-05
        key = jax.random.key(seed)
        k = jax.random.split(key, 16)
        return {'node_hiddens': jax.random.normal(k[0], (N_NODES, 4 * MUL), dtype=jnp.float32), 'edge_attr': jax.random.uniform(k[1], (N_EDGES, NUM_BASIS), dtype=jnp.float32), 'edge_sh': jax.random.normal(k[2], (N_EDGES, 4), dtype=jnp.float32), 'w1_s': jax.random.normal(k[3], (MUL, MUL), dtype=jnp.float32), 'w1_v': jax.random.normal(k[4], (MUL, MUL), dtype=jnp.float32), 'wsc_s': jax.random.normal(k[5], (MUL, MUL), dtype=jnp.float32), 'wsc_v': jax.random.normal(k[6], (MUL, MUL), dtype=jnp.float32), 'w2_s': jax.random.normal(k[7], (2 * MUL, MUL), dtype=jnp.float32), 'w2_v': jax.random.normal(k[8], (2 * MUL, MUL), dtype=jnp.float32), 'fc_w1': jax.random.normal(k[9], (NUM_BASIS, 64), dtype=jnp.float32), 'fc_w2': jax.random.normal(k[10], (64, 64), dtype=jnp.float32), 'fc_w3': jax.random.normal(k[11], (64, 4 * MUL), dtype=jnp.float32), 'g_s': jnp.ones((MUL,), dtype=jnp.float32), 'g_v': jnp.ones((MUL,), dtype=jnp.float32), 'edge_index': jax.random.randint(k[12], (2, N_EDGES), 0, N_NODES)}
    _L1_gnn_all = _L1_gnn_setup()
    _L1_gnn_in = {k: v for k, v in _L1_gnn_all.items() if k in ('w1_s', 'w1_v', 'wsc_s', 'wsc_v', 'w2_s', 'w2_v', 'fc_w1', 'fc_w2', 'fc_w3', 'g_s', 'g_v')}
    del _L1_gnn_all
    return {'x': x, 'src': src, 'dst': dst, 'edge_attr_4': edge_attr_4, 'edge_attr_8': edge_attr_8, 'L0_gnn_W': _L0_gnn_in['W'], 'L0_gnn_att_src': _L0_gnn_in['att_src'], 'L0_gnn_att_dst': _L0_gnn_in['att_dst'], 'L0_gnn_bias': _L0_gnn_in['bias'], 'L0_gnn_skip_W': _L0_gnn_in['skip_W'], 'L1_gnn_w1_s': _L1_gnn_in['w1_s'], 'L1_gnn_w1_v': _L1_gnn_in['w1_v'], 'L1_gnn_wsc_s': _L1_gnn_in['wsc_s'], 'L1_gnn_wsc_v': _L1_gnn_in['wsc_v'], 'L1_gnn_w2_s': _L1_gnn_in['w2_s'], 'L1_gnn_w2_v': _L1_gnn_in['w2_v'], 'L1_gnn_fc_w1': _L1_gnn_in['fc_w1'], 'L1_gnn_fc_w2': _L1_gnn_in['fc_w2'], 'L1_gnn_fc_w3': _L1_gnn_in['fc_w3'], 'L1_gnn_g_s': _L1_gnn_in['g_s'], 'L1_gnn_g_v': _L1_gnn_in['g_v']}

def reference(x, src, dst, edge_attr_4, edge_attr_8, L0_gnn_W, L0_gnn_att_src, L0_gnn_att_dst, L0_gnn_bias, L0_gnn_skip_W, L1_gnn_w1_s, L1_gnn_w1_v, L1_gnn_wsc_s, L1_gnn_wsc_v, L1_gnn_w2_s, L1_gnn_w2_v, L1_gnn_fc_w1, L1_gnn_fc_w2, L1_gnn_fc_w3, L1_gnn_g_s, L1_gnn_g_v):
    import jax
    import jax.numpy as jnp

    def _L0_gnn_ref(x, edge_index, W, att_src, att_dst, bias, skip_W):
        import jax, jax.numpy as jnp
        import numpy as np
        N_NODES = 6250
        N_EDGES = 100000
        IN_DIM = 256
        HEADS = 4
        OUT_DIM = 64
        NEG_SLOPE = 0.2
        EPS = 1e-16
        N = x.shape[0]
        H, C = att_src.shape
        loops = jnp.arange(N, dtype=edge_index.dtype)
        src = jnp.concatenate([edge_index[0], loops])
        dst = jnp.concatenate([edge_index[1], loops])
        h = (x @ W).reshape(N, H, C)
        a_src = jnp.einsum('nhc,hc->nh', h, att_src)
        a_dst = jnp.einsum('nhc,hc->nh', h, att_dst)
        e = a_src[src] + a_dst[dst]
        e = jnp.where(e > 0, e, NEG_SLOPE * e)
        e_max = jax.ops.segment_max(e, dst, num_segments=N)
        alpha = jnp.exp(e - e_max[dst])
        denom = jax.ops.segment_sum(alpha, dst, num_segments=N)
        alpha = alpha / (denom[dst] + EPS)
        msg = h[src] * alpha[:, :, None]
        agg = jax.ops.segment_sum(msg, dst, num_segments=N)
        out = agg.reshape(N, H * C) + bias
        out = out + x @ skip_W
        out = jax.nn.elu(out)
        return out

    def _L1_gnn_ref(node_hiddens, edge_attr, edge_sh, w1_s, w1_v, wsc_s, wsc_v, w2_s, w2_v, fc_w1, fc_w2, fc_w3, g_s, g_v, edge_index):
        import jax, jax.numpy as jnp
        import numpy as np
        N_NODES = 2500
        N_EDGES = 40000
        MUL = 64
        NUM_BASIS = 8
        INV_SQRT3 = 0.5773502691896258
        EPS = 1e-05
        N = node_hiddens.shape[0]
        xs = node_hiddens[:, :MUL]
        xv = node_hiddens[:, MUL:].reshape(N, MUL, 3)
        h = jax.nn.silu(edge_attr @ fc_w1 * (1.0 / np.sqrt(float(NUM_BASIS))))
        h = jax.nn.silu(h @ fc_w2 * (1.0 / np.sqrt(64.0)))
        w = h @ fc_w3 * (1.0 / np.sqrt(64.0))
        wA, wB, wC, wD = jnp.split(w, 4, axis=1)
        inv = 1.0 / np.sqrt(float(MUL))
        sc_s = xs @ wsc_s * inv
        sc_v = jnp.einsum('nud,uv->nvd', xv, wsc_v) * inv
        ys = xs @ w1_s * inv
        yv = jnp.einsum('nud,uv->nvd', xv, w1_v) * inv
        src = edge_index[0]
        dst = edge_index[1]
        es = ys[dst]
        ev = yv[dst]
        sh0 = edge_sh[:, :1]
        sh1 = edge_sh[:, 1:]
        m0a = wA * es * sh0
        m0b = wD * jnp.einsum('eud,ed->eu', ev, sh1) * INV_SQRT3
        m1a = wB[:, :, None] * es[:, :, None] * sh1[:, None, :]
        m1b = wC[:, :, None] * ev * sh0[:, :, None]
        mid_s = jnp.concatenate([m0a, m0b], axis=1)
        mid_v = jnp.concatenate([m1a, m1b], axis=1)
        ns = jax.ops.segment_sum(mid_s, src, num_segments=N)
        nv = jax.ops.segment_sum(mid_v, src, num_segments=N)
        deg = jax.ops.segment_sum(jnp.ones((src.shape[0],), node_hiddens.dtype), src, num_segments=N)
        dn = jax.lax.rsqrt(jnp.maximum(deg, 1.0))
        ns = ns * dn[:, None]
        nv = nv * dn[:, None, None]
        inv2 = 1.0 / np.sqrt(2.0 * MUL)
        os_ = ns @ w2_s * inv2 + sc_s
        ov = jnp.einsum('nud,uv->nvd', nv, w2_v) * inv2 + sc_v
        os_ = os_ * jax.lax.rsqrt(jnp.mean(os_ * os_, axis=1, keepdims=True) + EPS) * g_s
        rms_v = jax.lax.rsqrt(jnp.mean(ov * ov, axis=(1, 2))[:, None, None] + EPS)
        ov = ov * rms_v * g_v[None, :, None]
        return jnp.concatenate([os_, ov.reshape(N, 3 * MUL)], axis=1)
    edge_index = jnp.stack([src, dst])
    x = _layernorm(x + _L0_gnn_ref(x, edge_index, L0_gnn_W, L0_gnn_att_src, L0_gnn_att_dst, L0_gnn_bias, L0_gnn_skip_W), axis=-1)
    x = _layernorm(x + _L1_gnn_ref(x, edge_attr_8, edge_attr_4, L1_gnn_w1_s, L1_gnn_w1_v, L1_gnn_wsc_s, L1_gnn_wsc_v, L1_gnn_w2_s, L1_gnn_w2_v, L1_gnn_fc_w1, L1_gnn_fc_w2, L1_gnn_fc_w3, L1_gnn_g_s, L1_gnn_g_v, edge_index), axis=-1)
    return x

_drawn_inputs = setup_inputs


def setup_inputs(seed=0):
    import zlib

    import numpy as np

    out = dict(_drawn_inputs(seed))
    spreads = {'L0_gnn_bias': (0.0, 0.1), 'L1_gnn_g_s': (1.0, 0.2), 'L1_gnn_g_v': (1.0, 0.2)}
    factors = {}
    for name, (base, spread) in spreads.items():
        noise = np.random.default_rng([zlib.crc32(name.encode()), seed]).standard_normal(out[name].shape)
        drawn = base * np.exp(spread * noise) if base else spread * noise
        out[name] = jnp.asarray(drawn.astype(out[name].dtype))
    for name, factor in factors.items():
        out[name] = (out[name] * factor).astype(out[name].dtype)
    return out
```

```python
from contextlib import ExitStack

import numpy as np
import concourse.bass as bass
from concourse import mybir

F32 = mybir.dt.float32
BF16 = mybir.dt.bfloat16
I32 = mybir.dt.int32
ALU = mybir.AluOpType
ACT = mybir.ActivationFunctionType
AX = mybir.AxisListType
RMAX = bass.bass_isa.ReduceOp.max
ds = bass.ds

P = 128
NO_NODE = 1 << 20
GROUP = 4
PAIR = 2
CHUNK = 7
TURN = 4


def sizes(n_nodes, n_edges):
    nb = -(-n_nodes // (P * 2 * CHUNK)) * 2 * CHUNK
    ew = -(-n_edges // P)
    t = -(-(ew + nb - 1) // P) * P
    return nb, nb * P, ew, t


def wait(eng, s, value):
    if not (isinstance(value, int) and value <= 0):
        eng.wait_ge(s, value)


def wait_apart(eng, s, value):
    if not (isinstance(value, int) and value <= 0):
        eng.wait_ge(s, value)
        eng.nop(nofuse=True)


def landed(g, slot, dmas=1):
    return dmas * (16 // TURN * g + 16 - 16 // TURN * slot)


def steps(eng, n, lead, step):
    first, last = 2 * TURN, (n - 2) // TURN * TURN
    for g in range(-lead, first):
        step(g, g % TURN, lambda v: 0 <= v < n)
    with eng.Fori(first // TURN, last // TURN) as i:
        for slot in range(TURN):
            step(i * TURN + slot, slot, lambda v: True)
    for g in range(last, n + 2):
        step(g, g % TURN, lambda v: 0 <= v < n)


def bass_gat_equivariant_kernel(nc, x, xT, edges_sd, window_ends, ea8, ea4, W, WT, att_src, att_dst, bias, skip_W,
                                w1_s, w1_v, wsc_s, wsc_v, w2_s, w2_v, fc_w1, fc_w2, fc_w3, g_s, g_v, out,
                                n_nodes, n_edges):
    NB, NP, EW, T = sizes(n_nodes, n_edges)
    D = x.shape[1]
    H, C = att_src.shape
    MUL = w1_s.shape[0]
    NBAS = fc_w1.shape[0]
    HW = D + H
    WR = D + 4
    OR = D + 4
    NG, NU, NC = T // GROUP, T // PAIR, T // P
    SLOPE, EPS = 0.2, 1e-5
    S8, S64 = float(1 / np.sqrt(float(NBAS))), float(1 / np.sqrt(float(MUL)))
    INV_SQRT3 = 0.5773502691896258
    assert D == 256 and H * C == D and MUL == C == 64 and NBAS == 8 and NB <= P and D == 4 * MUL

    def dram(name, shape, dt):
        return nc.dram_tensor(name, shape, dt).ap()

    h_tab = dram("h_tab", [NP, HW], F32)
    w_tab = dram("w_tab", [T * P, WR], F32)
    ot_tab = dram("ot_tab", [NU, P, PAIR * P], BF16)
    x1_tab = dram("x1_tab", [NP, 2 * D], F32)
    part = [dram(f"part{k}", [NP + P, OR], F32) for k in range(GROUP)]

    with ExitStack() as ctx:
        def sb(name, shape, dt=F32):
            return ctx.enter_context(nc.sbuf_tensor(name, shape, dt))

        def sem(name):
            return ctx.enter_context(nc.semaphore(name))

        def sems(prefix, names):
            return [sem(f"{prefix}_{n}") for n in names.split()]

        PS = ctx.enter_context(nc.psum_tensor("PS", [P, 8, 512], F32))

        ident = sb("ident", [P, P])
        iota_n = sb("iota_n", [P, P])
        upper = sb("upper", [P, P])
        lower_eq = sb("lower_eq", [P, P])
        ones = sb("ones", [P, P])
        zeros = sb("zeros", [P, 3 * OR])
        part_no = sb("part_no", [P, 1])
        trash = sb("trash", [P, 1])
        half = sb("half", [P, 2])
        Wx = sb("Wx", [P, 2, D + 2 * H])
        WTs = sb("WTs", [P, 2, D])
        att = sb("att", [P, 2, 2 * H])
        skw = sb("skw", [P, 2, D])
        brow = sb("brow", [1, D])
        w1m = sb("w1m", [P, 2, P])
        wscm = sb("wscm", [P, 2, P])
        w2m = sb("w2m", [P, 2, MUL])
        fc1 = sb("fc1", [2 * NBAS, P])
        fc2 = sb("fc2", [P, P])
        fc3 = sb("fc3", [P, D])
        gfull = sb("gfull", [P, D])

        logits = sb("logits", [P, NB, 3 * H])
        lt = sb("lt", [P, NB, 2 * H])
        ac3 = sb("ac3", [P, NB, 3, 2 * H], BF16)
        pself = sb("pself", [P, NB, H])
        rden = sb("rden", [P, NB, H])
        amax = sb("amax", [P, H])
        gmax = sb("gmax", [P, H])
        srcF = sb("srcF", [P, T])
        dloc = sb("dloc", [P, T], BF16)
        valid = sb("valid", [P, T], BF16)
        rows = sb("rows", [33, T], I32)
        block_row, window_row = rows[0:1, :], rows[32:33, :]

        BIG = max(NB * HW, 2 * EW + 2 * T + 4 * NC * P)
        big = sb("big", [P, BIG])
        acc = big[:, 0:NB * HW].rearrange("p (b d) -> p b d", d=HW)
        ARENA = 9400
        arena = sb("arena", [P, ARENA])
        used = [0]

        def cut(n, new_stage=False):
            at = 0 if new_stage else used[0]
            used[0] = at + n
            assert used[0] <= ARENA
            return arena[:, at:at + n]

        ends = big[0:NB, 0:2 * EW].rearrange("p (s w) -> p s w", s=2)
        iota_t = big[:, 2 * EW:2 * EW + T]
        stepm = big[0:NB, 2 * EW + T:2 * EW + 2 * T]
        at = 2 * EW + 2 * T
        sd_in = big[:, at:at + 2 * NC * P].bitcast(I32).rearrange("p (c w e) -> p c w e", c=NC, w=2)
        sd_f = big[:, at + 2 * NC * P:at + 4 * NC * P].rearrange("p (c w e) -> p c w e", c=NC, w=2)
        x_in = cut(4 * CHUNK * P, True).rearrange("p (s k n) -> p s k n", s=2, k=2)
        h_out = cut(2 * CHUNK * HW).rearrange("p (s k d) -> p s k d", s=2, k=CHUNK)
        bounds = sb("bounds", [P, 2])
        cnt = sb("cnt", [P, 8])
        two = sb("two", [P, 33])
        b128 = sb("b128", [P, NC])
        tile_col = sb("tile_col", [P, NC])
        wcol = sb("wcol", [P, NC], I32)

        hg = cut(TURN * GROUP * HW, True).rearrange("p (s k d) -> p s k d", s=TURN, k=GROUP)
        oh = cut(2 * GROUP * P).rearrange("p (s k n) -> p s k n", s=2, k=GROUP)
        ots = cut(GROUP * P).bitcast(BF16).rearrange("p (s k e) -> p s k e", s=2, k=GROUP)
        wst = cut(2 * GROUP * WR).rearrange("p (s k d) -> p s k d", s=2, k=GROUP)
        eat = cut(2 * 2 * P).rearrange("p (s e) -> p s e", s=2)
        h1 = cut(2 * 2 * P).rearrange("p (s e) -> p s e", s=2)
        h2 = cut(2 * 2 * P).rearrange("p (s e) -> p s e", s=2)
        sidx = sb("sidx", [P, TURN, GROUP], I32)
        za = sb("za", [P, 2, GROUP, H])
        zb = sb("zb", [P, 2, GROUP, H])
        sh = sb("sh", [P, TURN, GROUP, 4])

        b_h = cut(TURN * D, True).rearrange("p (s d) -> p s d", s=TURN)
        b_x = cut(TURN * D).rearrange("p (s d) -> p s d", s=TURN)
        b_xT = cut(TURN * 2 * P).rearrange("p (s k n) -> p s k n", s=TURN, k=2)
        b_v = cut(TURN * D).rearrange("p (s d) -> p s d", s=TURN)
        b_e = cut(TURN * D).rearrange("p (s d) -> p s d", s=TURN)
        b_x1 = cut(TURN * 2 * D).rearrange("p (s d) -> p s d", s=TURN)
        b_x1T = cut(2 * 2 * P).rearrange("p (s k n) -> p s k n", s=2, k=2)
        stat = sb("stat", [P, TURN, 6])
        mv = sb("mv", [P, TURN, 4])

        wt = cut(TURN * PAIR * WR, True).rearrange("p (s k d) -> p s k d", s=TURN, k=PAIR)
        c_ot = cut(TURN * PAIR * P // 2).bitcast(BF16).rearrange("p (s k e) -> p s k e", s=TURN, k=PAIR)
        c_otf = cut(2 * PAIR * P).rearrange("p (s k e) -> p s k e", s=2, k=PAIR)
        mid = cut(2 * PAIR * 2 * D).rearrange("p (s k c u) -> p s k c u", s=2, k=PAIR, c=8)
        midT = cut(PAIR * 4 * P).rearrange("p (k c e) -> p k c e", k=PAIR, c=4)
        same = cut(2 * PAIR * P).rearrange("p (s k e) -> p s k e", s=2, k=PAIR)
        o_sb = cut(PAIR * OR).rearrange("p (k d) -> p k d", k=PAIR)
        o_cmb = cut(GROUP * OR).rearrange("p (k d) -> p k d", k=GROUP)
        evs = cut(PAIR * 3 * MUL).rearrange("p (k d u) -> p k d u", k=PAIR, d=3)
        evt = cut(PAIR * MUL).rearrange("p (k u) -> p k u", k=PAIR)
        c_src = sb("c_src", [P, TURN, PAIR])
        c_val = sb("c_val", [P, TURN, PAIR])
        c_cnt = sb("c_cnt", [P, TURN, PAIR])
        c_d = sb("c_d", [P, TURN, PAIR])
        c_idx = sb("c_idx", [P, TURN, PAIR], I32)

        d_p = cut(TURN * GROUP * OR, True).rearrange("p (s k d) -> p s k d", s=TURN, k=GROUP)
        d_x = cut(TURN * 2 * D).rearrange("p (s d) -> p s d", s=TURN)
        d_o = cut(TURN * D).rearrange("p (s d) -> p s d", s=TURN)
        d_q = cut(D)
        d_z = cut(TURN * D).rearrange("p (s d) -> p s d", s=TURN)
        d_out = b_out = sb("d_out", [P, TURN, D])
        d_n = sb("d_n", [P, TURN, 8])

        (s_iota, s_zeroed, s_const, s_w, s_scaled, s_ends, s_tab, s_tabp, s_win, s_watt, s_hwatt, s_zero) = sems(
            "s", "iota zeroed const w scaled ends tab tabp win watt hwatt zero")
        s_xin = sems("s_xin", "0 1")
        s_hst = sems("s_hst", "0 1")
        s_hps, s_hev, s_sdin, s_sdf, s_sdp, s_sdT, s_amax, s_gmax, s_lg, s_self, s_acc0, s_dl = sems(
            "s", "hps hev sdin sdf sdp sdT amax gmax lg self acc0 dl")
        s_idx, s_oh, s_otp, s_ots, s_ad, s_z, s_p, s_msg, s_agg, s_acc, s_f1, s_h1, s_f2, s_h2, s_f3, s_wev = sems(
            "a", "idx oh otp ots ad z p msg agg acc f1 h1 f2 h2 f3 wev")
        slots = "0 1 2 3"
        s_hg, s_otst, s_ea, s_wst = sems("a_hg", slots), sems("a_otst", slots), sems("a_ea", slots), sems("a_wst", slots)
        (s_rden, s_bt, s_bsum, s_bskip, s_bv, s_bm, s_be, s_belu, s_bs, s_bmv, s_brstd, s_bx1, s_bxp, s_bxT, s_by,
         s_bout) = sems("b", "rden t sum skip v m e elu s mv rstd x1 xp xT y out")
        s_bin, s_bst = sems("b_in", slots), sems("b_st", slots)
        (s_csl, s_cotf, s_cy, s_csr, s_csame, s_cix, s_cpr, s_cmid, s_cmt, s_cmT, s_co, s_cosb, s_cc, s_ccmb) = sems(
            "c", "sl otf y sr same ix pr mid mt mT o osb c cmb")
        s_cw, s_cot, s_add = sems("c_w", slots), sems("c_ot", slots), sems("c_add", slots)
        (s_dsum, s_ddeg, s_ddn, s_do, s_dsq, s_dms, s_drs, s_dn, s_dz, s_dmv, s_drstd, s_dout) = sems(
            "d", "sum deg dn o sq ms rs n z mv rstd out")
        s_din, s_dst = sems("d_in", slots), sems("d_st", slots)

        block = ctx.enter_context(nc.Block())
        TAB_WINDOWS, TAB_STEPS = 5, 8
        LG_PARTS, LG_SELF = 6, 9
        N_W = 2 + 2 * H + 2 + 8 + 2 + 2 * 6 + 4
        NCH = NB // CHUNK
        xv = xT.rearrange("(k p) n -> p k n", p=P)
        x1b = x1_tab.rearrange("(b p) d -> b p d", p=P)

        def one(v, i):
            return v[ds(i, 1)].rearrange("o p d -> (o p) d")

        @block.sync
        def _(sp):
            loads = [0]

            def load(to, what):
                sp.dma_start(to, what).then_inc(s_w, 16)
                loads[0] += 1

            sp.dma_start(ends.bitcast(I32), window_ends.rearrange("(o s) w -> o s w", o=1).to_broadcast([NB, 2, EW])
                         ).then_inc(s_ends, 16)
            load(WTs[:, :, :], WT.rearrange("(k p) n -> p k n", p=P))
            load(Wx[:, :, 0:D], W.rearrange("(k p) n -> p k n", p=P))
            sp.wait_ge(s_zeroed, 1)
            for h in range(H):
                at = h % 2 * C
                load(att[at:at + C, h // 2, h:h + 1], att_src[h].rearrange("(c o) -> c o", o=1))
                load(att[at:at + C, h // 2, H + h:H + h + 1], att_dst[h].rearrange("(c o) -> c o", o=1))
            load(skw[:, :, :], skip_W.rearrange("(k p) n -> p k n", p=P))
            load(brow[:, :], bias.rearrange("(o n) -> o n", o=1))
            for m, s_part, v_part in ((w1m, w1_s, w1_v), (wscm, wsc_s, wsc_v)):
                load(m[0:MUL, 0, 0:MUL], s_part)
                load(m[MUL:P, 0, MUL:P], v_part)
                load(m[0:MUL, 1, 0:MUL], v_part)
                load(m[MUL:P, 1, MUL:P], v_part)
            load(w2m[:, 0, :], w2_s)
            load(w2m[:, 1, :], w2_v)
            for i in range(2):
                load(fc1[i * NBAS:(i + 1) * NBAS, i * MUL:(i + 1) * MUL], fc_w1)
                load(fc2[i * MUL:(i + 1) * MUL, i * MUL:(i + 1) * MUL], fc_w2)
                for to, of in ((0, 0), (1, 2), (2, 1), (3, 3)):
                    load(fc3[i * MUL:(i + 1) * MUL, to * MUL:(to + 1) * MUL], fc_w3[:, of * MUL:(of + 1) * MUL])
            load(gfull[:, 0:MUL], g_s.rearrange("(o n) -> o n", o=1).to_broadcast([P, MUL]))
            for d in range(1, 4):
                load(gfull[:, MUL * d:MUL * (d + 1)], g_v.rearrange("(o n) -> o n", o=1).to_broadcast([P, MUL]))
            assert loads[0] == N_W

            def load_x(c, s, before):
                wait(sp, s_hps, before)
                sp.dma_start(x_in[:, s, :, :], xv[:, :, ds(c * (CHUNK * P), CHUNK * P)]).then_inc(s_xin[s], 16)

            for c in range(2):
                load_x(c, c, 0)
            with sp.Fori(1, NCH // 2) as i:
                for s in range(2):
                    load_x(i * 2 + s, s, (i * 2 + s - 1) * CHUNK)

            sp.wait_ge(s_hst[0], 16 * (NCH // 2))
            sp.wait_ge(s_hst[1], 16 * (NCH // 2))
            sp.wait_ge(s_sdp, NC)

            def step_a(g, s, there):
                n = (s + 1) % TURN
                if there(g + 1):
                    wait(sp, s_f1, g)
                    sp.dma_start(eat[0:2 * NBAS, n % 2, :], one(ea8, g + 1)).then_inc(s_ea[n], 16)
                    wait(sp, s_wev, GROUP * (g - 2))
                    sp.dma_start(sh[:, n, :, :], ea4[:, ds((g + 1) * GROUP, GROUP), :]).then_inc(s_ea[n], 16)
                if there(g):
                    wait(sp, s_ots, g + 1)
                    sp.dma_start(ot_tab[ds(g * 2, 2), :, :].rearrange("q p e -> p q e"),
                                 ots[:, s % 2, :, :].rearrange("p (q k) e -> p q (k e)", q=2)).then_inc(s_otst[s], 16)
                    wait(sp, s_wev, GROUP * (g + 1))
                    sp.dma_start(w_tab[ds(g * (GROUP * P), GROUP * P), :].rearrange("(k p) d -> p k d", p=P),
                                 wst[:, s % 2, :, :]).then_inc(s_wst[s], 16)

            steps(sp, NG, 1, step_a)
            for s in range(TURN):
                sp.wait_ge(s_wst[s], 16 * (NG // TURN))
                sp.wait_ge(s_otst[s], 16 * (NG // TURN))

            sp.wait_ge(s_acc, GROUP * NG)
            xb = x.rearrange("(b p) d -> b p d", p=P)
            hb = h_tab.rearrange("(b p) d -> b p d", p=P)

            def step_b(b, s, there):
                n = (s + 2) % TURN
                if there(b + 2):
                    wait(sp, s_bv, b - 1)
                    wait(sp, s_bs, b - 1)
                    wait(sp, s_bskip, b - 1)
                    sp.dma_start(b_h[:, n, :], hb[ds(b + 2, 1), :, 0:D].rearrange("o p d -> (o p) d")
                                 ).then_inc(s_bin[n], 16)
                    sp.dma_start(b_x[:, n, :], one(xb, b + 2)).then_inc(s_bin[n], 16)
                    sp.dma_start(b_xT[:, n, :, :], xv[:, :, ds((b + 2) * P, P)]).then_inc(s_bin[n], 16)
                m = (s - 1) % TURN
                if there(b - 1):
                    wait(sp, s_bout, 2 * b)
                    sp.dma_start(one(x1b, b - 1), b_x1[:, m, :]).then_inc(s_bst[m], 16)

            steps(sp, NB, 2, step_b)
            for s in range(TURN):
                sp.wait_ge(s_bst[s], 16 * len(range(s, NB, TURN)))

            wv = w_tab.rearrange("(w p) d -> w p d", p=P)

            def step_c(u, s, there):
                n = (s + 2) % TURN
                if there(u + 2):
                    wait(sp, s_cotf, u - 1)
                    sp.dma_start(c_ot[:, n, :, :].rearrange("p k e -> p (k e)"), one(ot_tab, u + 2)
                                 ).then_inc(s_cot[n], 16)
                    wait(sp, s_cmid, u - 1)
                    for k in range(PAIR):
                        w = sp.value_load(window_row[:, ds((u + 2) * PAIR + k, 1)], min_val=0, max_val=EW - 1)
                        sp.dma_start(wt[:, n, k, :], one(wv, w)).then_inc(s_cw[n], 16)

            steps(sp, NU, 2, step_c)

            for k in range(GROUP):
                sp.wait_ge(s_add[k], 16 * NG)
            pb = [q.rearrange("(b p) d -> b p d", p=P) for q in part]
            ob = out.rearrange("(b p) d -> b p d", p=P)

            def step_d(b, s, there):
                n = (s + 2) % TURN
                if there(b + 2):
                    wait(sp, s_dsum, b - 1)
                    wait(sp, s_dz, b - 1)
                    for k in range(GROUP):
                        sp.dma_start(d_p[:, n, k, :], one(pb[k], b + 2)).then_inc(s_din[n], 16)
                    sp.dma_start(d_x[:, n, :], one(x1b, b + 2)).then_inc(s_din[n], 16)
                m = (s - 1) % TURN
                if there(b - 1):
                    wait(sp, s_dout, 2 * b)
                    sp.dma_start(one(ob, b - 1), d_out[:, m, :]).then_inc(s_dst[m], 16)

            steps(sp, NB, 2, step_d)
            for s in range(TURN):
                sp.wait_ge(s_dst[s], 16 * len(range(s, NB, TURN)))

        @block.gpsimd
        def _(pool):
            g = nc.gpsimd
            g.iota(iota_n[:, :], [[1, P]], base=0, channel_multiplier=0, allow_small_or_imprecise_dtypes=True)
            g.iota(part_no[:, :], [[0, 1]], base=0, channel_multiplier=1, allow_small_or_imprecise_dtypes=True)
            g.iota(trash[:, :], [[0, 1]], base=NP, channel_multiplier=1, allow_small_or_imprecise_dtypes=True)
            g.iota(bounds[:, :], [[P, 2]], base=0, channel_multiplier=P, allow_small_or_imprecise_dtypes=True)
            g.iota(tile_col[:, :], [[P, NC]], base=0, channel_multiplier=1, allow_small_or_imprecise_dtypes=True)
            g.iota(iota_t, [[1, T]], base=0, channel_multiplier=0, allow_small_or_imprecise_dtypes=True)
            g.memset(half[:, :], -0.5).then_inc(s_iota, 1)

            hv = h_tab.rearrange("(c k p) d -> c p k d", k=CHUNK, p=P)

            def store_h(c, s):
                wait_apart(pool, s_hev, 2 * CHUNK * (c + 1))
                pool.dma_start(hv[ds(c, 1)].rearrange("o p k d -> (o p) k d"), h_out[:, s, :, :]
                               ).then_inc(s_hst[s], 16)

            for c in range(2):
                store_h(c, c)
            with pool.Fori(1, NCH // 2) as i:
                for s in range(2):
                    store_h(i * 2 + s, s)

            pool.wait_ge(s_win, 1)
            for c in range(NC):
                pool.indirect_dma_start(sd_in[:, c, :, :].rearrange("p w e -> p (w e)"), None, edges_sd,
                                        bass.IndirectOffsetOnAxis(ap=wcol[:, c:c + 1], axis=0)
                                        ).then_inc(s_sdin, 16)
            pool.wait_ge(s_amax, 1)
            g.partition_all_reduce(gmax[:, :], amax[:, :], P, RMAX).then_inc(s_gmax, 1)

            for s in range(2):
                pool.wait_ge(s_hst[s], 16 * (NCH // 2))

            def step_a(gr, s, there):
                if there(gr):
                    wait_apart(pool, s_idx, gr + 1)
                    wait_apart(pool, s_agg, GROUP * (gr - TURN + 1))
                    for k in range(GROUP):
                        pool.indirect_dma_start(hg[:, s, k, :], None, h_tab,
                                                bass.IndirectOffsetOnAxis(ap=sidx[:, s, k:k + 1], axis=0)
                                                ).then_inc(s_hg[s], 16)

            steps(pool, NG, 0, step_a)

            pool.wait_ge(s_self, 1)

            def step_b(b, s, there):
                n = (s + 1) % TURN
                if there(b + 1):
                    wait_apart(pool, s_bin[n], landed(b + 1, n, 3))
                    g.tensor_tensor(b_h[:, n, :].rearrange("p (h c) -> p h c", h=H),
                                    b_h[:, n, :].rearrange("p (h c) -> p h c", h=H),
                                    pself[:, ds(b + 1, 1), :].rearrange("p o (h c) -> p (o h) c", c=1
                                                                        ).to_broadcast([P, H, C]),
                                    ALU.mult).then_inc(s_bt, 1)
                if there(b):
                    wait(pool, s_bmv, 3 * (b + 1))
                    g.tensor_tensor(mv[:, s, 3:4], mv[:, s, 2:3], half[:, 0:1], ALU.pow).then_inc(s_brstd, 1)

            steps(pool, NB, 1, step_b)

            pool.wait_ge(s_zero, 16 * GROUP)
            def step_c(u, s, there):
                if there(u):
                    wait_apart(pool, s_cix, 3 * (u + 1))
                    for k in range(PAIR):
                        q = s % 2 * PAIR + k
                        wait_apart(pool, s_ccmb, PAIR * u + k + 1)
                        wait_apart(pool, s_add[q], 8 * u - 8 * (s % 2))
                        pool.indirect_dma_start(part[q], bass.IndirectOffsetOnAxis(ap=c_idx[:, s, k:k + 1], axis=0),
                                                o_cmb[:, q, :], None, compute_op=ALU.add).then_inc(s_add[q], 16)

            steps(pool, NU, 0, step_c)

            def step_d(b, s, there):
                n = (s + 2) % TURN
                if there(b + 2):
                    wait(pool, s_ddeg, b + 3)
                    g.tensor_tensor(d_n[:, n, 1:2], d_n[:, n, 0:1], half[:, 0:1], ALU.pow).then_inc(s_ddn, 1)
                m = (s + 1) % TURN
                if there(b + 1):
                    wait(pool, s_dms, 2 * (b + 2))
                    g.tensor_tensor(d_n[:, m, 4:6], d_n[:, m, 2:4], half[:, 0:2], ALU.pow).then_inc(s_drs, 1)
                if there(b):
                    wait(pool, s_dmv, 3 * (b + 1))
                    g.tensor_tensor(mv[:, s, 3:4], mv[:, s, 2:3], half[:, 0:1], ALU.pow).then_inc(s_drstd, 1)

            steps(pool, NB, 2, step_d)

        @block.scalar
        def _(act):
            a = nc.scalar
            act.wait_ge(s_zeroed, 1)
            for k in range(GROUP):
                c = 3 if (NB + 1) % 3 == 0 else 1
                act.dma_start(part[k].rearrange("(p r c) d -> p r (c d)", p=P, c=c),
                              zeros[:, 0:c * OR].rearrange("p (o d) -> p o d", o=1
                                                           ).to_broadcast([P, (NB + 1) // c, c * OR])
                              ).then_inc(s_zero, 16)

            act.wait_ge(s_watt, 1)
            a.copy(Wx[:, :, D:], PS[:, 6, 0:4 * H].rearrange("p (k j) -> p k j", k=2)).then_inc(s_hwatt, 1)

            def evacuate_h(c, s, stored):
                wait_apart(act, s_hst[s], stored)
                for k in range(CHUNK):
                    wait_apart(act, s_hps, CHUNK * c + k + 1)
                    a.copy(h_out[:, s, k, :], PS[:, k, 0:HW]).then_inc(s_hev, 1)
                    a.copy(logits[:, ds(c * CHUNK + k, 1), 0:2 * H].rearrange("p o j -> p (o j)"),
                           PS[:, k, D:D + 2 * H]).then_inc(s_hev, 1)

            for c in range(2):
                evacuate_h(c, c, 0)
            with act.Fori(1, NCH // 2) as i:
                for s in range(2):
                    evacuate_h(i * 2 + s, s, i * 16)

            for c in range(NC):
                act.wait_ge(s_sdp, c + 1)
                a.copy(srcF[:, c * P:(c + 1) * P], PS[:, c % 2, 0:P]).then_inc(s_sdT, 1)
            act.wait_ge(s_lg, LG_SELF)
            a.activation(pself[:, :, :], lt[:, :, 0:H], ACT.Exp).then_inc(s_self, 1)

            act.wait_ge(s_sdT, NC)

            def sources(g, s):
                a.copy(sidx[:, s, :], srcF[:, ds(g * GROUP, GROUP)]).then_inc(s_idx, 1)

            sources(0, 0)

            def step_a(g, s, there):
                n = (s + 1) % TURN
                if there(g):
                    wait(act, s_z, 3 * (g + 1))
                    a.activation(hg[:, s, :, D:HW], za[:, s % 2, :, :], ACT.Exp).then_inc(s_p, 1)
                if there(g + 1):
                    wait(act, s_otp, g + 2)
                    wait(act, s_otst[(n - 2) % TURN], landed(g - 1, (n - 2) % TURN) if there(g - 1) else 0)
                    a.copy(ots[:, n % 2, :, :], PS[:, 0, :].rearrange("p (k e) -> p k e", k=GROUP)
                           ).then_inc(s_ots, 1)
                    wait(act, s_f1, g + 2)
                    a.activation(h1[:, n % 2, :], PS[:, 6, 256:512], ACT.Silu, scale=S8).then_inc(s_h1, 1)
                if there(g):
                    for k in range(GROUP):
                        wait(act, s_f3, GROUP * g + k // 2 * 2 + 2)
                        if k == 0:
                            wait(act, s_wst[(s - 2) % TURN], landed(g - 2, (s - 2) % TURN) if there(g - 2) else 0)
                            wait(act, s_ea[s], landed(g, s, 2))
                            a.copy(wst[:, s % 2, :, D:WR], sh[:, s, :, :])
                        src = PS[:, 7, k % 2 * D:(k % 2 + 1) * D]
                        a.mul(wst[:, s % 2, k, 0:2 * MUL], src[:, 0:2 * MUL], sh[:, s, k, 0:1])
                        a.copy(wst[:, s % 2, k, 2 * MUL:D], src[:, 2 * MUL:D]).then_inc(s_wev, 1)
                if there(g + 2):
                    sources(g + 2, (s + 2) % TURN)
                if there(g + 1):
                    wait(act, s_f2, g + 2)
                    a.activation(h2[:, n % 2, :], PS[:, 6, 0:256], ACT.Silu, scale=S64).then_inc(s_h2, 1)

            steps(act, NG, 1, step_a)

            def step_b(b, s, there):
                if there(b):
                    wait(act, s_bm, b + 1)
                    a.activation(b_e[:, s, :], b_e[:, s, :], ACT.Exp).then_inc(s_be, 1)
                m = (s - 1) % TURN
                if there(b - 1):
                    wait(act, s_bxp, b)
                    a.copy(b_x1T[:, m % 2, :, :], PS[:, 2, 0:256].rearrange("p (k n) -> p k n", k=2)).then_inc(s_bxT, 1)
                    wait(act, s_by, b)
                    a.copy(acc[:, ds(b - 1, 1), 0:D].rearrange("p o d -> p (o d)"), PS[:, 3, 0:D]).then_inc(s_bout, 1)
                    a.copy(b_x1[:, m, D:], PS[:, 4, 0:D]).then_inc(s_bout, 1)

            steps(act, NB, 0, step_b)

            def step_c(u, s, there):
                n = (s + 1) % TURN
                if there(u + 1):
                    wait_apart(act, s_cix, 3 * (u - 2))
                    a.copy(c_src[:, n, :], srcF[:, ds((u + 1) * PAIR, PAIR)])
                    a.copy(c_val[:, n, :], valid[:, ds((u + 1) * PAIR, PAIR)]).then_inc(s_csl, 1)
                    wait(act, s_cot[n], landed(u + 1, n))
                    wait(act, s_cy, u)
                    a.copy(c_otf[:, n % 2, :, :], c_ot[:, n, :, :]).then_inc(s_cotf, 1)
                if there(u):
                    for k in range(PAIR):
                        wait(act, s_cmt, PAIR * u + k + 1)
                        wait(act, s_co, PAIR * (u - 1) + k + 1)
                        a.copy(midT[:, k, :, :], PS[:, 3 + k, :].rearrange("p (c e) -> p c e", c=4)).then_inc(s_cmT, 1)
                    for k in range(PAIR):
                        wait(act, s_co, PAIR * (u + 1))
                        wait(act, s_cc, PAIR * (u - 1) + k + 1)
                        a.copy(o_sb[:, k, D:D + 1], c_val[:, s, k:k + 1])
                        a.copy(o_sb[:, k, 0:D], PS[:, 5, k * D:(k + 1) * D]).then_inc(s_cosb, 1)
                    for k in range(PAIR):
                        q = s % 2 * PAIR + k
                        wait(act, s_cc, PAIR * u + k + 1)
                        wait(act, s_add[q], 8 * u - 8 * (s % 2))
                        a.copy(o_cmb[:, q, :], PS[:, 6 + k, 0:OR]).then_inc(s_ccmb, 1)

            steps(act, NU, 1, step_c)

            def step_d(b, s, there):
                n = (s + 1) % TURN
                if there(b + 1):
                    wait(act, s_do, b + 2)
                    a.activation(d_q[:, 0:MUL], d_o[:, n, 0:MUL], ACT.Square, accum_out=d_n[:, n, 6:7])
                    a.activation(d_q[:, MUL:D], d_o[:, n, MUL:D], ACT.Square, accum_out=d_n[:, n, 7:8]).then_inc(s_dsq, 1)

            steps(act, NB, 1, step_d)

        @block.tensor
        def _(pe):
            mm = nc.tensor.matmul
            pe.wait_ge(s_const, 1)
            pe.wait_ge(s_tab, TAB_WINDOWS)
            mm(PS[0:NB, 7, 64:65], upper[0:NB, 0:NB], cnt[0:NB, 3:4], start=True, stop=True).then_inc(s_tabp, 1)
            pe.wait_ge(s_tab, TAB_STEPS)
            for c in range(NC):
                mm(PS[:, 7, 128 + 2 * c:130 + 2 * c], stepm[:, c * P:(c + 1) * P], two[0:NB, 0:33:32],
                   start=True, stop=True)
            for c in range(-(-T // 512)):
                e = min(T, (c + 1) * 512)
                last = mm(PS[0:33, c, 0:e - c * 512], two[0:NB, :], stepm[:, c * 512:e], start=True, stop=True)
            last.then_inc(s_tabp, 1)
            pe.wait_ge(s_w, 16 * N_W)
            for k in range(2):
                for m in range(2):
                    last = mm(PS[:, 6, k * 2 * H:(k + 1) * 2 * H], WTs[:, m, k * P:(k + 1) * P], att[:, m, :],
                              start=(m == 0), stop=(m == 1))
            last.then_inc(s_watt, 1)
            pe.wait_ge(s_hwatt, 1)
            pe.wait_ge(s_win, 1)

            def node_maps(c, s, arrived):
                pe.wait_ge(s_xin[s], arrived)
                for k in range(CHUNK):
                    wait(pe, s_hev, 2 * (CHUNK * (c - 1) + k + 1))
                    for j in range(2):
                        last = mm(PS[:, k, 0:D + 2 * H], x_in[:, s, j, k * P:(k + 1) * P], Wx[:, j, :],
                                  start=(j == 0), stop=(j == 1))
                    last.then_inc(s_hps, 1)

            for c in range(2):
                node_maps(c, c, 16)
            with pe.Fori(1, NCH // 2) as i:
                for s in range(2):
                    node_maps(i * 2 + s, s, i * 16 + 16)

            pe.wait_ge(s_hev, 2 * NB)
            for c in range(NC):
                pe.wait_ge(s_sdf, 1)
                if c >= 2:
                    pe.wait_ge(s_sdT, c - 1)
                    pe.wait_ge(s_dl, c - 1)
                nc.tensor.transpose(PS[:, c % 2, 0:P], sd_f[:, c, 0, :], ident[:, :])
                nc.tensor.transpose(PS[:, 2 + c % 2, 0:P], sd_f[:, c, 1, :], ident[:, :]).then_inc(s_sdp, 1)

            pe.wait_ge(s_sdT, NC)
            pe.wait_ge(s_dl, NC)
            pe.wait_ge(s_scaled, 1)
            pe.wait_ge(s_lg, LG_PARTS)

            def step_a(g, s, there):
                n = (s + 1) % TURN
                if there(g + 1):
                    wait(pe, s_oh, g + 2)
                    wait(pe, s_ots, g + 1)
                    for k in range(GROUP):
                        last = nc.tensor.transpose(PS[:, 0, k * P:(k + 1) * P], oh[:, n % 2, k, :], ident[:, :])
                    last.then_inc(s_otp, 1)
                    wait(pe, s_ea[n], landed(g + 1, n, 2))
                    wait(pe, s_h2, g + 1)
                    mm(PS[:, 6, 256:512], fc1[:, :], eat[0:2 * NBAS, n % 2, :], start=True, stop=True).then_inc(s_f1, 1)
                if there(g):
                    for k in range(GROUP):
                        wait(pe, s_h2, g + 1)
                        wait(pe, s_wev, GROUP * g + k // 2 * 2)
                        r = k // 2 * MUL
                        mm(PS[:, 7, k % 2 * D:(k % 2 + 1) * D], h2[r:r + MUL, s % 2, k % 2 * P:(k % 2 + 1) * P],
                           fc3[r:r + MUL, :], start=True, stop=True).then_inc(s_f3, 1)
                if there(g + 1):
                    wait(pe, s_ots, g + 2)
                    wait(pe, s_z, 3 * (g + 1))
                    for k in range(GROUP):
                        b = pe.value_load(block_row[:, ds((g + 1) * GROUP + k, 1)], min_val=0, max_val=NB - 1)
                        for j in range(3):
                            last = mm(PS[:, 1, k * 2 * H:(k + 1) * 2 * H], ots[:, n % 2, k, :],
                                      ac3[:, ds(b, 1), j, :].rearrange("p o j -> p (o j)"),
                                      start=(j == 0), stop=(j == 2))
                    last.then_inc(s_ad, 1)
                if there(g):
                    for k in range(GROUP):
                        wait(pe, s_msg, GROUP * g + k + 1)
                        wait(pe, s_acc, GROUP * (g - 1) + k + 1)
                        mm(PS[:, 2 + k, 0:HW], oh[:, s % 2, k, :], hg[:, s, k, :], start=True, stop=True).then_inc(s_agg, 1)
                if there(g + 1):
                    wait(pe, s_h1, g + 2)
                    mm(PS[:, 6, 0:256], fc2[:, :], h1[:, n % 2, :], start=True, stop=True).then_inc(s_f2, 1)

            steps(pe, NG, 1, step_a)

            pe.wait_ge(s_acc, GROUP * NG)
            pe.wait_ge(s_wev, GROUP * NG)

            def step_b(b, s, there):
                n = (s + 1) % TURN
                if there(b + 1):
                    wait(pe, s_bin[n], landed(b + 1, n, 3))
                    wait(pe, s_bv, b)
                    mm(PS[:, n % 2, 0:D], b_xT[:, n, 0, :], skw[:, 0, :], start=True, stop=False)
                    mm(PS[:, n % 2, 0:D], b_xT[:, n, 1, :], skw[:, 1, :], start=False, stop=False)
                    mm(PS[:, n % 2, 0:D], ones[0:1, :], brow[:, :], start=False, stop=True).then_inc(s_bskip, 1)
                m = (s - 1) % TURN
                if there(b - 1):
                    wait(pe, s_bx1, 2 * b)
                    wait(pe, s_bxT, b - 1)
                    for j in range(2):
                        last = nc.tensor.transpose(PS[:, 2, j * P:(j + 1) * P], b_x1[:, m, j * P:(j + 1) * P], ident[:, :])
                    last.then_inc(s_bxp, 1)
                    wait(pe, s_bxT, b)
                    wait(pe, s_bout, 2 * (b - 1))
                    for j in range(2):
                        mm(PS[:, 3, j * P:(j + 1) * P], b_x1T[:, m % 2, j, :], w1m[:, j, :], start=True, stop=True)
                    for j in range(2):
                        last = mm(PS[:, 4, j * P:(j + 1) * P], b_x1T[:, m % 2, j, :], wscm[:, j, :], start=True, stop=True)
                    last.then_inc(s_by, 1)

            steps(pe, NB, 1, step_b)

            pe.wait_ge(s_bout, 2 * NB)

            def step_c(u, s, there):
                n = (s + 1) % TURN
                if there(u + 1):
                    wait(pe, s_cotf, u + 2)
                    wait(pe, s_cmid, u)
                    for k in range(PAIR):
                        b = pe.value_load(block_row[:, ds((u + 1) * PAIR + k, 1)], min_val=0, max_val=NB - 1)
                        last = mm(PS[:, n % 2, k * D:(k + 1) * D], c_otf[:, n % 2, k, :],
                                  acc[:, ds(b, 1), 0:D].rearrange("p o d -> p (o d)"), start=True, stop=True)
                    last.then_inc(s_cy, 1)
                    wait(pe, s_csl, u + 2)
                    wait(pe, s_csame, PAIR * (u + 1))
                    for k in range(PAIR):
                        last = nc.tensor.transpose(PS[:, 2, (n % 2 * 2 + k) * P:(n % 2 * 2 + k + 1) * P],
                                                   c_src[:, n, k:k + 1].to_broadcast([P, P]), ident[:, :])
                    last.then_inc(s_csr, 1)
                if there(u):
                    wait(pe, s_cmid, u + 1)
                    for k in range(PAIR):
                        wait(pe, s_cmT, PAIR * (u - 1) + k + 1)
                        for j in range(4):
                            last = nc.tensor.transpose(PS[:, 3 + k, j * P:(j + 1) * P],
                                                       mid[:, s % 2, k, 2 * j:2 * j + 2, :].rearrange("p c u -> p (c u)"),
                                                       ident[:, :])
                        last.then_inc(s_cmt, 1)
                    for k in range(PAIR):
                        wait(pe, s_cmT, PAIR * u + k + 1)
                        wait(pe, s_cosb, PAIR * u)
                        for j in range(4):
                            last = mm(PS[:, 5, k * D + j * MUL:k * D + (j + 1) * MUL], midT[:, k, j, :],
                                      w2m[:, min(j, 1), :], start=True, stop=True)
                        last.then_inc(s_co, 1)
                    for k in range(PAIR):
                        wait(pe, s_csame, PAIR * u + k + 1)
                        wait(pe, s_cosb, PAIR * u + k + 1)
                        wait(pe, s_ccmb, PAIR * (u - 1) + k + 1)
                        mm(PS[:, 6 + k, 0:OR], same[:, s % 2, k, :], o_sb[:, k, :], start=True, stop=True).then_inc(s_cc, 1)

            steps(pe, NU, 1, step_c)

            pe.wait_ge(s_ccmb, T)

            def step_d(b, s, there):
                n = (s + 2) % TURN
                if there(b + 2):
                    wait(pe, s_din[n], landed(b + 2, n, 5))
                    wait(pe, s_do, b + 1)
                    for k in range(GROUP):
                        last = mm(PS[:, n % 2, 0:OR], ident[:, :], d_p[:, n, k, :], start=(k == 0), stop=(k == GROUP - 1))
                    last.then_inc(s_dsum, 1)

            steps(pe, NB, 2, step_d)

        @block.vector
        def _(dve):
            v = nc.vector
            for tile in (att, w1m, wscm):
                v.memset(tile[:, :, :], 0.0)
            for tile in (zeros, fc2, two):
                v.memset(tile[:, :], 0.0)
            v.memset(ones[:, :], 1.0)
            v.memset(fc1[:, :], 0.0).then_inc(s_zeroed, 1)
            dve.wait_ge(s_iota, 1)
            v.tensor_scalar(ident[:, :], iota_n[:, :], part_no[:, 0:1], None, ALU.is_equal)
            v.tensor_scalar(upper[:, :], iota_n[:, :], part_no[:, 0:1], None, ALU.is_gt)
            v.tensor_scalar(lower_eq[:, :], iota_n[:, :], part_no[:, 0:1], None, ALU.is_le).then_inc(s_const, 1)

            tab = [0]

            def link(ins):
                tab[0] += 1
                ins.then_inc(s_tab, 1)
                dve.wait_ge(s_tab, tab[0])

            dve.wait_ge(s_ends, 16)
            link(v.tensor_copy(ends, ends.bitcast(I32)))
            for col, which, bound in ((0, 1, 0), (1, 0, 1), (2, 1, 1)):
                link(v.tensor_scalar(stepm[:, 0:EW], ends[:, which, :], bounds[0:NB, bound:bound + 1], None,
                                     ALU.is_lt, ALU.add, accum_out=cnt[0:NB, col:col + 1]))
            link(v.tensor_scalar(cnt[0:NB, 3:4], cnt[0:NB, 1:2], cnt[0:NB, 0:1], 0.0, ALU.subtract, ALU.max))
            dve.wait_ge(s_tabp, 1)
            link(v.tensor_tensor(cnt[0:NB, 4:5], PS[0:NB, 7, 64:65], cnt[0:NB, 3:4], ALU.add))
            link(v.tensor_tensor(cnt[0:NB, 5:6], cnt[0:NB, 2:3], cnt[0:NB, 0:1], ALU.subtract))
            v.memset(two[:, 0:1], 1.0)
            v.tensor_tensor(two[0:NB, 32:33], cnt[0:NB, 5:6], cnt[0:NB, 3:4], ALU.subtract)
            link(v.tensor_scalar(stepm, iota_t[0:NB, :], cnt[0:NB, 4:5], None, ALU.is_ge))
            dve.wait_ge(s_tabp, 2)
            flat = PS[:, 0:4, :].rearrange("p b n -> p (b n)")[:, 0:T]
            v.tensor_scalar(block_row, flat[0:1, :], float(NB - 1), None, ALU.min)
            link(v.tensor_tensor(iota_t[32:33, :], flat[32:33, :], iota_t[32:33, :], ALU.add))
            v.tensor_scalar(window_row, iota_t[32:33, :], float(EW - 1), None, ALU.min)
            cols = PS[:, 7, 128:128 + 2 * NC].rearrange("p (c j) -> p c j", j=2)
            v.tensor_scalar(b128[:, :], cols[:, :, 0], float(P), None, ALU.mult)
            link(v.tensor_tensor(tile_col[:, :], cols[:, :, 1], tile_col[:, :], ALU.add))
            v.tensor_scalar(wcol[:, :], tile_col[:, :], float(EW - 1), None, ALU.min).then_inc(s_win, 1)

            dve.wait_ge(s_w, 16 * N_W)
            for tile in (w1m, wscm):
                v.tensor_scalar(tile[:, :, :], tile[:, :, :], S64, None, ALU.mult)
            v.tensor_scalar(fc3[:, :], fc3[:, :], S64, None, ALU.mult)
            v.tensor_scalar(w2m[MUL:P, 0, :], w2m[MUL:P, 0, :], INV_SQRT3, None, ALU.mult).then_inc(s_scaled, 1)

            dve.wait_ge(s_sdin, 16 * NC)
            v.tensor_copy(sd_f[:, :, 0, :], sd_in[:, :, 0, :])
            v.tensor_tensor(sd_f[:, :, 1, :], sd_in[:, :, 1, :],
                            b128[:, :].rearrange("p (c o) -> p c o", o=1).to_broadcast([P, NC, P]),
                            ALU.subtract).then_inc(s_sdf, 1)

            dve.wait_ge(s_hev, 2 * NB)
            v.tensor_reduce(amax[:, :], logits[:, :, 0:H].rearrange("p b h -> p h b"), AX.X, ALU.max).then_inc(s_amax, 1)
            lg = [0]

            def link_lg(ins):
                lg[0] += 1
                ins.then_inc(s_lg, 1)
                dve.wait_ge(s_lg, lg[0])

            def leaky(to, z):
                return v.scalar_tensor_tensor(to, z, SLOPE, z, ALU.mult, ALU.max)

            dve.wait_ge(s_gmax, 1)
            link_lg(v.tensor_tensor(lt[:, :, H:], logits[:, :, H:2 * H],
                                    gmax[:, :].rearrange("p (o h) -> p o h", o=1).to_broadcast([P, NB, H]), ALU.add))
            link_lg(leaky(logits[:, :, 2 * H:], lt[:, :, H:]))
            link_lg(v.tensor_copy(ac3[:, :, 0, :], logits[:, :, H:]))
            link_lg(v.tensor_tensor(lt[:, :, :], logits[:, :, H:], ac3[:, :, 0, :], ALU.subtract))
            link_lg(v.tensor_copy(ac3[:, :, 1, :], lt[:, :, :]))
            link_lg(v.tensor_tensor(ac3[:, :, 2, :], lt[:, :, :], ac3[:, :, 1, :], ALU.subtract))
            link_lg(v.tensor_tensor(lt[:, :, 0:H], logits[:, :, 0:H], logits[:, :, H:2 * H], ALU.add))
            link_lg(leaky(lt[:, :, 0:H], lt[:, :, 0:H]))
            link_lg(v.tensor_tensor(lt[:, :, 0:H], lt[:, :, 0:H], logits[:, :, 2 * H:], ALU.subtract))
            assert lg[0] == LG_SELF

            for c in range(NC):
                dve.wait_ge(s_sdp, c + 1)
                v.tensor_scalar(dloc[:, c * P:(c + 1) * P], PS[:, 2 + c % 2, 0:P], -1.0, float(P), ALU.max,
                                ALU.min).then_inc(s_dl, 1)
            dve.wait_ge(s_dl, NC)
            v.tensor_scalar(valid[:, :], dloc[:, :], 0.0, None, ALU.is_ge).then_inc(s_dl, 1)
            dve.wait_ge(s_dl, NC + 1)
            v.scalar_tensor_tensor(valid[:, :], dloc[:, :], float(P), valid[:, :], ALU.is_lt, ALU.mult).then_inc(s_dl, 1)
            dve.wait_ge(s_win, 1)
            v.memset(acc[:, :, :], 0.0).then_inc(s_acc0, 1)

            dve.wait_ge(s_acc0, 1)

            def one_hots(g, s):
                wait_apart(dve, s_agg, GROUP * (g - 1))
                v.tensor_tensor(oh[:, s % 2, :, :],
                                iota_n[:, :].rearrange("p (o n) -> p o n", o=1).to_broadcast([P, GROUP, P]),
                                dloc[:, ds(g * GROUP, GROUP)].rearrange("p (k o) -> p k o", o=1
                                                                        ).to_broadcast([P, GROUP, P]),
                                ALU.is_equal).then_inc(s_oh, 1)

            def step_a(g, s, there):
                if there(g + 1):
                    one_hots(g + 1, (s + 1) % TURN)
                if there(g):
                    ad = PS[:, 1, 0:GROUP * 2 * H].rearrange("p (k j) -> p k j", j=2 * H)
                    wait(dve, s_hg[s], landed(g, s, GROUP))
                    wait(dve, s_ad, g + 1)
                    v.tensor_tensor(za[:, s % 2, :, :], hg[:, s, :, D:HW], ad[:, :, 0:H], ALU.add).then_inc(s_z, 1)
                    wait(dve, s_z, 3 * g + 1)
                    leaky(zb[:, s % 2, :, :], za[:, s % 2, :, :]).then_inc(s_z, 1)
                    wait(dve, s_z, 3 * g + 2)
                    v.tensor_tensor(za[:, s % 2, :, :], zb[:, s % 2, :, :], ad[:, :, H:], ALU.subtract).then_inc(s_z, 1)
                for k in range(GROUP):
                    if there(g - 1):
                        t = (g - 1) * GROUP + k
                        b = dve.value_load(block_row[:, ds(t, 1)], min_val=0, max_val=NB - 1)
                        wait(dve, s_agg, t + 1)
                        wait(dve, s_acc, t)
                        a = acc[:, ds(b, 1), :].rearrange("p o d -> p (o d)")
                        v.tensor_tensor(a, a, PS[:, 2 + k, 0:HW], ALU.add).then_inc(s_acc, 1)
                    if there(g):
                        if k == 0:
                            wait(dve, s_p, g + 1)
                        m = hg[:, s, k, 0:D].rearrange("p (h c) -> p h c", h=H)
                        v.tensor_tensor(m, m, hg[:, s, k, D:HW].rearrange("p (h o) -> p h o", o=1
                                                                          ).to_broadcast([P, H, C]),
                                        ALU.mult).then_inc(s_msg, 1)

            steps(dve, NG, 1, step_a)

            dve.wait_ge(s_acc, T)
            dve.wait_ge(s_self, 1)
            v.tensor_tensor(rden[:, :, :], acc[:, :, D:HW], pself[:, :, :], ALU.add).then_inc(s_rden, 1)
            dve.wait_ge(s_rden, 1)
            v.reciprocal(rden[:, :, :], rden[:, :, :]).then_inc(s_rden, 1)
            dve.wait_ge(s_rden, 2)

            def layer_norm_stats(z, s, b, done):
                v.bn_stats(stat[:, s, :], z).then_inc(done, 1)
                wait_apart(dve, done, 3 * b + 1)
                v.bn_aggr(mv[:, s, 0:2], stat[:, s, :]).then_inc(done, 1)
                wait(dve, done, 3 * b + 2)
                v.tensor_scalar(mv[:, s, 2:3], mv[:, s, 1:2], EPS, None, ALU.add).then_inc(done, 1)

            def normalized(to, of, s):
                return v.tensor_scalar(to, of, mv[:, s, 0:1], mv[:, s, 3:4], ALU.subtract, ALU.mult)

            def step_b(b, s, there):
                n, m = (s + 1) % TURN, (s - 1) % TURN
                if there(b + 1):
                    hs = b_h[:, n, :]
                    hs4 = hs.rearrange("p (h c) -> p h c", h=H)
                    wait_apart(dve, s_bt, b + 2)
                    v.tensor_tensor(hs, hs, acc[:, ds(b + 1, 1), 0:D].rearrange("p o d -> p (o d)"), ALU.add
                                    ).then_inc(s_bsum, 1)
                    wait_apart(dve, s_bsum, 2 * b + 3)
                    v.tensor_tensor(hs4, hs4, rden[:, ds(b + 1, 1), :].rearrange("p o (h c) -> p (o h) c", c=1
                                                                                 ).to_broadcast([P, H, C]),
                                    ALU.mult).then_inc(s_bsum, 1)
                    wait(dve, s_bsum, 2 * b + 4)
                    wait(dve, s_bskip, b + 2)
                    v.tensor_tensor(b_v[:, n, :], hs, PS[:, n % 2, 0:D], ALU.add).then_inc(s_bv, 1)
                    wait(dve, s_bv, b + 2)
                    v.tensor_scalar(b_e[:, n, :], b_v[:, n, :], 0.0, None, ALU.min).then_inc(s_bm, 1)
                if there(b):
                    wait(dve, s_be, b + 1)
                    v.scalar_tensor_tensor(b_v[:, s, :], b_v[:, s, :], 0.0, b_e[:, s, :], ALU.max, ALU.add
                                           ).then_inc(s_belu, 1)
                    wait(dve, s_belu, b + 1)
                    v.scalar_tensor_tensor(b_v[:, s, :], b_v[:, s, :], -1.0, b_x[:, s, :], ALU.add, ALU.add
                                           ).then_inc(s_bs, 1)
                    wait(dve, s_bs, b + 1)
                    layer_norm_stats(b_v[:, s, :], s, b, s_bmv)
                if there(b - 1):
                    wait(dve, s_brstd, b)
                    wait(dve, s_bst[m], landed(b - 5, m) if there(b - 5) else 0)
                    normalized(b_x1[:, m, 0:MUL], b_v[:, m, 0:MUL], m).then_inc(s_bx1, 1)
                    normalized(b_x1[:, m, MUL:D].rearrange("p (d u) -> p d u", d=3),
                               b_v[:, m, MUL:D].rearrange("p (u d) -> p d u", d=3), m).then_inc(s_bx1, 1)

            steps(dve, NB, 1, step_b)

            def step_c(u, s, there):
                if not there(u):
                    return
                y = PS[:, s % 2, :].rearrange("p (k d u) -> p k d u", k=PAIR, d=4)
                w = wt[:, s, :, 0:D].rearrange("p k (a b u) -> p k a b u", a=2, b=2)
                sh1 = wt[:, s, :, D + 1:D + 4].rearrange("p k (d o) -> p k d o", o=1).to_broadcast([P, PAIR, 3, MUL])
                q = mid[:, s % 2, :, 1, :]
                wait(dve, s_cy, u + 1)
                wait(dve, s_cw[s], landed(u, s, PAIR))
                wait(dve, s_cmt, PAIR * (u - 1))

                def spread(z):
                    return z.rearrange("p k (o u) -> p k o u", o=1).to_broadcast([P, PAIR, 3, MUL])

                v.tensor_tensor(mid[:, s % 2, :, 0:2, :], w[:, :, :, 0, :],
                                y[:, :, 0:1, :].to_broadcast([P, PAIR, 2, MUL]), ALU.mult).then_inc(s_cpr, 1)
                v.tensor_tensor(evs[:, :, :, :], y[:, :, 1:4, :], sh1, ALU.mult).then_inc(s_cpr, 1)
                v.tensor_tensor(mid[:, s % 2, :, 3:8:2, :], y[:, :, 1:4, :], spread(w[:, :, 0, 1, :]), ALU.mult)
                wait(dve, s_cpr, 4 * u + 1)
                v.tensor_tensor(mid[:, s % 2, :, 2:8:2, :], spread(q), sh1, ALU.mult)
                wait(dve, s_cpr, 4 * u + 2)
                v.tensor_tensor(evt[:, :, :], evs[:, :, 0, :], evs[:, :, 1, :], ALU.add).then_inc(s_cpr, 1)
                wait(dve, s_cpr, 4 * u + 3)
                v.tensor_tensor(evt[:, :, :], evt[:, :, :], evs[:, :, 2, :], ALU.add).then_inc(s_cpr, 1)
                wait(dve, s_cpr, 4 * u + 4)
                v.tensor_tensor(q, evt[:, :, :], w[:, :, 1, 1, :], ALU.mult).then_inc(s_cmid, 1)
                wait(dve, s_csr, u + 1)
                wait(dve, s_cc, PAIR * (u - 1))
                for k in range(PAIR):
                    v.scalar_tensor_tensor(same[:, s % 2, k, :], PS[:, 2, (s % 2 * 2 + k) * P:(s % 2 * 2 + k + 1) * P],
                                           c_src[:, s, k:k + 1], lower_eq[:, :], ALU.is_equal, ALU.mult,
                                           accum_out=c_cnt[:, s, k:k + 1]).then_inc(s_csame, 1)
                v.tensor_scalar(c_d[:, s, :], c_src[:, s, :], -1.0, trash[:, 0:1], ALU.mult, ALU.add).then_inc(s_cix, 1)
                wait(dve, s_cix, 3 * u + 1)
                wait(dve, s_csame, PAIR * (u + 1))
                v.scalar_tensor_tensor(c_d[:, s, :], c_cnt[:, s, :], 1.5, c_d[:, s, :], ALU.is_gt, ALU.mult
                                       ).then_inc(s_cix, 1)
                wait(dve, s_cix, 3 * u + 2)
                for k in range(PAIR):
                    wait(dve, s_add[s % 2 * PAIR + k], 8 * u - 16 - 8 * (s % 2))
                v.tensor_tensor(c_idx[:, s, :], c_d[:, s, :], c_src[:, s, :], ALU.add).then_inc(s_cix, 1)

            steps(dve, NU, 0, step_c)

            def step_d(b, s, there):
                n2, n, m = (s + 2) % TURN, (s + 1) % TURN, (s - 1) % TURN
                if there(b + 2):
                    wait(dve, s_dsum, b + 3)
                    v.tensor_scalar(d_n[:, n2, 0:1], PS[:, n2 % 2, D:D + 1], 1.0, float(2 * MUL), ALU.max, ALU.mult
                                    ).then_inc(s_ddeg, 1)
                if there(b + 1):
                    wait(dve, s_ddn, b + 2)
                    v.scalar_tensor_tensor(d_o[:, n, :], PS[:, n % 2, 0:D], d_n[:, n, 1:2], d_x[:, n, D:], ALU.mult,
                                           ALU.add).then_inc(s_do, 1)
                if there(b):
                    wait(dve, s_drs, b + 1)
                    v.scalar_tensor_tensor(d_z[:, s, 0:MUL], d_o[:, s, 0:MUL], d_n[:, s, 4:5], gfull[:, 0:MUL],
                                           ALU.mult, ALU.mult).then_inc(s_dn, 1)
                    v.scalar_tensor_tensor(d_z[:, s, MUL:D], d_o[:, s, MUL:D], d_n[:, s, 5:6], gfull[:, MUL:D],
                                           ALU.mult, ALU.mult).then_inc(s_dn, 1)
                    wait(dve, s_dn, 2 * b + 2)
                    v.tensor_tensor(d_z[:, s, :], d_z[:, s, :], d_x[:, s, 0:D], ALU.add).then_inc(s_dz, 1)
                    wait(dve, s_dz, b + 1)
                    layer_norm_stats(d_z[:, s, :], s, b, s_dmv)
                if there(b - 1):
                    wait(dve, s_drstd, b)
                    wait(dve, s_dst[m], landed(b - 5, m) if there(b - 5) else 0)
                    normalized(d_out[:, m, 0:MUL], d_z[:, m, 0:MUL], m).then_inc(s_dout, 1)
                    normalized(d_out[:, m, MUL:D].rearrange("p (u d) -> p d u", d=3),
                               d_z[:, m, MUL:D].rearrange("p (d u) -> p d u", d=3), m).then_inc(s_dout, 1)
                if there(b + 1):
                    wait(dve, s_dsq, b + 2)
                    v.tensor_scalar(d_n[:, n, 2:3], d_n[:, n, 6:7], 1.0 / MUL, EPS, ALU.mult, ALU.add).then_inc(s_dms, 1)
                    v.tensor_scalar(d_n[:, n, 3:4], d_n[:, n, 7:8], 1.0 / (3 * MUL), EPS, ALU.mult, ALU.add
                                    ).then_inc(s_dms, 1)

            steps(dve, NB, 2, step_d)


_WEIGHTS = ["bias", "skip_W", "w1_s", "w1_v", "wsc_s", "wsc_v", "w2_s", "w2_v", "fc_w1", "fc_w2", "fc_w3", "g_s", "g_v"]


def kernel(**inputs):
    import concourse.bacc as bacc
    from concourse.bass_utils import run_bass_kernel_spmd

    a = {k: np.asarray(v) for k, v in inputs.items()}
    x, src, dst = a["x"], a["src"], a["dst"]
    n, e = x.shape[0], src.shape[0]
    nb, np_, ew, t = sizes(n, e)
    w = {k: a.get("L0_gnn_" + k, a.get("L1_gnn_" + k)) for k in _WEIGHTS}
    xp = np.zeros((np_, x.shape[1]), x.dtype)
    xp[:n] = x
    sd = np.zeros((2, ew * P), src.dtype)
    sd[1] = NO_NODE
    sd[0, :e], sd[1, :e] = src, dst
    sd = sd.reshape(2, ew, P)
    ea8 = np.zeros((t * P, a["edge_attr_8"].shape[1]), x.dtype)
    ea8[:e] = a["edge_attr_8"]
    ea4 = np.zeros((t * P, 4), x.dtype)
    ea4[:e] = a["edge_attr_4"]
    arrays = {
        "x": xp,
        "xT": np.ascontiguousarray(xp.T),
        "edges_sd": np.ascontiguousarray(sd.transpose(1, 0, 2)).reshape(ew, 2 * P),
        "window_ends": np.ascontiguousarray(sd[1][:, [0, P - 1]].T),
        "ea8": np.ascontiguousarray(ea8.reshape(t // 4, 2, 2 * P, -1).transpose(0, 1, 3, 2)).reshape(t // 4, -1, 2 * P),
        "ea4": np.ascontiguousarray(ea4.reshape(t, P, 4).transpose(1, 0, 2)),
        "W": a["L0_gnn_W"],
        "WT": np.ascontiguousarray(a["L0_gnn_W"].T),
        "att_src": a["L0_gnn_att_src"],
        "att_dst": a["L0_gnn_att_dst"],
        **w,
    }
    nc = bacc.Bacc("TRN2", target_bir_lowering=False, num_devices=1)
    aps = {k: nc.dram_tensor(f"in_{k}", v.shape, mybir.dt.from_np(v.dtype), kind="ExternalInput").ap()
           for k, v in arrays.items()}
    out = nc.dram_tensor("out", [np_, x.shape[1]], F32, kind="ExternalOutput").ap()
    bass_gat_equivariant_kernel(nc, out=out, n_nodes=n, n_edges=e, **aps)
    r = run_bass_kernel_spmd(nc, [{f"in_{k}": v for k, v in arrays.items()}], core_ids=[0])
    return r.results[0]["out"][:n]
```

```python
from contextlib import ExitStack

import numpy as np
import concourse.bass as bass
from concourse import mybir

F32 = mybir.dt.float32
BF16 = mybir.dt.bfloat16
I32 = mybir.dt.int32
ALU = mybir.AluOpType
ACT = mybir.ActivationFunctionType
AX = mybir.AxisListType
RMAX = bass.bass_isa.ReduceOp.max
ds = bass.ds

P = 128
NO_NODE = 1 << 20
GROUP = 4
PAIR = 2
CHUNK = 7
TURN = 4


def sizes(n_nodes, n_edges):
    nb = -(-n_nodes // (P * 2 * CHUNK)) * 2 * CHUNK
    ew = -(-n_edges // P)
    t = -(-(ew + nb - 1) // P) * P
    return nb, nb * P, ew, t


def wait(eng, s, value):
    if not (isinstance(value, int) and value <= 0):
        eng.wait_ge(s, value)


def wait_apart(eng, s, value):
    if not (isinstance(value, int) and value <= 0):
        eng.wait_ge(s, value)
        eng.nop(nofuse=True)


def landed(g, slot, dmas=1):
    return dmas * (16 // TURN * g + 16 - 16 // TURN * slot)


def steps(eng, n, lead, tail, step):
    first, last = 2 * TURN, (n - lead) // TURN * TURN
    for g in range(-lead, first):
        step(g, g % TURN, lambda v: 0 <= v < n)
    with eng.Fori(first // TURN, last // TURN) as i:
        for slot in range(TURN):
            step(i * TURN + slot, slot, lambda v: True)
    for g in range(last, n + tail):
        step(g, g % TURN, lambda v: 0 <= v < n)


def bass_gat_equivariant_kernel(nc, x, xT, edges_sd, window_ends, ea8, ea4, W, WT, att_src, att_dst, bias, skip_W,
                                w1_s, w1_v, wsc_s, wsc_v, w2_s, w2_v, fc_w1, fc_w2, fc_w3, g_s, g_v, out,
                                n_nodes, n_edges):
    NB, NP, EW, T = sizes(n_nodes, n_edges)
    D = x.shape[1]
    H, C = att_src.shape
    MUL = w1_s.shape[0]
    NBAS = fc_w1.shape[0]
    HW = D + H
    WR = D + 4
    OR = D + 1
    NG, NU, NC = T // GROUP, T // PAIR, T // P
    SLOPE, EPS = 0.2, 1e-5
    S8, S64 = float(1 / np.sqrt(float(NBAS))), float(1 / np.sqrt(float(MUL)))
    INV_SQRT3 = 0.5773502691896258
    assert D == 256 and H * C == D and MUL == C == 64 and NBAS == 8 and NB <= P and D == 4 * MUL

    def dram(name, shape, dt):
        return nc.dram_tensor(name, shape, dt).ap()

    h_tab = dram("h_tab", [NP, HW], F32)
    w_tab = dram("w_tab", [T * P, WR], F32)
    ot_tab = dram("ot_tab", [NU, P, PAIR * P], BF16)
    x1_tab = dram("x1_tab", [NP, 2 * D], F32)
    part = [dram(f"part{k}", [NP + P, OR], F32) for k in range(GROUP)]

    with ExitStack() as ctx:
        def sb(name, shape, dt=F32):
            return ctx.enter_context(nc.sbuf_tensor(name, shape, dt))

        def sem(name):
            return ctx.enter_context(nc.semaphore(name))

        def sems(prefix, names):
            return [sem(f"{prefix}_{n}") for n in names.split()]

        PS = ctx.enter_context(nc.psum_tensor("PS", [P, 8, 512], F32))

        ident = sb("ident", [P, P])
        iota_n = sb("iota_n", [P, P])
        upper = sb("upper", [P, P])
        lower_eq = sb("lower_eq", [P, P])
        ones = sb("ones", [P, P])
        zeros = sb("zeros", [P, 3 * OR])
        part_no = sb("part_no", [P, 1])
        trash = sb("trash", [P, 1])
        half = sb("half", [P, 2])
        Wx = sb("Wx", [P, 2, D + 2 * H])
        WTs = sb("WTs", [P, 2, D])
        att = sb("att", [P, 2, 2 * H])
        skw = sb("skw", [P, 2, D])
        brow = sb("brow", [1, D])
        w1m = sb("w1m", [P, 2, P])
        wscm = sb("wscm", [P, 2, P])
        w2m = sb("w2m", [P, 2, MUL])
        fc1 = sb("fc1", [2 * NBAS, P])
        fc2 = sb("fc2", [P, P])
        fc3 = sb("fc3", [P, D])
        gfull = sb("gfull", [P, D])

        logits = sb("logits", [P, NB, 3 * H])
        lt = sb("lt", [P, NB, 2 * H])
        ac3 = sb("ac3", [P, NB, 3, 2 * H], BF16)
        pself = sb("pself", [P, NB, H])
        rden = sb("rden", [P, NB, H])
        amax = sb("amax", [P, H])
        gmax = sb("gmax", [P, H])
        srcF = sb("srcF", [P, T])
        dloc = sb("dloc", [P, T], BF16)
        valid = sb("valid", [P, T], BF16)
        rows = sb("rows", [33, T], I32)
        block_row, window_row = rows[0:1, :], rows[32:33, :]

        BIG = max(NB * HW, 2 * EW + 2 * T + 4 * NC * P)
        big = sb("big", [P, BIG])
        acc = big[:, 0:NB * HW].rearrange("p (b d) -> p b d", d=HW)
        ARENA = 11400
        arena = sb("arena", [P, ARENA])
        used = [0]

        def cut(n, new_stage=False):
            at = 0 if new_stage else used[0]
            used[0] = at + n
            assert used[0] <= ARENA
            return arena[:, at:at + n]

        ends = big[0:NB, 0:2 * EW].rearrange("p (s w) -> p s w", s=2)
        iota_t = big[:, 2 * EW:2 * EW + T]
        stepm = big[0:NB, 2 * EW + T:2 * EW + 2 * T]
        at = 2 * EW + 2 * T
        sd_in = big[:, at:at + 2 * NC * P].bitcast(I32).rearrange("p (c w e) -> p c w e", c=NC, w=2)
        sd_f = big[:, at + 2 * NC * P:at + 4 * NC * P].rearrange("p (c w e) -> p c w e", c=NC, w=2)
        x_in = cut(4 * CHUNK * P, True).rearrange("p (s k n) -> p s k n", s=2, k=2)
        h_out = cut(2 * CHUNK * HW).rearrange("p (s k d) -> p s k d", s=2, k=CHUNK)
        bounds = sb("bounds", [P, 2])
        cnt = sb("cnt", [P, 8])
        two = sb("two", [P, 33])
        b128 = sb("b128", [P, NC])
        tile_col = sb("tile_col", [P, NC])
        wcol = sb("wcol", [P, NC], I32)

        hg = cut(TURN * GROUP * HW, True).rearrange("p (s k d) -> p s k d", s=TURN, k=GROUP)
        oh = cut(TURN * GROUP * P).rearrange("p (s k n) -> p s k n", s=TURN, k=GROUP)
        ots = cut(GROUP * P).bitcast(BF16).rearrange("p (s k e) -> p s k e", s=2, k=GROUP)
        wst = cut(2 * GROUP * WR).rearrange("p (s k d) -> p s k d", s=2, k=GROUP)
        eat, t1, t2, h1, h2 = (cut(2 * 2 * P).rearrange("p (s e) -> p s e", s=2) for _ in range(5))
        sidx = sb("sidx", [P, TURN, GROUP], I32)
        za = sb("za", [P, 2, GROUP, H])
        ad = sb("ad", [P, 2, GROUP, 2 * H])
        zb = sb("zb", [P, 2, GROUP, H])
        sh = sb("sh", [P, TURN, GROUP, 4])

        b_h = cut(TURN * D, True).rearrange("p (s d) -> p s d", s=TURN)
        b_x = cut(TURN * D).rearrange("p (s d) -> p s d", s=TURN)
        b_xT = cut(TURN * 2 * P).rearrange("p (s k n) -> p s k n", s=TURN, k=2)
        b_v = cut(TURN * D).rearrange("p (s d) -> p s d", s=TURN)
        b_e = cut(TURN * D).rearrange("p (s d) -> p s d", s=TURN)
        b_x1 = cut(TURN * 2 * D).rearrange("p (s d) -> p s d", s=TURN)
        b_x1T = cut(2 * 2 * P).rearrange("p (s k n) -> p s k n", s=2, k=2)
        stat = sb("stat", [P, TURN, 6])
        mv = sb("mv", [P, TURN, 4])

        wt = cut(TURN * PAIR * WR, True).rearrange("p (s k d) -> p s k d", s=TURN, k=PAIR)
        c_ot = cut(TURN * PAIR * P // 2).bitcast(BF16).rearrange("p (s k e) -> p s k e", s=TURN, k=PAIR)
        c_otf = cut(2 * PAIR * P).rearrange("p (s k e) -> p s k e", s=2, k=PAIR)
        mid = cut(2 * PAIR * 2 * D).rearrange("p (s k c u) -> p s k c u", s=2, k=PAIR, c=8)
        midT = cut(2 * PAIR * 4 * P).rearrange("p (s k c e) -> p s k c e", s=2, k=PAIR, c=4)
        same = cut(TURN * PAIR * P).rearrange("p (s k e) -> p s k e", s=TURN, k=PAIR)
        o_cmb = cut(GROUP * OR).rearrange("p (k d) -> p k d", k=GROUP)
        evs = cut(PAIR * 3 * MUL).rearrange("p (k d u) -> p k d u", k=PAIR, d=3)
        evt = cut(PAIR * MUL).rearrange("p (k u) -> p k u", k=PAIR)
        c_src = sb("c_src", [P, TURN, PAIR])
        c_val = sb("c_val", [P, TURN, PAIR])
        c_cnt = sb("c_cnt", [P, TURN, PAIR])
        c_d = sb("c_d", [P, TURN, PAIR])
        c_idx = sb("c_idx", [P, TURN, PAIR], I32)

        d_p = cut(TURN * GROUP * OR, True).rearrange("p (s k d) -> p s k d", s=TURN, k=GROUP)
        d_x = cut(TURN * 2 * D).rearrange("p (s d) -> p s d", s=TURN)
        d_o = cut(TURN * D).rearrange("p (s d) -> p s d", s=TURN)
        d_q = cut(TURN * D).rearrange("p (s d) -> p s d", s=TURN)
        d_z = cut(TURN * D).rearrange("p (s d) -> p s d", s=TURN)
        d_out = b_out = sb("d_out", [P, TURN, D])
        d_n = sb("d_n", [P, TURN, 8])

        (s_iota, s_zeroed, s_const, s_w, s_scaled, s_ends, s_tab, s_tabp, s_win, s_watt, s_hwatt, s_zero) = sems(
            "s", "iota zeroed const w scaled ends tab tabp win watt hwatt zero")
        s_xin = sems("s_xin", "0 1")
        s_hst = sems("s_hst", "0 1")
        s_hps, s_hev, s_sdin, s_sdf, s_sdp, s_sdT, s_amax, s_gmax, s_lg, s_self, s_acc0, s_dl = sems(
            "s", "hps hev sdin sdf sdp sdT amax gmax lg self acc0 dl")
        (s_idx, s_oh, s_otp, s_ots, s_ad, s_z, s_p, s_msg, s_agg, s_acc, s_f1, s_t1, s_h1, s_f2, s_t2, s_h2, s_f3,
         s_wev) = sems("a", "idx oh otp ots ad z p msg agg acc f1 t1 h1 f2 t2 h2 f3 wev")
        slots = "0 1 2 3"
        s_hg, s_otst, s_ea, s_sh, s_wst = (sems(f"a_{n}", slots) for n in ("hg", "otst", "ea", "sh", "wst"))
        (s_rden, s_bt, s_bsum, s_bskip, s_bv, s_bm, s_be, s_belu, s_bs, s_bmv, s_brstd, s_bx1, s_bxp, s_bxT, s_by,
         s_bout) = sems("b", "rden t sum skip v m e elu s mv rstd x1 xp xT y out")
        s_bin, s_bst = sems("b_in", slots), sems("b_st", slots)
        (s_csl, s_cotf, s_cy, s_csr, s_csame, s_cix, s_cpr, s_cmid, s_cmt, s_cmT, s_co, s_ccmb) = sems(
            "c", "sl otf y sr same ix pr mid mt mT o cmb")
        s_cw, s_cot, s_add = sems("c_w", slots), sems("c_ot", slots), sems("c_add", slots)
        (s_dsum, s_ddeg, s_ddn, s_do, s_dsq, s_dms, s_drs, s_dn, s_dz, s_dmv, s_drstd, s_dout) = sems(
            "d", "sum deg dn o sq ms rs n z mv rstd out")
        s_din, s_dx, s_dst = sems("d_in", slots), sems("d_x", slots), sems("d_st", slots)

        block = ctx.enter_context(nc.Block())
        TAB_WINDOWS, TAB_STEPS = 5, 8
        LG_PARTS, LG_SELF = 6, 9
        N_W = 2 + 2 * H + 2 + 8 + 2 + 2 * 6 + 4
        NCH = NB // CHUNK
        xv = xT.rearrange("(k p) n -> p k n", p=P)
        x1b = x1_tab.rearrange("(b p) d -> b p d", p=P)

        def one(v, i):
            return v[ds(i, 1)].rearrange("o p d -> (o p) d")

        def numbers(eng, row, at, n, below):
            return nc.values_load_multi_w_load_instructions(row[:, ds(at, n)], engines=(eng.engine,), min_val=0,
                                                            max_val=below - 1)[1]

        @block.sync
        def _(sp):
            loads = [0]

            def load(to, what):
                sp.dma_start(to, what).then_inc(s_w, 16)
                loads[0] += 1

            sp.dma_start(ends.bitcast(I32), window_ends.rearrange("(o s) w -> o s w", o=1).to_broadcast([NB, 2, EW])
                         ).then_inc(s_ends, 16)
            load(WTs[:, :, :], WT.rearrange("(k p) n -> p k n", p=P))
            load(Wx[:, :, 0:D], W.rearrange("(k p) n -> p k n", p=P))
            sp.wait_ge(s_zeroed, 1)
            for h in range(H):
                at = h % 2 * C
                load(att[at:at + C, h // 2, h:h + 1], att_src[h].rearrange("(c o) -> c o", o=1))
                load(att[at:at + C, h // 2, H + h:H + h + 1], att_dst[h].rearrange("(c o) -> c o", o=1))
            load(skw[:, :, :], skip_W.rearrange("(k p) n -> p k n", p=P))
            load(brow[:, :], bias.rearrange("(o n) -> o n", o=1))
            for m, s_part, v_part in ((w1m, w1_s, w1_v), (wscm, wsc_s, wsc_v)):
                load(m[0:MUL, 0, 0:MUL], s_part)
                load(m[MUL:P, 0, MUL:P], v_part)
                load(m[0:MUL, 1, 0:MUL], v_part)
                load(m[MUL:P, 1, MUL:P], v_part)
            load(w2m[:, 0, :], w2_s)
            load(w2m[:, 1, :], w2_v)
            for i in range(2):
                load(fc1[i * NBAS:(i + 1) * NBAS, i * MUL:(i + 1) * MUL], fc_w1)
                load(fc2[i * MUL:(i + 1) * MUL, i * MUL:(i + 1) * MUL], fc_w2)
                for to, of in ((0, 0), (1, 2), (2, 1), (3, 3)):
                    load(fc3[i * MUL:(i + 1) * MUL, to * MUL:(to + 1) * MUL], fc_w3[:, of * MUL:(of + 1) * MUL])
            load(gfull[:, 0:MUL], g_s.rearrange("(o n) -> o n", o=1).to_broadcast([P, MUL]))
            for d in range(1, 4):
                load(gfull[:, MUL * d:MUL * (d + 1)], g_v.rearrange("(o n) -> o n", o=1).to_broadcast([P, MUL]))
            assert loads[0] == N_W

            def load_x(c, s, before):
                wait(sp, s_hps, before)
                sp.dma_start(x_in[:, s, :, :], xv[:, :, ds(c * (CHUNK * P), CHUNK * P)]).then_inc(s_xin[s], 16)

            for c in range(2):
                load_x(c, c, 0)
            with sp.Fori(1, NCH // 2) as i:
                for s in range(2):
                    load_x(i * 2 + s, s, (i * 2 + s - 1) * CHUNK)

            sp.wait_ge(s_hst[0], 16 * (NCH // 2))
            sp.wait_ge(s_hst[1], 16 * (NCH // 2))
            sp.wait_ge(s_sdp, NC)

            def step_a(g, s, there):
                if there(g + 2):
                    wait(sp, s_f1, g + 1)
                    sp.dma_start(eat[0:2 * NBAS, s % 2, :], one(ea8, g + 2)).then_inc(s_ea[(s + 2) % TURN], 16)
                if there(g):
                    wait(sp, s_wev, 6 * (g - 3))
                    sp.dma_start(sh[:, s, :, :], ea4[:, ds(g * GROUP, GROUP), :]).then_inc(s_sh[s], 16)
                n = (s + 1) % TURN
                if there(g + 1):
                    wait(sp, s_ots, g + 2)
                    sp.dma_start(ot_tab[ds((g + 1) * 2, 2), :, :].rearrange("q p e -> p q e"),
                                 ots[:, n % 2, :, :].rearrange("p (q k) e -> p q (k e)", q=2)).then_inc(s_otst[n], 16)
                if there(g - 3):
                    wait(sp, s_wev, 6 * (g - 2))
                    sp.dma_start(w_tab[ds((g - 3) * (GROUP * P), GROUP * P), :].rearrange("(k p) d -> p k d", p=P),
                                 wst[:, n % 2, :, :]).then_inc(s_wst[n], 16)

            steps(sp, NG, 2, 3, step_a)
            for s in range(TURN):
                sp.wait_ge(s_wst[s], 16 * (NG // TURN))
                sp.wait_ge(s_otst[s], 16 * (NG // TURN))

            sp.wait_ge(s_acc, GROUP * NG)
            xb = x.rearrange("(b p) d -> b p d", p=P)
            hb = h_tab.rearrange("(b p) d -> b p d", p=P)

            def step_b(b, s, there):
                n = (s + 3) % TURN
                if there(b + 3):
                    wait(sp, s_bv, b)
                    wait(sp, s_bs, b)
                    wait(sp, s_bskip, b)
                    sp.dma_start(b_h[:, n, :], hb[ds(b + 3, 1), :, 0:D].rearrange("o p d -> (o p) d")
                                 ).then_inc(s_bin[n], 16)
                    sp.dma_start(b_x[:, n, :], one(xb, b + 3)).then_inc(s_bin[n], 16)
                    sp.dma_start(b_xT[:, n, :, :], xv[:, :, ds((b + 3) * P, P)]).then_inc(s_bin[n], 16)
                m = (s - 2) % TURN
                if there(b - 2):
                    wait(sp, s_bout, 2 * (b - 1))
                    sp.dma_start(one(x1b, b - 2), b_x1[:, m, :]).then_inc(s_bst[m], 16)

            steps(sp, NB, 3, 2, step_b)
            for s in range(TURN):
                sp.wait_ge(s_bst[s], 16 * len(range(s, NB, TURN)))

            wv = w_tab.rearrange("(w p) d -> w p d", p=P)

            def step_c(u, s, there):
                if there(u + 4):
                    wait(sp, s_cotf, u + 1)
                    sp.dma_start(c_ot[:, s, :, :].rearrange("p k e -> p (k e)"), one(ot_tab, u + 4)
                                 ).then_inc(s_cot[s], 16)
                n = (s + 3) % TURN
                if there(u + 3):
                    w = numbers(sp, window_row, (u + 3) * PAIR, PAIR, EW)
                    wait(sp, s_cmid, u)
                    for k in range(PAIR):
                        sp.dma_start(wt[:, n, k, :], one(wv, w[k])).then_inc(s_cw[n], 16)

            steps(sp, NU, 4, 0, step_c)

            for k in range(GROUP):
                sp.wait_ge(s_add[k], 16 * NG)
            pb = [q.rearrange("(b p) d -> b p d", p=P) for q in part]
            ob = out.rearrange("(b p) d -> b p d", p=P)

            def step_d(b, s, there):
                if there(b + 4):
                    wait(sp, s_dsum, b + 1)
                    for k in range(GROUP):
                        sp.dma_start(d_p[:, s, k, :], one(pb[k], b + 4)).then_inc(s_din[s], 16)
                n = (s + 2) % TURN
                if there(b + 2):
                    wait(sp, s_dz, b - 1)
                    sp.dma_start(d_x[:, n, :], one(x1b, b + 2)).then_inc(s_dx[n], 16)
                if there(b - 2):
                    wait(sp, s_dout, 2 * (b - 1))
                    sp.dma_start(one(ob, b - 2), d_out[:, n, :]).then_inc(s_dst[n], 16)

            steps(sp, NB, 4, 2, step_d)
            for s in range(TURN):
                sp.wait_ge(s_dst[s], 16 * len(range(s, NB, TURN)))

        @block.gpsimd
        def _(pool):
            g = nc.gpsimd
            g.iota(iota_n[:, :], [[1, P]], base=0, channel_multiplier=0, allow_small_or_imprecise_dtypes=True)
            g.iota(part_no[:, :], [[0, 1]], base=0, channel_multiplier=1, allow_small_or_imprecise_dtypes=True)
            g.iota(trash[:, :], [[0, 1]], base=NP, channel_multiplier=1, allow_small_or_imprecise_dtypes=True)
            g.iota(bounds[:, :], [[P, 2]], base=0, channel_multiplier=P, allow_small_or_imprecise_dtypes=True)
            g.iota(tile_col[:, :], [[P, NC]], base=0, channel_multiplier=1, allow_small_or_imprecise_dtypes=True)
            g.iota(iota_t, [[1, T]], base=0, channel_multiplier=0, allow_small_or_imprecise_dtypes=True)
            g.memset(half[:, :], -0.5).then_inc(s_iota, 1)

            hv = h_tab.rearrange("(c k p) d -> c p k d", k=CHUNK, p=P)

            def store_h(c, s):
                wait_apart(pool, s_hev, 2 * CHUNK * (c + 1))
                pool.dma_start(hv[ds(c, 1)].rearrange("o p k d -> (o p) k d"), h_out[:, s, :, :]
                               ).then_inc(s_hst[s], 16)

            for c in range(2):
                store_h(c, c)
            with pool.Fori(1, NCH // 2) as i:
                for s in range(2):
                    store_h(i * 2 + s, s)

            pool.wait_ge(s_win, 1)
            for c in range(NC):
                pool.indirect_dma_start(sd_in[:, c, :, :].rearrange("p w e -> p (w e)"), None, edges_sd,
                                        bass.IndirectOffsetOnAxis(ap=wcol[:, c:c + 1], axis=0)
                                        ).then_inc(s_sdin, 16)
            pool.wait_ge(s_amax, 1)
            g.partition_all_reduce(gmax[:, :], amax[:, :], P, RMAX).then_inc(s_gmax, 1)

            for s in range(2):
                pool.wait_ge(s_hst[s], 16 * (NCH // 2))

            def step_a(g, s, there):
                if there(g):
                    wait_apart(pool, s_idx, g + 1)
                    for k in range(GROUP):
                        wait_apart(pool, s_agg, GROUP * (g - TURN) + k + 1)
                        pool.indirect_dma_start(hg[:, s, k, :], None, h_tab,
                                                bass.IndirectOffsetOnAxis(ap=sidx[:, s, k:k + 1], axis=0)
                                                ).then_inc(s_hg[s], 16)

            steps(pool, NG, 0, 0, step_a)

            pool.wait_ge(s_self, 1)

            def step_b(b, s, there):
                n = (s + 2) % TURN
                if there(b + 2):
                    wait_apart(pool, s_bin[n], landed(b + 2, n, 3))
                    g.tensor_tensor(b_h[:, n, :].rearrange("p (h c) -> p h c", h=H),
                                    b_h[:, n, :].rearrange("p (h c) -> p h c", h=H),
                                    pself[:, ds(b + 2, 1), :].rearrange("p o (h c) -> p (o h) c", c=1
                                                                        ).to_broadcast([P, H, C]),
                                    ALU.mult).then_inc(s_bt, 1)
                if there(b):
                    wait(pool, s_bmv, 3 * (b + 1))
                    g.tensor_tensor(mv[:, s, 3:4], mv[:, s, 2:3], half[:, 0:1], ALU.pow).then_inc(s_brstd, 1)

            steps(pool, NB, 2, 0, step_b)

            pool.wait_ge(s_zero, 16 * GROUP)
            def step_c(u, s, there):
                if there(u):
                    wait_apart(pool, s_cix, 3 * (u + 1))
                    for k in range(PAIR):
                        q = s % 2 * PAIR + k
                        wait_apart(pool, s_ccmb, u + 1)
                        wait_apart(pool, s_add[q], 8 * u - 8 * (s % 2))
                        pool.indirect_dma_start(part[q], bass.IndirectOffsetOnAxis(ap=c_idx[:, s, k:k + 1], axis=0),
                                                o_cmb[:, q, :], None, compute_op=ALU.add).then_inc(s_add[q], 16)

            steps(pool, NU, 0, 0, step_c)

            def step_d(b, s, there):
                m, n = (s - 1) % TURN, (s + 2) % TURN
                if there(b - 1):
                    wait(pool, s_dmv, 3 * b)
                    g.tensor_tensor(mv[:, m, 3:4], mv[:, m, 2:3], half[:, 0:1], ALU.pow).then_inc(s_drstd, 1)
                if there(b):
                    wait(pool, s_dms, 2 * (b + 1))
                    g.tensor_tensor(d_n[:, s, 4:6], d_n[:, s, 2:4], half[:, 0:2], ALU.pow).then_inc(s_drs, 1)
                if there(b + 2):
                    wait(pool, s_ddeg, b + 3)
                    g.tensor_tensor(d_n[:, n, 1:2], d_n[:, n, 0:1], half[:, 0:1], ALU.pow).then_inc(s_ddn, 1)

            steps(pool, NB, 2, 1, step_d)

        @block.scalar
        def _(act):
            a = nc.scalar
            act.wait_ge(s_zeroed, 1)
            for k in range(GROUP):
                c = 3 if (NB + 1) % 3 == 0 else 1
                act.dma_start(part[k].rearrange("(p r c) d -> p r (c d)", p=P, c=c),
                              zeros[:, 0:c * OR].rearrange("p (o d) -> p o d", o=1
                                                           ).to_broadcast([P, (NB + 1) // c, c * OR])
                              ).then_inc(s_zero, 16)

            act.wait_ge(s_watt, 1)
            a.copy(Wx[:, :, D:], PS[:, 6, 0:4 * H].rearrange("p (k j) -> p k j", k=2)).then_inc(s_hwatt, 1)

            def evacuate_h(c, s, stored):
                wait_apart(act, s_hst[s], stored)
                for k in range(CHUNK):
                    wait_apart(act, s_hps, CHUNK * c + k + 1)
                    a.copy(h_out[:, s, k, :], PS[:, k, 0:HW]).then_inc(s_hev, 1)
                    a.copy(logits[:, ds(c * CHUNK + k, 1), 0:2 * H].rearrange("p o j -> p (o j)"),
                           PS[:, k, D:D + 2 * H]).then_inc(s_hev, 1)

            for c in range(2):
                evacuate_h(c, c, 0)
            with act.Fori(1, NCH // 2) as i:
                for s in range(2):
                    evacuate_h(i * 2 + s, s, i * 16)

            for c in range(NC):
                act.wait_ge(s_sdp, c + 1)
                a.copy(srcF[:, c * P:(c + 1) * P], PS[:, c % 2, 0:P]).then_inc(s_sdT, 1)
            act.wait_ge(s_lg, LG_SELF)
            a.activation(pself[:, :, :], lt[:, :, 0:H], ACT.Exp).then_inc(s_self, 1)

            act.wait_ge(s_sdT, NC)

            def sources(g, s):
                a.copy(sidx[:, s, :], srcF[:, ds(g * GROUP, GROUP)]).then_inc(s_idx, 1)

            def step_a(g, s, there):
                n, m, o = (s + 1) % TURN, (s - 1) % TURN, (s - 3) % TURN

                def radial_weights(i):
                    wait(act, s_f3, 2 * (g - 3) + i + 1)
                    for k in (2 * i, 2 * i + 1):
                        a.mul(wst[:, o % 2, k, 0:2 * MUL], PS[:, 4 + i, k % 2 * D:k % 2 * D + 2 * MUL],
                              sh[:, o, k, 0:1]).then_inc(s_wev, 1)
                    a.copy(wst[:, o % 2, 2 * i:2 * i + 2, 2 * MUL:D],
                           PS[:, 4 + i, :].rearrange("p (k d) -> p k d", k=2)[:, :, 2 * MUL:D]).then_inc(s_wev, 1)

                if there(g + 1):
                    wait(act, s_otp, g + 2)
                    wait(act, s_otst[m], landed(g - 1, m) if there(g - 1) else 0)
                    wait(act, s_ad, g)
                    a.copy(ots[:, n % 2, :, :], PS[:, 0, :].rearrange("p (k e) -> p k e", k=GROUP)
                           ).then_inc(s_ots, 1)
                if there(g - 3):
                    wait(act, s_wst[m], landed(g - 5, m) if there(g - 5) else 0)
                    wait(act, s_sh[o], landed(g - 3, o))
                    a.copy(wst[:, o % 2, :, D:WR], sh[:, o, :, :])
                    radial_weights(0)
                if there(g):
                    wait(act, s_z, 4 * (g + 1))
                    a.activation(hg[:, s, :, D:HW], za[:, s % 2, :, :], ACT.Exp).then_inc(s_p, 1)
                if there(g - 3):
                    radial_weights(1)
                if there(g + 3):
                    sources(g + 3, (s + 3) % TURN)
                if there(g - 1):
                    wait(act, s_f2, g)
                    wait(act, s_h2, g - 2)
                    a.activation(t2[:, m % 2, :], PS[:, 7, 0:2 * P], ACT.Tanh, scale=0.5).then_inc(s_t2, 1)
                if there(g + 1):
                    wait(act, s_f1, g + 2)
                    wait(act, s_h1, g)
                    a.activation(t1[:, n % 2, :], PS[:, 6, 0:2 * P], ACT.Tanh, scale=0.5).then_inc(s_t1, 1)

            steps(act, NG, 3, 3, step_a)

            def step_b(b, s, there):
                m, o, n = (s - 1) % TURN, (s - 2) % TURN, (s + 1) % TURN
                if there(b - 1):
                    wait(act, s_bxp, b)
                    wait(act, s_by, b - 2)
                    a.copy(b_x1T[:, m % 2, :, :], PS[:, 2, 0:256].rearrange("p (k n) -> p k n", k=2)).then_inc(s_bxT, 1)
                if there(b - 2):
                    wait(act, s_by, b - 1)
                    a.copy(acc[:, ds(b - 2, 1), 0:D].rearrange("p o d -> p (o d)"), PS[:, 3, 0:D]).then_inc(s_bout, 1)
                    a.copy(b_x1[:, o, D:], PS[:, 4, 0:D]).then_inc(s_bout, 1)
                if there(b + 1):
                    wait(act, s_bm, b + 2)
                    a.activation(b_e[:, n, :], b_e[:, n, :], ACT.Exp).then_inc(s_be, 1)

            steps(act, NB, 1, 2, step_b)

            def step_c(u, s, there):
                n, m, o = (s + 1) % TURN, (s - 1) % TURN, (s + 2) % TURN
                if there(u + 1):
                    wait_apart(act, s_cix, 3 * (u - 2))
                    wait_apart(act, s_co, u - 2)
                    a.copy(c_src[:, n, :], srcF[:, ds((u + 1) * PAIR, PAIR)])
                    a.copy(c_val[:, n, :], valid[:, ds((u + 1) * PAIR, PAIR)]).then_inc(s_csl, 1)
                if there(u - 1):
                    wait(act, s_co, u - 2)
                    for k in range(PAIR):
                        wait(act, s_cmt, PAIR * (u - 1) + k + 1)
                        a.copy(midT[:, m % 2, k, :, :], PS[:, 4 + k, :].rearrange("p (c e) -> p c e", c=4)
                               ).then_inc(s_cmT, 1)
                if there(u + 2):
                    wait(act, s_cot[o], landed(u + 2, o))
                    wait(act, s_cy, u + 1)
                    a.copy(c_otf[:, o % 2, :, :], c_ot[:, o, :, :]).then_inc(s_cotf, 1)
                if there(u - 2):
                    q = o % 2 * PAIR
                    wait(act, s_co, u - 1)
                    for k in range(PAIR):
                        wait(act, s_add[q + k], 8 * (u - 2) - 8 * (o % 2))
                    a.copy(o_cmb[:, q:q + PAIR, 0:D], PS[:, 6, :].rearrange("p (k d) -> p k d", k=PAIR))
                    a.copy(o_cmb[:, q:q + PAIR, D:OR], PS[:, 7, 0:PAIR].rearrange("p (k d) -> p k d", k=PAIR)
                           ).then_inc(s_ccmb, 1)

            steps(act, NU, 2, 2, step_c)

            def step_d(b, s, there):
                n = (s + 1) % TURN
                if there(b + 1):
                    wait(act, s_do, b + 2)
                    wait(act, s_dms, 2 * (b - 2))
                    a.activation(d_q[:, n, 0:MUL], d_o[:, n, 0:MUL], ACT.Square, accum_out=d_n[:, n, 6:7])
                    a.activation(d_q[:, n, MUL:D], d_o[:, n, MUL:D], ACT.Square, accum_out=d_n[:, n, 7:8]).then_inc(s_dsq, 1)

            steps(act, NB, 1, 0, step_d)

        @block.tensor
        def _(pe):
            mm = nc.tensor.matmul
            pe.wait_ge(s_const, 1)
            pe.wait_ge(s_tab, TAB_WINDOWS)
            mm(PS[0:NB, 7, 64:65], upper[0:NB, 0:NB], cnt[0:NB, 3:4], start=True, stop=True).then_inc(s_tabp, 1)
            pe.wait_ge(s_tab, TAB_STEPS)
            for c in range(NC):
                mm(PS[:, 7, 128 + 2 * c:130 + 2 * c], stepm[:, c * P:(c + 1) * P], two[0:NB, 0:33:32],
                   start=True, stop=True)
            for c in range(-(-T // 512)):
                e = min(T, (c + 1) * 512)
                last = mm(PS[0:33, c, 0:e - c * 512], two[0:NB, :], stepm[:, c * 512:e], start=True, stop=True)
            last.then_inc(s_tabp, 1)
            pe.wait_ge(s_w, 16 * N_W)
            for k in range(2):
                for m in range(2):
                    last = mm(PS[:, 6, k * 2 * H:(k + 1) * 2 * H], WTs[:, m, k * P:(k + 1) * P], att[:, m, :],
                              start=(m == 0), stop=(m == 1))
            last.then_inc(s_watt, 1)
            pe.wait_ge(s_hwatt, 1)
            pe.wait_ge(s_win, 1)

            def node_maps(c, s, arrived):
                pe.wait_ge(s_xin[s], arrived)
                for k in range(CHUNK):
                    wait(pe, s_hev, 2 * (CHUNK * (c - 1) + k + 1))
                    for j in range(2):
                        last = mm(PS[:, k, 0:D + 2 * H], x_in[:, s, j, k * P:(k + 1) * P], Wx[:, j, :],
                                  start=(j == 0), stop=(j == 1))
                    last.then_inc(s_hps, 1)

            for c in range(2):
                node_maps(c, c, 16)
            with pe.Fori(1, NCH // 2) as i:
                for s in range(2):
                    node_maps(i * 2 + s, s, i * 16 + 16)

            pe.wait_ge(s_hev, 2 * NB)
            for c in range(NC):
                pe.wait_ge(s_sdf, 1)
                if c >= 2:
                    pe.wait_ge(s_sdT, c - 1)
                    pe.wait_ge(s_dl, c - 1)
                nc.tensor.transpose(PS[:, c % 2, 0:P], sd_f[:, c, 0, :], ident[:, :])
                nc.tensor.transpose(PS[:, 2 + c % 2, 0:P], sd_f[:, c, 1, :], ident[:, :]).then_inc(s_sdp, 1)

            pe.wait_ge(s_sdT, NC)
            pe.wait_ge(s_dl, NC)
            pe.wait_ge(s_scaled, 1)
            pe.wait_ge(s_lg, LG_PARTS)

            def step_a(g, s, there):
                n, m, o = (s + 1) % TURN, (s - 1) % TURN, (s - 3) % TURN

                def third_layer(i):
                    wait(pe, s_h2, g - 2)
                    wait(pe, s_wev, 6 * (g - 4) + 3 * i + 3)
                    for k in range(2):
                        last = mm(PS[:, 4 + i, k * D:(k + 1) * D], h2[i * MUL:(i + 1) * MUL, o % 2, k * P:(k + 1) * P],
                                  fc3[i * MUL:(i + 1) * MUL, :], start=True, stop=True)
                    last.then_inc(s_f3, 1)

                def sums(k):
                    t = GROUP * (g - 1) + k
                    wait(pe, s_msg, t + 1)
                    wait(pe, s_acc, t - 1)
                    mm(PS[:, 2 + k % 2, 0:HW], oh[:, m, k, :], hg[:, m, k, :], start=True, stop=True).then_inc(s_agg, 1)

                if there(g + 1):
                    wait(pe, s_oh, g + 2)
                    wait(pe, s_ots, g + 1)
                    for k in range(GROUP):
                        last = nc.tensor.transpose(PS[:, 0, k * P:(k + 1) * P], oh[:, n, k, :], ident[:, :])
                    last.then_inc(s_otp, 1)
                if there(g - 3):
                    third_layer(0)
                if there(g):
                    b = numbers(pe, block_row, g * GROUP, GROUP, NB)
                    wait(pe, s_ots, g + 1)
                    wait(pe, s_z, 4 * (g - 1) + 1)
                    for k in range(GROUP):
                        last = mm(PS[:, 1, k * 6 * H:(k + 1) * 6 * H], ots[:, s % 2, k, :],
                                  ac3[:, ds(b[k], 1), :, :].rearrange("p o i j -> p (o i j)"), start=True, stop=True)
                    last.then_inc(s_ad, 1)
                if there(g - 1):
                    sums(0)
                    sums(1)
                if there(g - 3):
                    third_layer(1)
                if there(g - 1):
                    sums(2)
                    sums(3)
                if there(g - 1):
                    wait(pe, s_h1, g)
                    wait(pe, s_h2, g - 1)
                    mm(PS[:, 7, 0:2 * P], fc2[:, :], h1[:, m % 2, :], start=True, stop=True).then_inc(s_f2, 1)
                if there(g + 1):
                    wait(pe, s_ea[n], landed(g + 1, n))
                    wait(pe, s_h1, g + 1)
                    mm(PS[:, 6, 0:2 * P], fc1[:, :], eat[0:2 * NBAS, n % 2, :], start=True, stop=True).then_inc(s_f1, 1)

            steps(pe, NG, 1, 3, step_a)

            pe.wait_ge(s_acc, GROUP * NG)
            pe.wait_ge(s_wev, 6 * NG)

            def step_b(b, s, there):
                m, n = (s - 1) % TURN, (s + 2) % TURN
                if there(b - 2):
                    wait(pe, s_bxT, b - 1)
                    wait(pe, s_bout, 2 * (b - 2))
                    for j in range(2):
                        mm(PS[:, 3, j * P:(j + 1) * P], b_x1T[:, n % 2, j, :], w1m[:, j, :], start=True, stop=True)
                    for j in range(2):
                        last = mm(PS[:, 4, j * P:(j + 1) * P], b_x1T[:, n % 2, j, :], wscm[:, j, :], start=True, stop=True)
                    last.then_inc(s_by, 1)
                if there(b + 2):
                    wait(pe, s_bin[n], landed(b + 2, n, 3))
                    wait(pe, s_bv, b + 1)
                    mm(PS[:, n % 2, 0:D], b_xT[:, n, 0, :], skw[:, 0, :], start=True, stop=False)
                    mm(PS[:, n % 2, 0:D], b_xT[:, n, 1, :], skw[:, 1, :], start=False, stop=False)
                    mm(PS[:, n % 2, 0:D], ones[0:1, :], brow[:, :], start=False, stop=True).then_inc(s_bskip, 1)
                if there(b - 1):
                    wait(pe, s_bx1, 2 * b)
                    wait(pe, s_bxT, b - 1)
                    for j in range(2):
                        last = nc.tensor.transpose(PS[:, 2, j * P:(j + 1) * P], b_x1[:, m, j * P:(j + 1) * P], ident[:, :])
                    last.then_inc(s_bxp, 1)

            steps(pe, NB, 2, 2, step_b)

            pe.wait_ge(s_bout, 2 * NB)

            def step_c(u, s, there):
                n, m, o = (s + 1) % TURN, (s - 1) % TURN, (s - 2) % TURN
                if there(u + 1):
                    b = numbers(pe, block_row, (u + 1) * PAIR, PAIR, NB)
                if there(u - 1):
                    wait(pe, s_csame, PAIR * u)
                    wait(pe, s_cmid, u)
                    for k in range(PAIR):
                        wait(pe, s_cmT, PAIR * (u - 2) + k + 1)
                        for j in range(4):
                            last = mm(PS[:, 4 + k, j * P:(j + 1) * P],
                                      mid[:, m % 2, k, 2 * j:2 * j + 2, :].rearrange("p c u -> p (c u)"),
                                      same[:, m, k, :], start=True, stop=True)
                        last.then_inc(s_cmt, 1)
                if there(u - 2):
                    wait(pe, s_cmT, PAIR * (u - 1))
                    wait(pe, s_ccmb, u - 2)
                    for k in range(PAIR):
                        mm(PS[:, 7, k:k + 1], same[:, o, k, :], c_val[:, o, k:k + 1], start=True, stop=True)
                        for j in range(4):
                            last = mm(PS[:, 6, k * D + j * MUL:k * D + (j + 1) * MUL], midT[:, o % 2, k, j, :],
                                      w2m[:, min(j, 1), :], start=True, stop=True)
                    last.then_inc(s_co, 1)
                if there(u + 1):
                    wait(pe, s_cotf, u + 2)
                    wait(pe, s_cmid, u)
                    for k in range(PAIR):
                        last = mm(PS[:, n % 2, k * D:(k + 1) * D], c_otf[:, n % 2, k, :],
                                  acc[:, ds(b[k], 1), 0:D].rearrange("p o d -> p (o d)"), start=True, stop=True)
                    last.then_inc(s_cy, 1)
                    wait(pe, s_csl, u + 2)
                    wait(pe, s_csame, PAIR * u)
                    for k in range(PAIR):
                        last = nc.tensor.transpose(PS[:, 2 + n % 2, k * P:(k + 1) * P],
                                                   c_src[:, n, k:k + 1].to_broadcast([P, P]), ident[:, :])
                    last.then_inc(s_csr, 1)

            steps(pe, NU, 1, 2, step_c)

            pe.wait_ge(s_ccmb, NU)

            def step_d(b, s, there):
                n = (s + 3) % TURN
                if there(b + 3):
                    wait(pe, s_din[n], landed(b + 3, n, GROUP))
                    wait(pe, s_do, b)
                    for k in range(GROUP):
                        last = mm(PS[:, n, 0:OR], ident[:, :], d_p[:, n, k, :], start=(k == 0), stop=(k == GROUP - 1))
                    last.then_inc(s_dsum, 1)

            steps(pe, NB, 3, 0, step_d)

        @block.vector
        def _(dve):
            v = nc.vector
            for tile in (att, w1m, wscm):
                v.memset(tile[:, :, :], 0.0)
            for tile in (zeros, fc2, two):
                v.memset(tile[:, :], 0.0)
            v.memset(ones[:, :], 1.0)
            v.memset(fc1[:, :], 0.0).then_inc(s_zeroed, 1)
            dve.wait_ge(s_iota, 1)
            v.tensor_scalar(ident[:, :], iota_n[:, :], part_no[:, 0:1], None, ALU.is_equal)
            v.tensor_scalar(upper[:, :], iota_n[:, :], part_no[:, 0:1], None, ALU.is_gt)
            v.tensor_scalar(lower_eq[:, :], iota_n[:, :], part_no[:, 0:1], None, ALU.is_le).then_inc(s_const, 1)

            tab = [0]

            def link(ins):
                tab[0] += 1
                ins.then_inc(s_tab, 1)
                dve.wait_ge(s_tab, tab[0])

            dve.wait_ge(s_ends, 16)
            link(v.tensor_copy(ends, ends.bitcast(I32)))
            for col, which, bound in ((0, 1, 0), (1, 0, 1), (2, 1, 1)):
                link(v.tensor_scalar(stepm[:, 0:EW], ends[:, which, :], bounds[0:NB, bound:bound + 1], None,
                                     ALU.is_lt, ALU.add, accum_out=cnt[0:NB, col:col + 1]))
            link(v.tensor_scalar(cnt[0:NB, 3:4], cnt[0:NB, 1:2], cnt[0:NB, 0:1], 0.0, ALU.subtract, ALU.max))
            dve.wait_ge(s_tabp, 1)
            link(v.tensor_tensor(cnt[0:NB, 4:5], PS[0:NB, 7, 64:65], cnt[0:NB, 3:4], ALU.add))
            link(v.tensor_tensor(cnt[0:NB, 5:6], cnt[0:NB, 2:3], cnt[0:NB, 0:1], ALU.subtract))
            v.memset(two[:, 0:1], 1.0)
            v.tensor_tensor(two[0:NB, 32:33], cnt[0:NB, 5:6], cnt[0:NB, 3:4], ALU.subtract)
            link(v.tensor_scalar(stepm, iota_t[0:NB, :], cnt[0:NB, 4:5], None, ALU.is_ge))
            dve.wait_ge(s_tabp, 2)
            flat = PS[:, 0:4, :].rearrange("p b n -> p (b n)")[:, 0:T]
            v.tensor_scalar(block_row, flat[0:1, :], float(NB - 1), None, ALU.min)
            link(v.tensor_tensor(iota_t[32:33, :], flat[32:33, :], iota_t[32:33, :], ALU.add))
            v.tensor_scalar(window_row, iota_t[32:33, :], float(EW - 1), None, ALU.min)
            cols = PS[:, 7, 128:128 + 2 * NC].rearrange("p (c j) -> p c j", j=2)
            v.tensor_scalar(b128[:, :], cols[:, :, 0], float(P), None, ALU.mult)
            link(v.tensor_tensor(tile_col[:, :], cols[:, :, 1], tile_col[:, :], ALU.add))
            v.tensor_scalar(wcol[:, :], tile_col[:, :], float(EW - 1), None, ALU.min).then_inc(s_win, 1)

            dve.wait_ge(s_w, 16 * N_W)
            for tile in (w1m, wscm):
                v.tensor_scalar(tile[:, :, :], tile[:, :, :], S64, None, ALU.mult)
            v.tensor_scalar(fc3[:, :], fc3[:, :], S64 / 2, None, ALU.mult)
            v.tensor_scalar(fc2[:, :], fc2[:, :], S64 / 2, None, ALU.mult)
            v.tensor_scalar(fc1[:, :], fc1[:, :], S8, None, ALU.mult)
            v.tensor_scalar(w2m[MUL:P, 0, :], w2m[MUL:P, 0, :], INV_SQRT3, None, ALU.mult).then_inc(s_scaled, 1)

            dve.wait_ge(s_sdin, 16 * NC)
            v.tensor_copy(sd_f[:, :, 0, :], sd_in[:, :, 0, :])
            v.tensor_tensor(sd_f[:, :, 1, :], sd_in[:, :, 1, :],
                            b128[:, :].rearrange("p (c o) -> p c o", o=1).to_broadcast([P, NC, P]),
                            ALU.subtract).then_inc(s_sdf, 1)

            dve.wait_ge(s_hev, 2 * NB)
            v.tensor_reduce(amax[:, :], logits[:, :, 0:H].rearrange("p b h -> p h b"), AX.X, ALU.max).then_inc(s_amax, 1)
            lg = [0]

            def link_lg(ins):
                lg[0] += 1
                ins.then_inc(s_lg, 1)
                dve.wait_ge(s_lg, lg[0])

            def leaky(to, z):
                return v.scalar_tensor_tensor(to, z, SLOPE, z, ALU.mult, ALU.max)

            dve.wait_ge(s_gmax, 1)
            link_lg(v.tensor_tensor(lt[:, :, H:], logits[:, :, H:2 * H],
                                    gmax[:, :].rearrange("p (o h) -> p o h", o=1).to_broadcast([P, NB, H]), ALU.add))
            link_lg(leaky(logits[:, :, 2 * H:], lt[:, :, H:]))
            link_lg(v.tensor_copy(ac3[:, :, 0, :], logits[:, :, H:]))
            link_lg(v.tensor_tensor(lt[:, :, :], logits[:, :, H:], ac3[:, :, 0, :], ALU.subtract))
            link_lg(v.tensor_copy(ac3[:, :, 1, :], lt[:, :, :]))
            link_lg(v.tensor_tensor(ac3[:, :, 2, :], lt[:, :, :], ac3[:, :, 1, :], ALU.subtract))
            link_lg(v.tensor_tensor(lt[:, :, 0:H], logits[:, :, 0:H], logits[:, :, H:2 * H], ALU.add))
            link_lg(leaky(lt[:, :, 0:H], lt[:, :, 0:H]))
            link_lg(v.tensor_tensor(lt[:, :, 0:H], lt[:, :, 0:H], logits[:, :, 2 * H:], ALU.subtract))
            assert lg[0] == LG_SELF

            for c in range(NC):
                dve.wait_ge(s_sdp, c + 1)
                v.tensor_scalar(dloc[:, c * P:(c + 1) * P], PS[:, 2 + c % 2, 0:P], -1.0, float(P), ALU.max,
                                ALU.min).then_inc(s_dl, 1)
            dve.wait_ge(s_dl, NC)
            v.tensor_scalar(valid[:, :], dloc[:, :], 0.0, None, ALU.is_ge).then_inc(s_dl, 1)
            dve.wait_ge(s_dl, NC + 1)
            v.scalar_tensor_tensor(valid[:, :], dloc[:, :], float(P), valid[:, :], ALU.is_lt, ALU.mult).then_inc(s_dl, 1)
            dve.wait_ge(s_win, 1)
            v.memset(acc[:, :, :], 0.0).then_inc(s_acc0, 1)

            dve.wait_ge(s_acc0, 1)

            def step_a(g, s, there):
                n, m, o = (s + 2) % TURN, (s - 1) % TURN, (s - 2) % TURN

                def half_silu(to, t, z):
                    return v.scalar_tensor_tensor(to, t, 1.0, z, ALU.add, ALU.mult)

                def message(k):
                    x = hg[:, m, k, 0:D].rearrange("p (h c) -> p h c", h=H)
                    v.tensor_tensor(x, x, hg[:, m, k, D:HW].rearrange("p (h o) -> p h o", o=1).to_broadcast([P, H, C]),
                                    ALU.mult).then_inc(s_msg, 1)

                def add_up(k):
                    t = GROUP * (g - 1) + k
                    wait(dve, s_agg, t + 1)
                    wait(dve, s_acc, t)
                    x = acc[:, ds(b[k], 1), :].rearrange("p o d -> p (o d)")
                    v.tensor_tensor(x, x, PS[:, 2 + k % 2, 0:HW], ALU.add).then_inc(s_acc, 1)

                if there(g - 1):
                    wait(dve, s_p, g)
                    message(0)
                    message(1)
                if there(g):
                    wait(dve, s_t1, g + 1)
                    wait(dve, s_f2, g - 1)
                    half_silu(h1[:, s % 2, :], t1[:, s % 2, :], PS[:, 6, 0:2 * P]).then_inc(s_h1, 1)
                if there(g - 2):
                    wait(dve, s_t2, g - 1)
                    wait(dve, s_f3, 2 * (g - 3))
                    half_silu(h2[:, o % 2, :], t2[:, o % 2, :], PS[:, 7, 0:2 * P]).then_inc(s_h2, 1)
                if there(g - 1):
                    message(2)
                    message(3)
                    b = numbers(dve, block_row, (g - 1) * GROUP, GROUP, NB)
                if there(g):
                    wait(dve, s_ad, g + 1)
                    v.tensor_reduce(ad[:, s % 2, :, :],
                                    PS[:, 1, 0:GROUP * 6 * H].rearrange("p (k i j) -> p k j i", k=GROUP, i=3),
                                    AX.X, ALU.add).then_inc(s_z, 1)
                if there(g):
                    wait(dve, s_hg[s], landed(g, s, GROUP))
                    wait(dve, s_z, 4 * g + 1)
                    v.tensor_tensor(za[:, s % 2, :, :], hg[:, s, :, D:HW], ad[:, s % 2, :, 0:H], ALU.add).then_inc(s_z, 1)
                if there(g - 1):
                    add_up(0)
                if there(g):
                    wait(dve, s_z, 4 * g + 2)
                    leaky(zb[:, s % 2, :, :], za[:, s % 2, :, :]).then_inc(s_z, 1)
                if there(g - 1):
                    add_up(1)
                if there(g):
                    wait(dve, s_z, 4 * g + 3)
                    v.tensor_tensor(za[:, s % 2, :, :], zb[:, s % 2, :, :], ad[:, s % 2, :, H:], ALU.subtract
                                    ).then_inc(s_z, 1)
                if there(g + 2):
                    wait(dve, s_agg, GROUP * (g - 1))
                    v.tensor_tensor(oh[:, n, :, :],
                                    iota_n[:, :].rearrange("p (o n) -> p o n", o=1).to_broadcast([P, GROUP, P]),
                                    dloc[:, ds((g + 2) * GROUP, GROUP)].rearrange("p (k o) -> p k o", o=1
                                                                                  ).to_broadcast([P, GROUP, P]),
                                    ALU.is_equal).then_inc(s_oh, 1)
                if there(g - 1):
                    add_up(2)
                    add_up(3)

            steps(dve, NG, 2, 2, step_a)

            dve.wait_ge(s_acc, T)
            dve.wait_ge(s_self, 1)
            v.tensor_tensor(rden[:, :, :], acc[:, :, D:HW], pself[:, :, :], ALU.add).then_inc(s_rden, 1)
            dve.wait_ge(s_rden, 1)
            v.reciprocal(rden[:, :, :], rden[:, :, :]).then_inc(s_rden, 1)
            dve.wait_ge(s_rden, 2)

            def layer_norm_stats(z, s, b, done):
                v.bn_stats(stat[:, s, :], z).then_inc(done, 1)
                wait_apart(dve, done, 3 * b + 1)
                v.bn_aggr(mv[:, s, 0:2], stat[:, s, :]).then_inc(done, 1)
                wait(dve, done, 3 * b + 2)
                v.tensor_scalar(mv[:, s, 2:3], mv[:, s, 1:2], EPS, None, ALU.add).then_inc(done, 1)

            def normalized(to, of, s):
                return v.tensor_scalar(to, of, mv[:, s, 0:1], mv[:, s, 3:4], ALU.subtract, ALU.mult)

            def step_b(b, s, there):
                n, m = (s + 1) % TURN, (s - 1) % TURN
                if there(b - 1):
                    wait(dve, s_brstd, b)
                    wait(dve, s_bst[m], landed(b - 5, m) if there(b - 5) else 0)
                    normalized(b_x1[:, m, 0:MUL], b_v[:, m, 0:MUL], m).then_inc(s_bx1, 1)
                    normalized(b_x1[:, m, MUL:D].rearrange("p (d u) -> p d u", d=3),
                               b_v[:, m, MUL:D].rearrange("p (u d) -> p d u", d=3), m).then_inc(s_bx1, 1)
                if there(b):
                    wait(dve, s_be, b + 1)
                    v.scalar_tensor_tensor(b_v[:, s, :], b_v[:, s, :], 0.0, b_e[:, s, :], ALU.max, ALU.add
                                           ).then_inc(s_belu, 1)
                    wait(dve, s_belu, b + 1)
                    v.scalar_tensor_tensor(b_v[:, s, :], b_v[:, s, :], -1.0, b_x[:, s, :], ALU.add, ALU.add
                                           ).then_inc(s_bs, 1)
                    wait(dve, s_bs, b + 1)
                    layer_norm_stats(b_v[:, s, :], s, b, s_bmv)
                if there(b + 1):
                    hs = b_h[:, n, :]
                    hs4 = hs.rearrange("p (h c) -> p h c", h=H)
                    wait_apart(dve, s_bt, b + 2)
                    v.tensor_tensor(hs, hs, acc[:, ds(b + 1, 1), 0:D].rearrange("p o d -> p (o d)"), ALU.add
                                    ).then_inc(s_bsum, 1)
                    wait_apart(dve, s_bsum, 2 * b + 3)
                    v.tensor_tensor(hs4, hs4, rden[:, ds(b + 1, 1), :].rearrange("p o (h c) -> p (o h) c", c=1
                                                                                 ).to_broadcast([P, H, C]),
                                    ALU.mult).then_inc(s_bsum, 1)
                    wait(dve, s_bsum, 2 * b + 4)
                    wait(dve, s_bskip, b + 2)
                    v.tensor_tensor(b_v[:, n, :], hs, PS[:, n % 2, 0:D], ALU.add).then_inc(s_bv, 1)
                    wait(dve, s_bv, b + 2)
                    v.tensor_scalar(b_e[:, n, :], b_v[:, n, :], 0.0, None, ALU.min).then_inc(s_bm, 1)

            steps(dve, NB, 1, 1, step_b)

            def step_c(u, s, there):
                m = (s - 1) % TURN
                if there(u):
                    wait(dve, s_csr, u + 1)
                    wait(dve, s_co, u - 3)
                    for k in range(PAIR):
                        v.scalar_tensor_tensor(same[:, s, k, :], PS[:, 2 + s % 2, k * P:(k + 1) * P],
                                               c_src[:, s, k:k + 1], lower_eq[:, :], ALU.is_equal, ALU.mult,
                                               accum_out=c_cnt[:, s, k:k + 1]).then_inc(s_csame, 1)
                    y = PS[:, s % 2, :].rearrange("p (k d u) -> p k d u", k=PAIR, d=4)
                    w = wt[:, s, :, 0:D].rearrange("p k (a b u) -> p k a b u", a=2, b=2)
                    sh1 = wt[:, s, :, D + 1:D + 4].rearrange("p k (d o) -> p k d o", o=1).to_broadcast([P, PAIR, 3, MUL])
                    q = mid[:, s % 2, :, 1, :]
                    wait(dve, s_cy, u + 1)
                    wait(dve, s_cw[s], landed(u, s, PAIR))
                    wait(dve, s_cmt, PAIR * (u - 1))

                    def spread(z):
                        return z.rearrange("p k (o u) -> p k o u", o=1).to_broadcast([P, PAIR, 3, MUL])

                    v.tensor_tensor(evs[:, :, :, :], y[:, :, 1:4, :], sh1, ALU.mult).then_inc(s_cpr, 1)
                    v.tensor_tensor(mid[:, s % 2, :, 0:2, :], w[:, :, :, 0, :],
                                    y[:, :, 0:1, :].to_broadcast([P, PAIR, 2, MUL]), ALU.mult).then_inc(s_cpr, 1)
                if there(u - 1):
                    v.tensor_scalar(c_d[:, m, :], c_src[:, m, :], -1.0, trash[:, 0:1], ALU.mult, ALU.add
                                    ).then_inc(s_cix, 1)
                if there(u):
                    wait(dve, s_cpr, 5 * u + 1)
                    v.tensor_tensor(evt[:, :, :], evs[:, :, 0, :], evs[:, :, 1, :], ALU.add).then_inc(s_cpr, 1)
                    wait(dve, s_cpr, 5 * u + 2)
                    v.tensor_tensor(mid[:, s % 2, :, 2:8:2, :], spread(q), sh1, ALU.mult).then_inc(s_cpr, 1)
                    v.tensor_tensor(mid[:, s % 2, :, 3:8:2, :], y[:, :, 1:4, :], spread(w[:, :, 0, 1, :]), ALU.mult)
                    wait(dve, s_cpr, 5 * u + 3)
                    v.tensor_tensor(evt[:, :, :], evt[:, :, :], evs[:, :, 2, :], ALU.add).then_inc(s_cpr, 1)
                if there(u - 1):
                    wait(dve, s_cix, 3 * u - 2)
                    wait(dve, s_csame, PAIR * u)
                    v.scalar_tensor_tensor(c_d[:, m, :], c_cnt[:, m, :], 1.5, c_d[:, m, :], ALU.is_gt, ALU.mult
                                           ).then_inc(s_cix, 1)
                if there(u):
                    wait(dve, s_cpr, 5 * u + 5)
                    v.tensor_tensor(q, evt[:, :, :], w[:, :, 1, 1, :], ALU.mult).then_inc(s_cmid, 1)
                if there(u - 1):
                    wait(dve, s_cix, 3 * u - 1)
                    for k in range(PAIR):
                        wait(dve, s_add[m % 2 * PAIR + k], 8 * (u - 5) + 16 - 8 * (m % 2) if there(u - 5) else 0)
                    v.tensor_tensor(c_idx[:, m, :], c_d[:, m, :], c_src[:, m, :], ALU.add).then_inc(s_cix, 1)

            steps(dve, NU, 0, 1, step_c)

            def step_d(b, s, there):
                n2, n, m = (s + 2) % TURN, (s + 1) % TURN, (s - 1) % TURN
                if there(b - 2):
                    wait(dve, s_drstd, b - 1)
                    wait(dve, s_dst[n2], landed(b - 6, n2) if there(b - 6) else 0)
                    normalized(d_out[:, n2, 0:MUL], d_z[:, n2, 0:MUL], n2).then_inc(s_dout, 1)
                    normalized(d_out[:, n2, MUL:D].rearrange("p (u d) -> p d u", d=3),
                               d_z[:, n2, MUL:D].rearrange("p (d u) -> p d u", d=3), n2).then_inc(s_dout, 1)
                if there(b - 1):
                    wait(dve, s_drs, b)
                    v.scalar_tensor_tensor(d_z[:, m, 0:MUL], d_o[:, m, 0:MUL], d_n[:, m, 4:5], gfull[:, 0:MUL],
                                           ALU.mult, ALU.mult).then_inc(s_dn, 1)
                    v.scalar_tensor_tensor(d_z[:, m, MUL:D], d_o[:, m, MUL:D], d_n[:, m, 5:6], gfull[:, MUL:D],
                                           ALU.mult, ALU.mult).then_inc(s_dn, 1)
                if there(b + 1):
                    wait(dve, s_ddn, b + 2)
                    wait(dve, s_dx[n], landed(b + 1, n))
                    v.scalar_tensor_tensor(d_o[:, n, :], PS[:, n, 0:D], d_n[:, n, 1:2], d_x[:, n, D:], ALU.mult,
                                           ALU.add).then_inc(s_do, 1)
                if there(b - 1):
                    wait(dve, s_dn, 2 * b)
                    v.tensor_tensor(d_z[:, m, :], d_z[:, m, :], d_x[:, m, 0:D], ALU.add).then_inc(s_dz, 1)
                    wait(dve, s_dz, b)
                    layer_norm_stats(d_z[:, m, :], m, b - 1, s_dmv)
                if there(b):
                    wait(dve, s_dsq, b + 1)
                    v.tensor_scalar(d_n[:, s, 2:3], d_n[:, s, 6:7], 1.0 / MUL, EPS, ALU.mult, ALU.add).then_inc(s_dms, 1)
                    v.tensor_scalar(d_n[:, s, 3:4], d_n[:, s, 7:8], 1.0 / (3 * MUL), EPS, ALU.mult, ALU.add
                                    ).then_inc(s_dms, 1)
                if there(b + 2):
                    wait(dve, s_dsum, b + 3)
                    v.tensor_scalar(d_n[:, n2, 0:1], PS[:, n2, D:D + 1], 1.0, float(2 * MUL), ALU.max, ALU.mult
                                    ).then_inc(s_ddeg, 1)

            steps(dve, NB, 2, 2, step_d)


_WEIGHTS = ["bias", "skip_W", "w1_s", "w1_v", "wsc_s", "wsc_v", "w2_s", "w2_v", "fc_w1", "fc_w2", "fc_w3", "g_s", "g_v"]


def kernel(**inputs):
    import concourse.bacc as bacc
    from concourse.bass_utils import run_bass_kernel_spmd

    a = {k: np.asarray(v) for k, v in inputs.items()}
    x, src, dst = a["x"], a["src"], a["dst"]
    n, e = x.shape[0], src.shape[0]
    nb, np_, ew, t = sizes(n, e)
    w = {k: a.get("L0_gnn_" + k, a.get("L1_gnn_" + k)) for k in _WEIGHTS}
    xp = np.zeros((np_, x.shape[1]), x.dtype)
    xp[:n] = x
    sd = np.zeros((2, ew * P), src.dtype)
    sd[1] = NO_NODE
    sd[0, :e], sd[1, :e] = src, dst
    sd = sd.reshape(2, ew, P)
    ea8 = np.zeros((t * P, a["edge_attr_8"].shape[1]), x.dtype)
    ea8[:e] = a["edge_attr_8"]
    ea4 = np.zeros((t * P, 4), x.dtype)
    ea4[:e] = a["edge_attr_4"]
    arrays = {
        "x": xp,
        "xT": np.ascontiguousarray(xp.T),
        "edges_sd": np.ascontiguousarray(sd.transpose(1, 0, 2)).reshape(ew, 2 * P),
        "window_ends": np.ascontiguousarray(sd[1][:, [0, P - 1]].T),
        "ea8": np.ascontiguousarray(ea8.reshape(t // 4, 2, 2 * P, -1).transpose(0, 1, 3, 2)).reshape(t // 4, -1, 2 * P),
        "ea4": np.ascontiguousarray(ea4.reshape(t, P, 4).transpose(1, 0, 2)),
        "W": a["L0_gnn_W"],
        "WT": np.ascontiguousarray(a["L0_gnn_W"].T),
        "att_src": a["L0_gnn_att_src"],
        "att_dst": a["L0_gnn_att_dst"],
        **w,
    }
    nc = bacc.Bacc("TRN2", target_bir_lowering=False, num_devices=1)
    aps = {k: nc.dram_tensor(f"in_{k}", v.shape, mybir.dt.from_np(v.dtype), kind="ExternalInput").ap()
           for k, v in arrays.items()}
    out = nc.dram_tensor("out", [np_, x.shape[1]], F32, kind="ExternalOutput").ap()
    bass_gat_equivariant_kernel(nc, out=out, n_nodes=n, n_edges=e, **aps)
    r = run_bass_kernel_spmd(nc, [{f"in_{k}": v for k, v in arrays.items()}], core_ids=[0])
    return r.results[0]["out"][:n]
```

```python
from contextlib import ExitStack

import numpy as np
import concourse.bass as bass
from concourse import mybir

F32 = mybir.dt.float32
BF16 = mybir.dt.bfloat16
I32 = mybir.dt.int32
ALU = mybir.AluOpType
ACT = mybir.ActivationFunctionType
AX = mybir.AxisListType
RMAX = bass.bass_isa.ReduceOp.max
ds = bass.ds

P = 128
NO_NODE = 1 << 20
GROUP = 4
PAIR = 2
CHUNK = 7
TURN = 4


def sizes(n_nodes, n_edges):
    nb = -(-n_nodes // (P * 2 * CHUNK)) * 2 * CHUNK
    ew = -(-n_edges // P)
    t = -(-(ew + nb - 1) // P) * P
    return nb, nb * P, ew, t


def wait(eng, s, value):
    if not (isinstance(value, int) and value <= 0):
        eng.wait_ge(s, value)


def wait_apart(eng, s, value):
    if not (isinstance(value, int) and value <= 0):
        eng.wait_ge(s, value)
        eng.nop(nofuse=True)


def landed(g, slot, dmas=1):
    return dmas * (16 // TURN * g + 16 - 16 // TURN * slot)


def steps(eng, n, lead, tail, step):
    first, last = 2 * TURN, (n - lead) // TURN * TURN
    for g in range(-lead, first):
        step(g, g % TURN, lambda v: 0 <= v < n)
    with eng.Fori(first // TURN, last // TURN) as i:
        for slot in range(TURN):
            step(i * TURN + slot, slot, lambda v: True)
    for g in range(last, n + tail):
        step(g, g % TURN, lambda v: 0 <= v < n)


def bass_gat_equivariant_kernel(nc, x, xT, edges_sd, window_ends, ea8, ea4, W, WT, att_src, att_dst, bias, skip_W,
                                w1_s, w1_v, wsc_s, wsc_v, w2_s, w2_v, fc_w1, fc_w2, fc_w3, g_s, g_v, out,
                                n_nodes, n_edges):
    NB, NP, EW, T = sizes(n_nodes, n_edges)
    D = x.shape[1]
    H, C = att_src.shape
    MUL = w1_s.shape[0]
    NBAS = fc_w1.shape[0]
    HW = D + H
    WR = D + 4
    OR = D + 1
    NG, NU, NC = T // GROUP, T // PAIR, T // P
    NQ = -(-NC // 4)
    SLOPE, EPS = 0.2, 1e-5
    S8, S64 = float(1 / np.sqrt(float(NBAS))), float(1 / np.sqrt(float(MUL)))
    INV_SQRT3 = 0.5773502691896258
    assert NP <= 1 << 16 and D == 256 and H * C == D and MUL == C == 64 and NBAS == 8 and NB <= P and D == 4 * MUL

    def dram(name, shape, dt):
        return nc.dram_tensor(name, shape, dt).ap()

    h_tab = dram("h_tab", [NP, HW], F32)
    w_tab = dram("w_tab", [T * P, WR], F32)
    ot_tab = dram("ot_tab", [NU // 2, P, PAIR * P], BF16)
    y_tab = dram("y_tab", [NP + 32, D], F32)
    src_tab = dram("src_tab", [T, 2, P], BF16)
    x1_tab = dram("x1_tab", [NP, 2 * D], F32)
    ZERO = -(-(NP + P) // (NG * 32))
    part = [dram(f"part{k}", [NG * 32 * ZERO, OR], F32) for k in range(GROUP)]

    with ExitStack() as ctx:
        def sb(name, shape, dt=F32):
            return ctx.enter_context(nc.sbuf_tensor(name, shape, dt))

        def sem(name):
            return ctx.enter_context(nc.semaphore(name))

        def sems(prefix, names):
            return [sem(f"{prefix}_{n}") for n in names.split()]

        PS = ctx.enter_context(nc.psum_tensor("PS", [P, 8, 512], F32))

        ident = sb("ident", [P, P])
        ident_b = sb("ident_b", [P, P], BF16)
        iota_n = sb("iota_n", [P, P])
        upper = sb("upper", [P, P])
        lower_eq = sb("lower_eq", [P, P])
        ones = sb("ones", [P, P])
        ones_b = sb("ones_b", [2, P], BF16)
        zeros = sb("zeros", [32, ZERO * OR])
        part_no = sb("part_no", [P, 1])
        trash = sb("trash", [P, 1])
        half = sb("half", [P, 2])
        Wx = sb("Wx", [P, 2, D + 2 * H])
        WTs = sb("WTs", [P, 2, D])
        att = sb("att", [P, 2, 2 * H])
        skw = sb("skw", [P, 2, D])
        brow = sb("brow", [1, D])
        wm = sb("wm", [P, 2, 2, P])
        w2m = sb("w2m", [P, 2, MUL])
        fc1 = sb("fc1", [2 * NBAS, P])
        fc2 = sb("fc2", [P, P])
        fc3 = sb("fc3", [P, D])
        gfull = sb("gfull", [P, D])

        logits = sb("logits", [P, NB, 3 * H])
        lt = sb("lt", [P, NB, 2 * H])
        ac3 = sb("ac3", [P, NB, 3, 2 * H], BF16)
        pself = sb("pself", [P, NB, H])
        rden = sb("rden", [P, NB, H])
        amax = sb("amax", [P, 2 * H])
        gmax = sb("gmax", [P, 2 * H])
        spread = sb("spread", [1, 2])
        wide = sb("wide", [1, 1], I32)
        srcF = sb("srcF", [P, T])
        dloc = sb("dloc", [P, T], BF16)
        valid = sb("valid", [P, T], BF16)
        y_row = sb("y_row", [P, T // 2])
        rows = sb("rows", [33, T], I32)
        block_row, window_row = rows[0:1, :], rows[32:33, :]

        BIG = max(NB * HW, 2 * EW + 2 * T + 4 * NC * P)
        big = sb("big", [P, BIG])
        acc = big[:, 0:NB * HW].rearrange("p (b d) -> p b d", d=HW)
        ARENA = 11400
        arena = sb("arena", [P, ARENA])
        used = [0]

        def cut(n, new_stage=False):
            at = 0 if new_stage else used[0]
            used[0] = at + n
            assert used[0] <= ARENA
            return arena[:, at:at + n]

        TABLES = 2 * EW + 2 * T + 4 * NC * P
        ends = big[0:NB, 0:2 * EW].rearrange("p (s w) -> p s w", s=2)
        iota_t = big[:, 2 * EW:2 * EW + T]
        stepm = big[0:NB, 2 * EW + T:2 * EW + 2 * T]
        at = 2 * EW + 2 * T
        sd_in = big[:, at:at + 2 * NC * P].bitcast(I32).rearrange("p (c w e) -> p c w e", c=NC, w=2)
        sd_f = big[:, at + 2 * NC * P:at + 4 * NC * P].rearrange("p (c w e) -> p c w e", c=NC, w=2)
        sd_parts = big[:, at:at + NC * P].bitcast(BF16).rearrange("p (c w e) -> p c w e", c=NC, w=2)
        x_in = cut(4 * CHUNK * P, True).rearrange("p (s k n) -> p s k n", s=2, k=2)
        sd_dst = big[:, at + NC * P:at + 2 * NC * P].rearrange("p (c e) -> p c e", c=NC)
        sd_row = cut(4 * CHUNK * P + NC * P, True)[:, 4 * CHUNK * P:].rearrange("p (c e) -> p c e", c=NC)
        h_out = cut(2 * CHUNK * HW).rearrange("p (s k d) -> p s k d", s=2, k=CHUNK)
        bounds = sb("bounds", [P, 2])
        cnt = sb("cnt", [P, 8])
        two = sb("two", [P, 33])
        b128 = sb("b128", [P, NC])
        tile_col = sb("tile_col", [P, NC])
        wcol = sb("wcol", [P, NC], I32)

        hg = cut(TURN * GROUP * HW, True).rearrange("p (s k d) -> p s k d", s=TURN, k=GROUP)
        oh = cut(TURN * GROUP * P).rearrange("p (s k n) -> p s k n", s=TURN, k=GROUP)
        ots = cut(GROUP * P).bitcast(BF16).rearrange("p (s k e) -> p s k e", s=2, k=GROUP)
        wst = cut(2 * GROUP * WR).rearrange("p (s k d) -> p s k d", s=2, k=GROUP)
        eat, t1, t2, h1, h2 = (cut(2 * 2 * P).rearrange("p (s e) -> p s e", s=2) for _ in range(5))
        otp = PS[:, 0, 0:GROUP * P // 2].bitcast(BF16).rearrange("p (k e) -> p k e", k=GROUP)
        sidx = sb("sidx", [P, TURN, GROUP], I32)
        za = sb("za", [P, 2, GROUP, H])
        ad = sb("ad", [P, 2, GROUP, 2 * H])
        zb = sb("zb", [P, 2, GROUP, H])
        sh = sb("sh", [P, TURN, GROUP, 4])

        b_h = cut(TURN * D, True).rearrange("p (s d) -> p s d", s=TURN)
        b_x = cut(TURN * D).rearrange("p (s d) -> p s d", s=TURN)
        b_xT = cut(TURN * 2 * P).rearrange("p (s k n) -> p s k n", s=TURN, k=2)
        b_v = cut(TURN * D).rearrange("p (s d) -> p s d", s=TURN)
        b_e = cut(TURN * D).rearrange("p (s d) -> p s d", s=TURN)
        b_x1 = cut(TURN * 2 * D).rearrange("p (s d) -> p s d", s=TURN)
        b_x1T = cut(2 * 2 * P).rearrange("p (s k n) -> p s k n", s=2, k=2)
        stat = sb("stat", [P, TURN, 6])
        mv = sb("mv", [P, TURN, 4])

        wt = cut(TURN * PAIR * WR, True).rearrange("p (s k d) -> p s k d", s=TURN, k=PAIR)
        c_ot = cut(2 * PAIR * P // 2).bitcast(BF16).rearrange("p (s k e) -> p s k e", s=2, k=PAIR)
        c_otf = cut(2 * PAIR * P).rearrange("p (s k e) -> p s k e", s=2, k=PAIR)
        mid = cut(2 * PAIR * 2 * D).rearrange("p (s k c u) -> p s k c u", s=2, k=PAIR, c=8)
        midT = cut(2 * PAIR * 4 * P).rearrange("p (s k c e) -> p s k c e", s=2, k=PAIR, c=4)
        oT_sb = cut(4 * P).rearrange("p (j e) -> p j e", j=4)
        o_sb = cut(2 * PAIR * OR).rearrange("p (s k d) -> p s k d", s=2, k=PAIR)
        same = cut(TURN * PAIR * P).rearrange("p (s k e) -> p s k e", s=TURN, k=PAIR)
        o_cmb = cut(GROUP * OR).rearrange("p (k d) -> p k d", k=GROUP)
        evs = cut(PAIR * 3 * MUL).rearrange("p (k d u) -> p k d u", k=PAIR, d=3)
        evt = cut(PAIR * MUL).rearrange("p (k u) -> p k u", k=PAIR)
        c_row = sb("c_row", [P, 2, PAIR], I32)
        c_src = sb("c_src", [P, TURN, PAIR])
        c_parts = sb("c_parts", [2, TURN, PAIR * P], BF16)
        c_cnt = sb("c_cnt", [P, TURN, PAIR])
        c_d = sb("c_d", [P, TURN, PAIR])
        c_idx = sb("c_idx", [P, TURN, PAIR], I32)

        d_p = cut(TURN * GROUP * OR, True).rearrange("p (s k d) -> p s k d", s=TURN, k=GROUP)
        d_x = cut(TURN * 2 * D).rearrange("p (s d) -> p s d", s=TURN)
        d_o = cut(TURN * D).rearrange("p (s d) -> p s d", s=TURN)
        d_q = cut(TURN * D).rearrange("p (s d) -> p s d", s=TURN)
        d_z = cut(TURN * D).rearrange("p (s d) -> p s d", s=TURN)
        d_out = sb("d_out", [P, TURN, D])
        d_n = sb("d_n", [P, TURN, 8])

        c_y = d_out[:, :, :].rearrange("p (s k) d -> p s k d", s=2)

        m_buf = d_out[:, :, :].rearrange("p s d -> p (s d)")
        m_row = m_buf[:, 0:HW]
        m_val = m_buf[:, HW:HW + H * P].rearrange("p (h e) -> p h e", h=H)
        m_out = m_buf[:, HW + H * P:HW + (H + 1) * P]
        m_idx = sb("m_idx", [P, 1], I32)
        m_dst = sb("m_dst", [P, 1])
        m_red = sb("m_red", [P, H])

        (s_iota, s_zeroed, s_const, s_watt_in, s_w, s_scaled, s_ends, s_tab, s_tabp, s_win, s_watt, s_hwatt) = sems(
            "s", "iota zeroed const watt_in w scaled ends tab tabp win watt hwatt")
        s_flag, s_mcol, s_mrow, s_mps, s_mc, s_mdone = sems("m", "flag col row ps c done")
        s_xin = sems("s_xin", "0 1")
        s_zero = sem("s_zero")
        s_hst = sems("s_hst", "0 1")
        s_hps, s_hev, s_sdin, s_sdf, s_sdst, s_sdp, s_sdT, s_amax, s_gmax, s_lg, s_self, s_acc0, s_dl = sems(
            "s", "hps hev sdin sdf sdst sdp sdT amax gmax lg self acc0 dl")
        (s_idx, s_oh, s_otp, s_ots, s_ad, s_z, s_p, s_msg, s_agg, s_acc, s_f1, s_t1, s_h1, s_f2, s_t2, s_h2, s_f3,
         s_wev) = sems("a", "idx oh otp ots ad z p msg agg acc f1 t1 h1 f2 t2 h2 f3 wev")
        slots = "0 1 2 3"
        s_hg, s_otst, s_ea, s_sh, s_wst = (sems(f"a_{n}", slots) for n in ("hg", "otst", "ea", "sh", "wst"))
        (s_rden, s_bt, s_bsum, s_bskip, s_bv, s_bm, s_be, s_belu, s_bs, s_bmv, s_brstd, s_bx1, s_bxp, s_bxT, s_by,
         s_bout) = sems("b", "rden t sum skip v m e elu s mv rstd x1 xp xT y out")
        s_bin, s_bst = sems("b_in", slots), sems("b_st", slots)
        (s_csl, s_cotf, s_cy, s_csr, s_csame, s_cix, s_cpr, s_cmid, s_cmt, s_cmT, s_coT, s_coTsb, s_co, s_cosb, s_cc,
         s_ccmb, s_crow) = sems("c", "sl otf y sr same ix pr mid mt mT oT oTsb o osb c cmb row")
        s_cyg = sems("c_yg", "0 1")
        s_cw, s_cin, s_add = (sems(f"c_{n}", slots) for n in ("w", "in", "add"))
        (s_dsum, s_ddeg, s_ddn, s_do, s_dsq, s_dms, s_drs, s_dn, s_dz, s_dmv, s_drstd, s_dout) = sems(
            "d", "sum deg dn o sq ms rs n z mv rstd out")
        s_din, s_dx, s_dst = sems("d_in", slots), sems("d_x", slots), sems("d_st", slots)

        block = ctx.enter_context(nc.Block())
        TAB_WINDOWS, TAB_STEPS = 5, 8
        T_BANK = (3, 1)
        SD_PARTS = 7
        LG_PARTS, LG_SELF = 10, 13
        HUGE, RANGE = 1e30, 60.0
        N_W_ATT = 2 + 2 * H
        N_W = 2 + 8 + 2 + 2 * 6 + 4 + 1
        NCH = NB // CHUNK
        xv = xT.rearrange("(k p) n -> p k n", p=P)
        x1b = x1_tab.rearrange("(b p) d -> b p d", p=P)

        def one(v, i):
            return v[ds(i, 1)].rearrange("o p d -> (o p) d")

        def when_wide(eng):
            eng.wait_ge(s_flag, 1)
            return eng.If(eng.value_load(wide[:, :], min_val=0, max_val=1) > 0)

        def numbers(eng, row, at, n, below):
            return nc.values_load_multi_w_load_instructions(row[:, ds(at, n)], engines=(eng.engine,), min_val=0,
                                                            max_val=below - 1)[1]

        @block.sync
        def _(sp):
            loads = [0]

            def load(to, what, done=s_w):
                sp.dma_start(to, what).then_inc(done, 16)
                loads[0] += 1

            sp.dma_start(ends.bitcast(I32), window_ends.rearrange("(o s) w -> o s w", o=1).to_broadcast([NB, 2, EW])
                         ).then_inc(s_ends, 16)
            load(WTs[:, :, :], WT.rearrange("(k p) n -> p k n", p=P), s_watt_in)
            load(Wx[:, :, 0:D], W.rearrange("(k p) n -> p k n", p=P), s_watt_in)
            sp.wait_ge(s_zeroed, 1)
            for h in range(H):
                at = h % 2 * C
                load(att[at:at + C, h // 2, h:h + 1], att_src[h].rearrange("(c o) -> c o", o=1), s_watt_in)
                load(att[at:at + C, h // 2, H + h:H + h + 1], att_dst[h].rearrange("(c o) -> c o", o=1), s_watt_in)

            def load_x(c, s, before):
                wait(sp, s_hps, before)
                sp.dma_start(x_in[:, s, :, :], xv[:, :, ds(c * (CHUNK * P), CHUNK * P)]).then_inc(s_xin[s], 16)

            for c in range(2):
                load_x(c, c, 0)
            load(skw[:, :, :], skip_W.rearrange("(k p) n -> p k n", p=P))
            load(brow[:, :], bias.rearrange("(o n) -> o n", o=1))
            for m, s_part, v_part in ((0, w1_s, w1_v), (1, wsc_s, wsc_v)):
                load(wm[0:MUL, 0, m, 0:MUL], s_part)
                load(wm[MUL:P, 0, m, MUL:P], v_part)
                load(wm[0:MUL, 1, m, 0:MUL], v_part)
                load(wm[MUL:P, 1, m, MUL:P], v_part)
            load(w2m[:, 0, :], w2_s)
            load(w2m[:, 1, :], w2_v)
            for i in range(2):
                load(fc1[i * NBAS:(i + 1) * NBAS, i * MUL:(i + 1) * MUL], fc_w1)
                load(fc2[i * MUL:(i + 1) * MUL, i * MUL:(i + 1) * MUL], fc_w2)
                for to, of in ((0, 0), (1, 2), (2, 1), (3, 3)):
                    load(fc3[i * MUL:(i + 1) * MUL, to * MUL:(to + 1) * MUL], fc_w3[:, of * MUL:(of + 1) * MUL])
            load(gfull[:, 0:MUL], g_s.rearrange("(o n) -> o n", o=1).to_broadcast([P, MUL]))
            for d in range(1, 4):
                load(gfull[:, MUL * d:MUL * (d + 1)], g_v.rearrange("(o n) -> o n", o=1).to_broadcast([P, MUL]))
            load(y_tab[NP:NP + 32, :], zeros[:, 0:D])
            assert loads[0] == N_W_ATT + N_W
            with sp.Fori(1, NCH // 2) as i:
                for s in range(2):
                    load_x(i * 2 + s, s, (i * 2 + s - 1) * CHUNK)

            sp.wait_ge(s_sdf, 3)
            sp.dma_start(src_tab.rearrange("(c p) w e -> p c w e", p=P), sd_parts).then_inc(s_sdst, 16)

            sp.wait_ge(s_hst[0], 16 * (NCH // 2))
            sp.wait_ge(s_hst[1], 16 * (NCH // 2))
            sp.wait_ge(s_sdp, NQ)

            def step_a(g, s, there):
                if there(g + 2):
                    wait(sp, s_f1, g + 1)
                    sp.dma_start(eat[0:2 * NBAS, s % 2, :], one(ea8, g + 2)).then_inc(s_ea[(s + 2) % TURN], 16)
                if there(g):
                    for k in range(GROUP):
                        sp.dma_start(part[k][ds(g * (32 * ZERO), 32 * ZERO), :].rearrange("(p r) d -> p (r d)", p=32),
                                     zeros[:, :]).then_inc(s_zero, 16)
                    wait(sp, s_wev, 6 * (g - 3))
                    sp.dma_start(sh[:, s, :, :], ea4[:, ds(g * GROUP, GROUP), :]).then_inc(s_sh[s], 16)
                n = (s + 1) % TURN
                if there(g + 1):
                    wait(sp, s_ots, g + 2)
                    sp.dma_start(one(ot_tab, g + 1), ots[:, n % 2, 0:PAIR, :].rearrange("p k e -> p (k e)")
                                 ).then_inc(s_otst[n], 16)
                if there(g - 3):
                    wait(sp, s_wev, 6 * (g - 2))
                    sp.dma_start(w_tab[ds((g - 3) * (GROUP * P), GROUP * P), :].rearrange("(k p) d -> p k d", p=P),
                                 wst[:, n % 2, :, :]).then_inc(s_wst[n], 16)

            steps(sp, NG, 2, 3, step_a)
            for s in range(TURN):
                sp.wait_ge(s_wst[s], 16 * (NG // TURN))
                sp.wait_ge(s_otst[s], 16 * (NG // TURN))

            sp.wait_ge(s_acc, GROUP * NG)
            xb = x.rearrange("(b p) d -> b p d", p=P)
            hb = h_tab.rearrange("(b p) d -> b p d", p=P)
            yb = y_tab[0:NP, :].rearrange("(b p) d -> b p d", p=P)

            def step_b(b, s, there):
                n = (s + 3) % TURN
                if there(b + 3):
                    wait(sp, s_bv, b)
                    wait(sp, s_bs, b)
                    wait(sp, s_bskip, b)
                    sp.dma_start(b_h[:, n, :], hb[ds(b + 3, 1), :, 0:D].rearrange("o p d -> (o p) d")
                                 ).then_inc(s_bin[n], 16)
                    sp.dma_start(b_x[:, n, :], one(xb, b + 3)).then_inc(s_bin[n], 16)
                    sp.dma_start(b_xT[:, n, :, :], xv[:, :, ds((b + 3) * P, P)]).then_inc(s_bin[n], 16)
                m = (s - 3) % TURN
                if there(b - 3):
                    wait(sp, s_bout, 2 * (b - 2))
                    sp.dma_start(one(x1b, b - 3), b_x1[:, m, :]).then_inc(s_bst[m], 16)
                    sp.dma_start(one(yb, b - 3), acc[:, ds(b - 3, 1), 0:D].rearrange("p o d -> p (o d)")
                                 ).then_inc(s_bst[m], 16)

            steps(sp, NB, 3, 3, step_b)
            for s in range(TURN):
                sp.wait_ge(s_bst[s], 32 * len(range(s, NB, TURN)))

            wv = w_tab.rearrange("(w p) d -> w p d", p=P)
            otv = ot_tab.rearrange("v p e -> (v p) e")

            def step_c(u, s, there):
                if there(u + 4):
                    if s % 2 == 0:
                        wait(sp, s_cotf, u + 2)
                        sp.dma_start(c_ot[:, s // 2, :, :].rearrange("p k e -> p (k e)"), otv[ds((u + 4) * (P // 2), P), :]
                                     ).then_inc(s_cin[s], 16)
                    wait(sp, s_csr, u + 1)
                    sp.dma_start(c_parts[:, s, :].rearrange("w (k e) -> w k e", k=PAIR),
                                 src_tab[ds((u + 4) * PAIR, PAIR), :, :].rearrange("k w e -> w k e")).then_inc(s_cin[s], 16)
                n = (s + 3) % TURN
                if there(u + 3):
                    w = numbers(sp, window_row, (u + 3) * PAIR, PAIR, EW)
                    wait(sp, s_cmid, u)
                    for k in range(PAIR):
                        sp.dma_start(wt[:, n, k, :], one(wv, w[k])).then_inc(s_cw[n], 16)

            steps(sp, NU, 4, 0, step_c)

            for k in range(GROUP):
                sp.wait_ge(s_add[k], 16 * NG)
            pb = [q[0:NP, :].rearrange("(b p) d -> b p d", p=P) for q in part]

            def step_d(b, s, there):
                if there(b + 4):
                    wait(sp, s_dsum, b + 1)
                    for k in range(GROUP):
                        sp.dma_start(d_p[:, s, k, :], one(pb[k], b + 4)).then_inc(s_din[s], 16)
                n = (s + 2) % TURN
                if there(b + 2):
                    wait(sp, s_dz, b - 1)
                    sp.dma_start(d_x[:, n, :], one(x1b, b + 2)).then_inc(s_dx[n], 16)

            steps(sp, NB, 4, 0, step_d)
            for s in range(TURN):
                sp.wait_ge(s_dst[s], 16 * len(range(s, NB, TURN)))

        @block.gpsimd
        def _(pool):
            g = nc.gpsimd
            g.iota(iota_n[:, :], [[1, P]], base=0, channel_multiplier=0, allow_small_or_imprecise_dtypes=True)
            g.iota(part_no[:, :], [[0, 1]], base=0, channel_multiplier=1, allow_small_or_imprecise_dtypes=True)
            g.iota(trash[:, :], [[0, 1]], base=NP, channel_multiplier=1, allow_small_or_imprecise_dtypes=True)
            g.iota(bounds[:, :], [[P, 2]], base=0, channel_multiplier=P, allow_small_or_imprecise_dtypes=True)
            g.iota(tile_col[:, :], [[P, NC]], base=0, channel_multiplier=1, allow_small_or_imprecise_dtypes=True)
            g.iota(iota_t, [[1, T]], base=0, channel_multiplier=0, allow_small_or_imprecise_dtypes=True)
            g.memset(half[:, :], -0.5).then_inc(s_iota, 1)
            pool.wait_ge(s_win, 1)
            for c in range(NC):
                pool.indirect_dma_start(sd_in[:, c, :, :].rearrange("p w e -> p (w e)"), None, edges_sd,
                                        bass.IndirectOffsetOnAxis(ap=wcol[:, c:c + 1], axis=0)
                                        ).then_inc(s_sdin, 16)
            if BIG > TABLES:
                g.memset(big[:, TABLES:], 0.0).then_inc(s_acc0, 1)
            hv = h_tab.rearrange("(c k p) d -> c p k d", k=CHUNK, p=P)

            def store_h(c, s):
                wait_apart(pool, s_hev, 2 * CHUNK * (c + 1))
                pool.dma_start(hv[ds(c, 1)].rearrange("o p k d -> (o p) k d"), h_out[:, s, :, :]
                               ).then_inc(s_hst[s], 16)

            for c in range(2):
                store_h(c, c)
            with pool.Fori(1, NCH // 2) as i:
                for s in range(2):
                    store_h(i * 2 + s, s)

            pool.wait_ge(s_amax, 1)
            g.partition_all_reduce(gmax[:, :], amax[:, :], P, RMAX).then_inc(s_gmax, 1)
            pool.wait_ge(s_sdp, NQ)
            g.memset(big[:, TABLES - 2 * NC * P:TABLES], 0.0).then_inc(s_acc0, 1)
            pool.wait_ge(s_sdst, 16)
            g.memset(big[:, 2 * EW + 2 * T:2 * EW + 2 * T + NC * P], 0.0).then_inc(s_acc0, 1)
            for s in range(2):
                pool.wait_ge(s_hst[s], 16 * (NCH // 2))
            with when_wide(pool):
                with pool.Fori(0, T) as t:
                    wait_apart(pool, s_mcol, t + 1)
                    pool.indirect_dma_start(m_row, None, h_tab, bass.IndirectOffsetOnAxis(ap=m_idx[:, 0:1], axis=0)
                                            ).then_inc(s_mrow, 16)

            def step_a(g, s, there):
                if there(g):
                    wait_apart(pool, s_idx, g + 1)
                    for k in range(GROUP):
                        wait_apart(pool, s_agg, GROUP * (g - TURN) + k + 1)
                        pool.indirect_dma_start(hg[:, s, k, :], None, h_tab,
                                                bass.IndirectOffsetOnAxis(ap=sidx[:, s, k:k + 1], axis=0)
                                                ).then_inc(s_hg[s], 16)

            steps(pool, NG, 0, 0, step_a)

            pool.wait_ge(s_self, 1)

            def step_b(b, s, there):
                n = (s + 2) % TURN
                if there(b + 2):
                    hs = b_h[:, n, :]
                    hs4 = hs.rearrange("p (h c) -> p h c", h=H)

                    wait_apart(pool, s_bin[n], landed(b + 2, n, 3))
                    g.tensor_tensor(hs4, hs4, pself[:, ds(b + 2, 1), :].rearrange("p o (h c) -> p (o h) c", c=1
                                                                                  ).to_broadcast([P, H, C]),
                                    ALU.mult).then_inc(s_bt, 1)
                    wait_apart(pool, s_bt, 2 * (b + 2) + 1)
                    g.tensor_tensor(hs, hs, acc[:, ds(b + 2, 1), 0:D].rearrange("p o d -> p (o d)"), ALU.add
                                    ).then_inc(s_bt, 1)
                if there(b):
                    wait(pool, s_bmv, 3 * (b + 1))
                    g.tensor_tensor(mv[:, s, 3:4], mv[:, s, 2:3], half[:, 0:1], ALU.pow).then_inc(s_brstd, 1)

            steps(pool, NB, 2, 0, step_b)

            pool.wait_ge(s_zero, 16 * GROUP * NG)
            pool.wait_ge(s_w, 16 * N_W)
            for s in range(TURN):
                pool.wait_ge(s_bst[s], 32 * len(range(s, NB, TURN)))

            def step_c(u, s, there):
                n = (s + 6) % TURN
                if n % 2 and there(u + 6):
                    wait_apart(pool, s_crow, u + 7)
                    wait_apart(pool, s_cmid, u + 3)
                    for k in range(PAIR):
                        pool.indirect_dma_start(c_y[:, n // 2, k, :], None, y_tab,
                                                bass.IndirectOffsetOnAxis(ap=c_row[:, n // 2, k:k + 1], axis=0)
                                                ).then_inc(s_cyg[n // 2], 16)
                if there(u):
                    wait_apart(pool, s_cix, 3 * (u + 1))
                    for k in range(PAIR):
                        q = s % 2 * PAIR + k
                        wait_apart(pool, s_ccmb, u + 1)
                        wait_apart(pool, s_add[q], 8 * u - 8 * (s % 2))
                        pool.indirect_dma_start(part[q], bass.IndirectOffsetOnAxis(ap=c_idx[:, s, k:k + 1], axis=0),
                                                o_cmb[:, q, :], None, compute_op=ALU.add).then_inc(s_add[q], 16)

            steps(pool, NU, 6, 0, step_c)

            ob = out.rearrange("(b p) d -> b p d", p=P)

            def step_d(b, s, there):
                m, n, o = (s - 1) % TURN, (s + 2) % TURN, (s - 3) % TURN
                if there(b - 3):
                    wait_apart(pool, s_dout, 2 * (b - 2))
                    pool.dma_start(one(ob, b - 3), d_out[:, o, :]).then_inc(s_dst[o], 16)
                if there(b):
                    wait(pool, s_dms, b + 1)
                    g.tensor_tensor(d_n[:, s, 4:6], d_n[:, s, 2:4], half[:, 0:2], ALU.pow).then_inc(s_drs, 1)
                if there(b + 2):
                    wait(pool, s_ddeg, b + 3)
                    g.tensor_tensor(d_n[:, n, 1:2], d_n[:, n, 0:1], half[:, 0:1], ALU.pow).then_inc(s_ddn, 1)
                if there(b - 1):
                    wait(pool, s_dmv, 3 * b)
                    g.tensor_tensor(mv[:, m, 3:4], mv[:, m, 2:3], half[:, 0:1], ALU.pow).then_inc(s_drstd, 1)

            steps(pool, NB, 2, 3, step_d)

        @block.scalar
        def _(act):
            a = nc.scalar
            act.wait_ge(s_watt, 1)
            a.copy(Wx[:, :, D:], PS[:, 6, 0:4 * H].rearrange("p (k j) -> p k j", k=2)).then_inc(s_hwatt, 1)

            def evacuate_h(c, s, stored):
                wait_apart(act, s_hst[s], stored)
                for k in range(CHUNK):
                    wait_apart(act, s_hps, CHUNK * c + k + 1)
                    a.copy(h_out[:, s, k, :], PS[:, k, 0:HW]).then_inc(s_hev, 1)
                    a.copy(logits[:, ds(c * CHUNK + k, 1), 0:2 * H].rearrange("p o j -> p (o j)"),
                           PS[:, k, D:D + 2 * H]).then_inc(s_hev, 1)

            for c in range(2):
                evacuate_h(c, c, 0)
            with act.Fori(1, NCH // 2) as i:
                for s in range(2):
                    evacuate_h(i * 2 + s, s, i * 16)

            for q in range(NQ):
                n = min(4, NC - 4 * q) * P
                act.wait_ge(s_sdp, q + 1)
                a.copy(srcF[:, q * 4 * P:q * 4 * P + n], PS[:, q % 2, 0:n]).then_inc(s_sdT, 1)
            with when_wide(act):
                act.wait_ge(s_sdT, NQ)
                with act.Fori(0, T) as t:
                    wait_apart(act, s_mdone, t + 1)
                    a.copy(m_idx[:, :], srcF[:, ds(t, 1)])
                    a.copy(m_dst[:, :], dloc[:, ds(t, 1)]).then_inc(s_mcol, 1)
            act.wait_ge(s_lg, LG_SELF)
            a.activation(pself[:, :, :], lt[:, :, 0:H], ACT.Exp).then_inc(s_self, 1)

            act.wait_ge(s_sdT, NQ)

            def sources(g, s):
                a.copy(sidx[:, s, :], srcF[:, ds(g * GROUP, GROUP)]).then_inc(s_idx, 1)

            def step_a(g, s, there):
                n, m, o = (s + 1) % TURN, (s - 1) % TURN, (s - 3) % TURN

                def radial_weights(i):
                    wait(act, s_f3, 2 * (g - 3) + i + 1)
                    for k in (2 * i, 2 * i + 1):
                        a.mul(wst[:, o % 2, k, 0:2 * MUL], PS[:, 4 + i, k % 2 * D:k % 2 * D + 2 * MUL],
                              sh[:, o, k, 0:1]).then_inc(s_wev, 1)
                    a.copy(wst[:, o % 2, 2 * i:2 * i + 2, 2 * MUL:D],
                           PS[:, 4 + i, :].rearrange("p (k d) -> p k d", k=2)[:, :, 2 * MUL:D]).then_inc(s_wev, 1)

                if there(g - 3):
                    wait(act, s_wst[m], landed(g - 5, m) if there(g - 5) else 0)
                    wait(act, s_sh[o], landed(g - 3, o))
                    a.copy(wst[:, o % 2, :, D:WR], sh[:, o, :, :])
                    radial_weights(0)
                if there(g - 1):
                    wait(act, s_z, 5 * g)
                    a.activation(hg[:, m, :, D:HW], za[:, m % 2, :, :], ACT.Exp).then_inc(s_p, 1)
                if there(g - 3):
                    radial_weights(1)
                if there(g + 3):
                    sources(g + 3, (s + 3) % TURN)
                if there(g - 1):
                    wait(act, s_f2, g)
                    wait(act, s_h2, g - 2)
                    a.activation(t2[:, m % 2, :], PS[:, 7, 0:2 * P], ACT.Tanh, scale=0.5).then_inc(s_t2, 1)
                if there(g + 1):
                    wait(act, s_f1, g + 2)
                    wait(act, s_h1, g)
                    a.activation(t1[:, n % 2, :], PS[:, 6, 0:2 * P], ACT.Tanh, scale=0.5).then_inc(s_t1, 1)
                if there(g + 1):
                    wait(act, s_otp, g + 2)
                    wait(act, s_otst[m], landed(g - 1, m) if there(g - 1) else 0)
                    wait(act, s_ad, g)
                    a.copy(ots[:, n % 2, :, :], otp).then_inc(s_ots, 1)

            steps(act, NG, 3, 3, step_a)

            def step_b(b, s, there):
                m, o, n = (s - 1) % TURN, (s - 2) % TURN, (s + 1) % TURN
                if there(b + 1):
                    wait(act, s_bv, b + 2)
                    wait(act, s_bs, b - 2)
                    a.activation(b_e[:, n, :], b_v[:, n, :], ACT.Relu, scale=-1.0).then_inc(s_bm, 1)
                if there(b + 1):
                    wait(act, s_bm, b + 2)
                    a.activation(b_e[:, n, :], b_e[:, n, :], ACT.Exp, scale=-1.0).then_inc(s_be, 1)
                if there(b - 2):
                    maps = PS[:, 3 + s % 2, :].rearrange("p (j m u) -> p j m u", j=2, m=2)
                    wait(act, s_by, b - 1)
                    a.copy(acc[:, ds(b - 2, 1), 0:D].rearrange("p o (j u) -> p (o j) u", j=2), maps[:, :, 0, :]
                           ).then_inc(s_bout, 1)
                    a.copy(b_x1[:, o, D:].rearrange("p (j u) -> p j u", j=2), maps[:, :, 1, :]).then_inc(s_bout, 1)
                if there(b - 1):
                    wait(act, s_bxp, b)
                    wait(act, s_by, b - 2)
                    a.copy(b_x1T[:, m % 2, :, :], PS[:, 2, 0:256].rearrange("p (k n) -> p k n", k=2)).then_inc(s_bxT, 1)

            steps(act, NB, 1, 2, step_b)

            def step_c(u, s, there):
                n, m, o = (s + 1) % TURN, (s - 1) % TURN, (s + 2) % TURN

                def transposed(k):
                    wait(act, s_coT, u - 2)
                    wait(act, s_cmt, PAIR * (u - 1) + k + 1)
                    a.copy(midT[:, m % 2, k, :, :], PS[:, T_BANK[k], :].rearrange("p (c e) -> p c e", c=4)).then_inc(s_cmT, 1)

                if there(u - 4):
                    q = s % 2 * PAIR
                    wait(act, s_cc, u - 3)
                    for k in range(PAIR):
                        wait(act, s_add[q + k], 8 * (u - 4) - 8 * (s % 2))
                    a.copy(o_cmb[:, q:q + PAIR, :], PS[:, 6:8, 0:OR]).then_inc(s_ccmb, 1)
                if there(u + 1):
                    wait_apart(act, s_cix, 3 * (u - 2))
                    a.copy(c_src[:, n, :], srcF[:, ds((u + 1) * PAIR, PAIR)]).then_inc(s_csl, 1)
                if there(u - 2):
                    wait(act, s_coT, u - 1)
                    wait(act, s_co, u - 2)
                    a.copy(oT_sb[:, :, :], PS[:, 4, :].rearrange("p (j e) -> p j e", j=4)).then_inc(s_coTsb, 1)
                if there(u - 1):
                    transposed(0)
                if o % 2 == 0 and there(u + 2):
                    wait(act, s_cin[o], landed(u + 2, o, 2))
                    wait(act, s_cy, u)
                    a.copy(c_otf[:, o // 2, :, :], c_ot[:, o // 2, :, :]).then_inc(s_cotf, 2)
                if s % 2 and there(u + 4):
                    wait_apart(act, s_cyg[s // 2], landed(u, s, PAIR) if there(u) else 0)
                    a.copy(c_row[:, s // 2, :], y_row[:, ds(u + 3, PAIR)]).then_inc(s_crow, 2)
                if there(u - 1):
                    transposed(1)
                if there(u - 2):
                    wait_apart(act, s_cc, u - 3)
                    a.copy(o_sb[:, s % 2, :, D], valid[:, ds((u - 2) * PAIR, PAIR)])
                    wait(act, s_co, u - 1)
                    a.copy(o_sb[:, s % 2, :, 0:D].rearrange("p k (j u) -> p k j u", j=4),
                           PS[:, 5, :].rearrange("p (j k u) -> p k j u", j=4, k=PAIR)).then_inc(s_cosb, 1)

            steps(act, NU, 4, 4, step_c)

            def step_d(b, s, there):
                n = (s + 1) % TURN
                if there(b + 1):
                    wait(act, s_do, b + 2)
                    wait(act, s_dms, b - 2)
                    a.activation(d_q[:, n, 0:MUL], d_o[:, n, 0:MUL], ACT.Square, scale=float(1 / np.sqrt(MUL)),
                                 accum_out=d_n[:, n, 6:7])
                    a.activation(d_q[:, n, MUL:D], d_o[:, n, MUL:D], ACT.Square, scale=float(1 / np.sqrt(3 * MUL)),
                                 accum_out=d_n[:, n, 7:8]).then_inc(s_dsq, 1)

            steps(act, NB, 1, 0, step_d)

        @block.tensor
        def _(pe):
            mm = nc.tensor.matmul
            pe.wait_ge(s_const, 1)
            pe.wait_ge(s_tab, TAB_WINDOWS)
            mm(PS[0:NB, 7, 64:65], upper[0:NB, 0:NB], cnt[0:NB, 3:4], start=True, stop=True).then_inc(s_tabp, 1)
            pe.wait_ge(s_tab, TAB_STEPS)
            for c in range(NC):
                mm(PS[:, 7, 128 + 2 * c:130 + 2 * c], stepm[:, c * P:(c + 1) * P], two[0:NB, 0:33:32],
                   start=True, stop=True)
            for c in range(-(-T // 512)):
                e = min(T, (c + 1) * 512)
                last = mm(PS[0:33, c, 0:e - c * 512], two[0:NB, :], stepm[:, c * 512:e], start=True, stop=True)
            last.then_inc(s_tabp, 1)
            pe.wait_ge(s_watt_in, 16 * N_W_ATT)
            for k in range(2):
                for m in range(2):
                    last = mm(PS[:, 6, k * 2 * H:(k + 1) * 2 * H], WTs[:, m, k * P:(k + 1) * P], att[:, m, :],
                              start=(m == 0), stop=(m == 1))
            last.then_inc(s_watt, 1)
            pe.wait_ge(s_hwatt, 1)
            pe.wait_ge(s_win, 1)

            def node_maps(c, s, arrived):
                pe.wait_ge(s_xin[s], arrived)
                for k in range(CHUNK):
                    wait(pe, s_hev, 2 * (CHUNK * (c - 1) + k + 1))
                    for j in range(2):
                        last = mm(PS[:, k, 0:D + 2 * H], x_in[:, s, j, k * P:(k + 1) * P], Wx[:, j, :],
                                  start=(j == 0), stop=(j == 1))
                    last.then_inc(s_hps, 1)

            for c in range(2):
                node_maps(c, c, 16)
            with pe.Fori(1, NCH // 2) as i:
                for s in range(2):
                    node_maps(i * 2 + s, s, i * 16 + 16)

            pe.wait_ge(s_hev, 2 * NB)
            pe.wait_ge(s_sdf, SD_PARTS)
            for q in range(NQ):
                if q >= 2:
                    pe.wait_ge(s_sdT, q - 1)
                    pe.wait_ge(s_dl, q - 1)
                for w, z in enumerate((sd_f[:, :, 0, :], sd_f[:, :, 1, :], sd_row)):
                    for c in range(4 * q, min(4 * q + 4, NC)):
                        last = nc.tensor.transpose(PS[:, 2 * w + q % 2, c % 4 * P:(c % 4 + 1) * P], z[:, c, :],
                                                   ident[:, :])
                last.then_inc(s_sdp, 1)

            pe.wait_ge(s_sdT, NQ)
            pe.wait_ge(s_dl, NQ)
            with when_wide(pe):
                with pe.Fori(0, T) as t:
                    pe.wait_ge(s_mcol, t + 1)
                    nc.tensor.transpose(PS[:, 1, 0:P], m_dst[:, 0:1].to_broadcast([P, P]), ident[:, :])
                    pe.wait_ge(s_mrow, t * 16 + 16)
                    for h in range(H):
                        last = nc.tensor.transpose(PS[:, 0, h * P:(h + 1) * P],
                                                   m_row[:, D + h:D + h + 1].to_broadcast([P, P]), ident[:, :])
                    last.then_inc(s_mps, 1)

            pe.wait_ge(s_scaled, 1)
            pe.wait_ge(s_lg, LG_PARTS)

            def step_a(g, s, there):
                n, m, p, o = (s + 1) % TURN, (s - 1) % TURN, (s - 2) % TURN, (s - 3) % TURN

                def third_layer(i):
                    wait(pe, s_h2, g - 2)
                    wait(pe, s_wev, 6 * (g - 4) + 3 * i + 3)
                    for k in range(2):
                        last = mm(PS[:, 4 + i, k * D:(k + 1) * D], h2[i * MUL:(i + 1) * MUL, o % 2, k * P:(k + 1) * P],
                                  fc3[i * MUL:(i + 1) * MUL, :], start=True, stop=True)
                    last.then_inc(s_f3, 1)

                def sums(k):
                    t = GROUP * (g - 2) + k
                    wait(pe, s_msg, t + 1)
                    wait(pe, s_acc, t - 1)
                    mm(PS[:, 2 + k % 2, 0:HW], oh[:, p, k, :], hg[:, p, k, :], start=True, stop=True).then_inc(s_agg, 1)

                if there(g - 3):
                    third_layer(0)
                if there(g - 2):
                    sums(0)
                    sums(1)
                if there(g - 3):
                    third_layer(1)
                if there(g):
                    b = numbers(pe, block_row, g * GROUP, GROUP, NB)
                if there(g - 2):
                    sums(2)
                    sums(3)
                if there(g - 1):
                    wait(pe, s_h1, g)
                    wait(pe, s_h2, g - 1)
                    mm(PS[:, 7, 0:2 * P], fc2[:, :], h1[:, m % 2, :], start=True, stop=True).then_inc(s_f2, 1)
                if there(g + 1):
                    wait(pe, s_ea[n], landed(g + 1, n))
                    wait(pe, s_h1, g + 1)
                    mm(PS[:, 6, 0:2 * P], fc1[:, :], eat[0:2 * NBAS, n % 2, :], start=True, stop=True).then_inc(s_f1, 1)
                if there(g):
                    wait(pe, s_ots, g + 1)
                    wait(pe, s_z, 5 * (g - 1) + 1)
                    for k in range(GROUP):
                        last = mm(PS[:, 1, k * 6 * H:(k + 1) * 6 * H], ots[:, s % 2, k, :],
                                  ac3[:, ds(b[k], 1), :, :].rearrange("p o i j -> p (o i j)"), start=True, stop=True)
                    last.then_inc(s_ad, 1)
                if there(g + 1):
                    wait(pe, s_oh, g + 2)
                    wait(pe, s_ots, g + 1)
                    for k in range(GROUP):
                        last = nc.tensor.transpose(otp[:, k, :], oh[:, n, k, :].bitcast(BF16)[:, 1::2], ident_b[:, :])
                    last.then_inc(s_otp, 1)

            steps(pe, NG, 1, 3, step_a)

            pe.wait_ge(s_acc, GROUP * NG)
            pe.wait_ge(s_wev, 6 * NG)

            def step_b(b, s, there):
                m, n = (s - 1) % TURN, (s + 2) % TURN
                if there(b - 2):
                    wait(pe, s_bxT, b - 1)
                    wait(pe, s_bout, 2 * (b - 3))
                    for j in range(2):
                        last = mm(PS[:, 3 + n % 2, j * D:(j + 1) * D], b_x1T[:, n % 2, j, :],
                                  wm[:, j, :, :].rearrange("p m u -> p (m u)"), start=True, stop=True)
                    last.then_inc(s_by, 1)
                if there(b + 2):
                    wait(pe, s_bin[n], landed(b + 2, n, 3))
                    wait(pe, s_bv, b + 1)
                    mm(PS[:, n % 2, 0:D], b_xT[:, n, 0, :], skw[:, 0, :], start=True, stop=False)
                    mm(PS[:, n % 2, 0:D], b_xT[:, n, 1, :], skw[:, 1, :], start=False, stop=False)
                    mm(PS[:, n % 2, 0:D], ones[0:1, :], brow[:, :], start=False, stop=True).then_inc(s_bskip, 1)
                if there(b - 1):
                    wait(pe, s_bx1, 2 * b)
                    wait(pe, s_bxT, b - 1)
                    for j in range(2):
                        last = nc.tensor.transpose(PS[:, 2, j * P:(j + 1) * P], b_x1[:, m, j * P:(j + 1) * P], ident[:, :])
                    last.then_inc(s_bxp, 1)

            steps(pe, NB, 2, 2, step_b)

            pe.wait_ge(s_bout, 2 * NB)

            def step_c(u, s, there):
                n, m, o = (s + 1) % TURN, (s - 1) % TURN, (s - 3) % TURN

                def transpose(k):
                    wait(pe, s_cmid, u)
                    wait(pe, s_cmT, PAIR * (u - 2) + k + 1)
                    for j in range(4):
                        last = nc.tensor.transpose(PS[:, T_BANK[k], j * P:(j + 1) * P],
                                                   mid[:, m % 2, k, 2 * j:2 * j + 2, :].rearrange("p c u -> p (c u)"),
                                                   ident[:, :])
                    last.then_inc(s_cmt, 1)

                if there(u - 2):
                    wait(pe, s_cmT, PAIR * (u - 1))
                    wait(pe, s_coTsb, u - 2)
                    for first, n_comps in ((0, 1), (1, 3)):
                        for k in range(PAIR):
                            last = mm(PS[k * MUL:(k + 1) * MUL, 4, first * P:(first + n_comps) * P], w2m[:, min(first, 1), :],
                                      midT[:, s % 2, k, first:first + n_comps, :].rearrange("p c e -> p (c e)"),
                                      start=True, stop=True, tile_position=(0, k * MUL))
                    last.then_inc(s_coT, 1)
                if n % 2 == 0 and there(u + 1):
                    b = numbers(pe, block_row, (u + 1) * PAIR, PAIR, NB)
                if there(u - 1):
                    transpose(0)
                if n % 2 == 0 and there(u + 1):
                    wait(pe, s_cotf, u + 3)
                    wait(pe, s_cmid, u)
                    for k in range(PAIR):
                        last = mm(PS[:, 0, k * D:(k + 1) * D], c_otf[:, n // 2, k, :],
                                  acc[:, ds(b[k], 1), 0:D].rearrange("p o d -> p (o d)"), start=True, stop=True)
                    last.then_inc(s_cy, 2)
                if there(u - 1):
                    transpose(1)
                if there(u - 2):
                    wait(pe, s_coTsb, u - 1)
                    wait(pe, s_cosb, u - 2)
                    for j in range(4):
                        last = nc.tensor.transpose(PS[:, 5, j * P:(j + 1) * P], oT_sb[:, j, :], ident[:, :])
                    last.then_inc(s_co, 1)
                if there(u - 3):
                    wait(pe, s_csame, PAIR * (u - 2))
                    wait(pe, s_cosb, u - 2)
                    wait(pe, s_ccmb, u - 3)
                    for k in range(PAIR):
                        last = mm(PS[:, 6 + k, 0:OR], same[:, o, k, :], o_sb[:, o % 2, k, :], start=True, stop=True)
                    last.then_inc(s_cc, 1)
                if there(u + 1):
                    wait(pe, s_cin[n], landed(u + 1, n, 2 - n % 2))
                    wait(pe, s_csame, PAIR * (u + 1))
                    mm(PS[:, 2, 0:PAIR * P], ones_b[:, :], c_parts[:, n, :], start=True, stop=True).then_inc(s_csr, 1)

            steps(pe, NU, 1, 3, step_c)

            pe.wait_ge(s_ccmb, NU)

            def step_d(b, s, there):
                n = (s + 3) % TURN
                if there(b + 3):
                    wait(pe, s_din[n], landed(b + 3, n, GROUP))
                    wait(pe, s_do, b)
                    for k in range(GROUP):
                        last = mm(PS[:, n, 0:OR], ident[:, :], d_p[:, n, k, :], start=(k == 0), stop=(k == GROUP - 1))
                    last.then_inc(s_dsum, 1)

            steps(pe, NB, 3, 0, step_d)

        @block.vector
        def _(dve):
            v = nc.vector
            v.memset(att[:, :, :], 0.0)
            v.memset(wm[:, :, :, :], 0.0)
            for tile in (zeros, fc2, two):
                v.memset(tile[:, :], 0.0)
            v.memset(ones[:, :], 1.0)
            v.memset(ones_b[:, :], 1.0)
            v.memset(fc1[:, :], 0.0).then_inc(s_zeroed, 1)
            dve.wait_ge(s_iota, 1)
            v.tensor_scalar(ident[:, :], iota_n[:, :], part_no[:, 0:1], None, ALU.is_equal)
            v.tensor_scalar(ident_b[:, :], iota_n[:, :], part_no[:, 0:1], None, ALU.is_equal)
            v.tensor_scalar(upper[:, :], iota_n[:, :], part_no[:, 0:1], None, ALU.is_gt)
            v.tensor_scalar(lower_eq[:, :], iota_n[:, :], part_no[:, 0:1], None, ALU.is_le).then_inc(s_const, 1)

            tab = [0]

            def link(ins):
                tab[0] += 1
                ins.then_inc(s_tab, 1)
                dve.wait_ge(s_tab, tab[0])

            dve.wait_ge(s_ends, 16)
            link(v.tensor_copy(ends, ends.bitcast(I32)))
            for col, which, bound in ((0, 1, 0), (1, 0, 1), (2, 1, 1)):
                link(v.tensor_scalar(stepm[:, 0:EW], ends[:, which, :], bounds[0:NB, bound:bound + 1], None,
                                     ALU.is_lt, ALU.add, accum_out=cnt[0:NB, col:col + 1]))
            link(v.tensor_scalar(cnt[0:NB, 3:4], cnt[0:NB, 1:2], cnt[0:NB, 0:1], 0.0, ALU.subtract, ALU.max))
            dve.wait_ge(s_tabp, 1)
            link(v.tensor_tensor(cnt[0:NB, 4:5], PS[0:NB, 7, 64:65], cnt[0:NB, 3:4], ALU.add))
            link(v.tensor_tensor(cnt[0:NB, 5:6], cnt[0:NB, 2:3], cnt[0:NB, 0:1], ALU.subtract))
            v.memset(two[:, 0:1], 1.0)
            v.tensor_tensor(two[0:NB, 32:33], cnt[0:NB, 5:6], cnt[0:NB, 3:4], ALU.subtract)
            link(v.tensor_scalar(stepm, iota_t[0:NB, :], cnt[0:NB, 4:5], None, ALU.is_ge))
            dve.wait_ge(s_tabp, 2)
            flat = PS[:, 0:4, :].rearrange("p b n -> p (b n)")[:, 0:T]
            v.tensor_scalar(block_row, flat[0:1, :], float(NB - 1), None, ALU.min)
            link(v.tensor_tensor(iota_t[32:33, :], flat[32:33, :], iota_t[32:33, :], ALU.add))
            v.tensor_scalar(window_row, iota_t[32:33, :], float(EW - 1), None, ALU.min)
            cols = PS[:, 7, 128:128 + 2 * NC].rearrange("p (c j) -> p c j", j=2)
            v.tensor_scalar(b128[:, :], cols[:, :, 0], float(P), None, ALU.mult)
            link(v.tensor_tensor(tile_col[:, :], cols[:, :, 1], tile_col[:, :], ALU.add))
            v.tensor_scalar(wcol[:, :], tile_col[:, :], float(EW - 1), None, ALU.min).then_inc(s_win, 1)
            dve.wait_ge(s_win, 1)
            v.memset(big[:, 0:2 * EW + 2 * T], 0.0).then_inc(s_acc0, 1)

            dve.wait_ge(s_w, 16 * N_W)
            v.tensor_scalar(wm[:, :, :, :], wm[:, :, :, :], S64, None, ALU.mult)
            v.tensor_scalar(fc3[:, :], fc3[:, :], S64 / 2, None, ALU.mult)
            v.tensor_scalar(fc2[:, :], fc2[:, :], S64 / 2, None, ALU.mult)
            v.tensor_scalar(fc1[:, :], fc1[:, :], S8, None, ALU.mult)
            v.tensor_scalar(w2m[MUL:P, 0, :], w2m[MUL:P, 0, :], INV_SQRT3, None, ALU.mult).then_inc(s_scaled, 1)

            dve.wait_ge(s_sdin, 16 * NC)
            v.tensor_copy(sd_f[:, :, 0, :], sd_in[:, :, 0, :])
            v.tensor_tensor(sd_f[:, :, 1, :], sd_in[:, :, 1, :],
                            b128[:, :].rearrange("p (c o) -> p c o", o=1).to_broadcast([P, NC, P]),
                            ALU.subtract).then_inc(s_sdf, 1)
            dve.wait_ge(s_sdf, 1)
            v.tensor_copy(sd_parts[:, :, 0, :], sd_f[:, :, 0, :]).then_inc(s_sdf, 1)
            dve.wait_ge(s_sdf, 2)
            v.tensor_tensor(sd_parts[:, :, 1, :], sd_f[:, :, 0, :], sd_parts[:, :, 0, :], ALU.subtract).then_inc(s_sdf, 1)
            dl = sd_f[:, :, 1, :]
            v.tensor_scalar(sd_row, dl, 0.0, None, ALU.is_ge).then_inc(s_sdf, 1)
            v.tensor_tensor(sd_dst, dl, b128[:, :].rearrange("p (c o) -> p c o", o=1).to_broadcast([P, NC, P]), ALU.add
                            ).then_inc(s_sdf, 1)
            dve.wait_ge(s_sdf, 4)
            v.scalar_tensor_tensor(sd_row, dl, float(P), sd_row, ALU.is_lt, ALU.mult).then_inc(s_sdf, 1)
            dve.wait_ge(s_sdf, 6)
            v.scalar_tensor_tensor(sd_row, sd_dst, -float(NP), sd_row, ALU.add, ALU.mult).then_inc(s_sdf, 1)
            dve.wait_ge(s_sdf, SD_PARTS)
            v.memset(big[:, 2 * EW + 2 * T + NC * P:TABLES - 2 * NC * P], 0.0).then_inc(s_acc0, 1)

            dve.wait_ge(s_hev, 2 * NB)
            lg = [0]

            def link_lg(ins):
                lg[0] += 1
                ins.then_inc(s_lg, 1)
                dve.wait_ge(s_lg, lg[0])

            def leaky(to, z):
                return v.scalar_tensor_tensor(to, z, SLOPE, z, ALU.mult, ALU.max)

            a_src = logits[:, :, 0:H]
            top = logits[:, :, 2 * H:]
            v.tensor_reduce(amax[:, 0:H], a_src.rearrange("p b h -> p h b"), AX.X, ALU.max)
            link_lg(v.tensor_scalar(lt[:, :, 0:H], a_src, -1.0, None, ALU.mult))
            v.tensor_reduce(amax[:, H:], lt[:, :, 0:H].rearrange("p b h -> p h b"), AX.X, ALU.max).then_inc(s_amax, 1)
            dve.wait_ge(s_gmax, 1)
            link_lg(v.tensor_copy(top, gmax[:, 0:H].rearrange("p (o h) -> p o h", o=1).to_broadcast([P, NB, H])))
            link_lg(v.tensor_tensor(m_red[0:1, :], gmax[0:1, 0:H], gmax[0:1, H:], ALU.add))
            link_lg(v.tensor_reduce(spread[:, 0:1], m_red[0:1, :], AX.X, ALU.max))
            v.tensor_scalar(wide[:, :], spread[:, 0:1], RANGE, None, ALU.is_gt).then_inc(s_flag, 1)

            for q in range(NQ):
                n = min(4, NC - 4 * q) * P
                dve.wait_ge(s_sdp, q + 1)
                v.tensor_scalar(dloc[:, q * 4 * P:q * 4 * P + n], PS[:, 2 + q % 2, 0:n], -1.0, float(P), ALU.max,
                                ALU.min)
                odd = PS[:, 4 + q % 2, 0:n].rearrange("p (v o k) -> p v o k", o=2, k=PAIR)[:, :, 1, :]
                v.tensor_scalar(y_row[:, q * 2 * P:q * 2 * P + n // 2].rearrange("p (v k) -> p v k", k=PAIR), odd,
                                float(NP), None, ALU.add).then_inc(s_dl, 1)
            with when_wide(dve):
                dve.wait_ge(s_dl, NQ)
                v.tensor_copy(top, a_src).then_inc(s_mdone, 1)
                with dve.Fori(0, T) as t:
                    b = dve.value_load(block_row[:, ds(t, 1)], min_val=0, max_val=NB - 1)
                    dve.wait_ge(s_mps, t + 1)
                    v.tensor_scalar(m_out, PS[:, 1, 0:P], part_no[:, 0:1], -HUGE, ALU.not_equal, ALU.mult).then_inc(s_mc, 1)
                    dve.wait_ge(s_mc, t * 3 + 1)
                    v.tensor_tensor(m_val, PS[:, 0, :].rearrange("p (h e) -> p h e", h=H),
                                    m_out.rearrange("p (o e) -> p o e", o=1).to_broadcast([P, H, P]), ALU.add
                                    ).then_inc(s_mc, 1)
                    dve.wait_ge(s_mc, t * 3 + 2)
                    v.tensor_reduce(m_red[:, :], m_val, AX.X, ALU.max).then_inc(s_mc, 1)
                    dve.wait_ge(s_mc, t * 3 + 3)
                    dve.wait_ge(s_mdone, t + 1)
                    x = logits[:, ds(b, 1), 2 * H:].rearrange("p o h -> p (o h)")
                    v.tensor_tensor(x, x, m_red[:, :], ALU.max).then_inc(s_mdone, 1)
                dve.wait_ge(s_mdone, T + 1)

            link_lg(v.tensor_tensor(lt[:, :, H:], logits[:, :, H:2 * H], top, ALU.add))
            link_lg(leaky(top, lt[:, :, H:]))
            link_lg(v.tensor_copy(ac3[:, :, 0, :], logits[:, :, H:]))
            link_lg(v.tensor_tensor(lt[:, :, :], logits[:, :, H:], ac3[:, :, 0, :], ALU.subtract))
            link_lg(v.tensor_copy(ac3[:, :, 1, :], lt[:, :, :]))
            link_lg(v.tensor_tensor(ac3[:, :, 2, :], lt[:, :, :], ac3[:, :, 1, :], ALU.subtract))
            assert lg[0] == LG_PARTS
            link_lg(v.tensor_tensor(lt[:, :, 0:H], a_src, logits[:, :, H:2 * H], ALU.add))
            link_lg(leaky(lt[:, :, 0:H], lt[:, :, 0:H]))
            link_lg(v.tensor_tensor(lt[:, :, 0:H], lt[:, :, 0:H], top, ALU.subtract))
            assert lg[0] == LG_SELF

            dve.wait_ge(s_dl, NQ)
            v.tensor_scalar(valid[:, :], dloc[:, :], 0.0, None, ALU.is_ge).then_inc(s_dl, 1)
            dve.wait_ge(s_dl, NQ + 1)
            v.scalar_tensor_tensor(valid[:, :], dloc[:, :], float(P), valid[:, :], ALU.is_lt, ALU.mult).then_inc(s_dl, 1)

            for s in range(2):
                dve.wait_ge(s_hst[s], 16 * (NCH // 2))
            dve.wait_ge(s_acc0, 5 if BIG > TABLES else 4)

            def step_a(g, s, there):
                n, m, o = (s + 2) % TURN, (s - 1) % TURN, (s - 2) % TURN

                def half_silu(to, t, z):
                    return v.scalar_tensor_tensor(to, t, 1.0, z, ALU.add, ALU.mult)

                def message(k):
                    x = hg[:, o, k, 0:D].rearrange("p (h c) -> p h c", h=H)
                    v.tensor_tensor(x, x, hg[:, o, k, D:HW].rearrange("p (h o) -> p h o", o=1).to_broadcast([P, H, C]),
                                    ALU.mult).then_inc(s_msg, 1)

                def add_up(k):
                    t = GROUP * (g - 2) + k
                    wait(dve, s_agg, t + 1)
                    wait(dve, s_acc, t)
                    x = acc[:, ds(b[k], 1), :].rearrange("p o d -> p (o d)")
                    v.tensor_tensor(x, x, PS[:, 2 + k % 2, 0:HW], ALU.add).then_inc(s_acc, 1)

                if there(g - 2):
                    wait(dve, s_p, g - 1)
                    message(0)
                    message(1)
                    message(2)
                    b = numbers(dve, block_row, (g - 2) * GROUP, GROUP, NB)
                if there(g - 1):
                    wait(dve, s_ad, g)
                    v.tensor_reduce(ad[:, m % 2, :, :],
                                    PS[:, 1, 0:GROUP * 6 * H].rearrange("p (k i j) -> p k j i", k=GROUP, i=3),
                                    AX.X, ALU.add).then_inc(s_z, 1)
                if there(g):
                    wait(dve, s_t1, g + 1)
                    wait(dve, s_f2, g - 1)
                    half_silu(h1[:, s % 2, :], t1[:, s % 2, :], PS[:, 6, 0:2 * P]).then_inc(s_h1, 1)
                if there(g - 1):
                    wait(dve, s_hg[m], landed(g - 1, m, GROUP))
                    wait(dve, s_z, 5 * g - 4)
                    v.tensor_tensor(za[:, m % 2, :, :], hg[:, m, :, D:HW], ad[:, m % 2, :, 0:H], ALU.add).then_inc(s_z, 1)
                if there(g - 2):
                    add_up(0)
                if there(g - 1):
                    wait(dve, s_z, 5 * g - 3)
                    leaky(zb[:, m % 2, :, :], za[:, m % 2, :, :]).then_inc(s_z, 1)
                if there(g - 2):
                    message(3)
                if there(g - 1):
                    wait(dve, s_z, 5 * g - 2)
                    v.tensor_tensor(za[:, m % 2, :, :], zb[:, m % 2, :, :], ad[:, m % 2, :, H:], ALU.subtract
                                    ).then_inc(s_z, 1)
                if there(g - 2):
                    add_up(1)
                    wait(dve, s_t2, g - 1)
                    wait(dve, s_f3, 2 * (g - 3))
                    half_silu(h2[:, o % 2, :], t2[:, o % 2, :], PS[:, 7, 0:2 * P]).then_inc(s_h2, 1)
                    add_up(2)
                if there(g - 1):
                    wait(dve, s_z, 5 * g - 1)
                    v.tensor_scalar(za[:, m % 2, :, :], za[:, m % 2, :, :], 0.0, None, ALU.min).then_inc(s_z, 1)
                if there(g - 2):
                    add_up(3)
                if there(g + 2):
                    wait(dve, s_agg, GROUP * (g - 1))
                    v.tensor_tensor(oh[:, n, :, :],
                                    iota_n[:, :].rearrange("p (o n) -> p o n", o=1).to_broadcast([P, GROUP, P]),
                                    dloc[:, ds((g + 2) * GROUP, GROUP)].rearrange("p (k o) -> p k o", o=1
                                                                                  ).to_broadcast([P, GROUP, P]),
                                    ALU.is_equal).then_inc(s_oh, 1)

            steps(dve, NG, 2, 2, step_a)

            dve.wait_ge(s_acc, T)
            dve.wait_ge(s_self, 1)
            v.tensor_tensor(rden[:, :, :], acc[:, :, D:HW], pself[:, :, :], ALU.add).then_inc(s_rden, 1)
            dve.wait_ge(s_rden, 1)
            v.reciprocal(rden[:, :, :], rden[:, :, :]).then_inc(s_rden, 1)
            dve.wait_ge(s_rden, 2)

            def mean_and_variance(s, b, done):
                wait_apart(dve, done, 3 * b + 1)
                v.bn_aggr(mv[:, s, 0:2], stat[:, s, :]).then_inc(done, 1)

            def variance_plus_eps(s, b, done):
                wait(dve, done, 3 * b + 2)
                v.tensor_scalar(mv[:, s, 2:3], mv[:, s, 1:2], EPS, None, ALU.add).then_inc(done, 1)

            def normalized(to, of, s):
                return v.tensor_scalar(to, of, mv[:, s, 0:1], mv[:, s, 3:4], ALU.subtract, ALU.mult)

            def step_b(b, s, there):
                n, m = (s + 1) % TURN, (s - 1) % TURN
                if there(b + 1):
                    hs4 = b_h[:, n, :].rearrange("p (h c) -> p h c", h=H)
                    wait_apart(dve, s_bt, 2 * (b + 2))
                    v.tensor_tensor(hs4, hs4, rden[:, ds(b + 1, 1), :].rearrange("p o (h c) -> p (o h) c", c=1
                                                                                 ).to_broadcast([P, H, C]),
                                    ALU.mult).then_inc(s_bsum, 1)
                if there(b):
                    wait(dve, s_be, b + 1)
                    v.scalar_tensor_tensor(b_e[:, s, :], b_e[:, s, :], -1.0, b_x[:, s, :], ALU.add, ALU.add
                                           ).then_inc(s_belu, 1)
                if there(b + 1):
                    wait(dve, s_bsum, b + 2)
                    wait(dve, s_bskip, b + 2)
                    v.tensor_tensor(b_v[:, n, :], b_h[:, n, :], PS[:, n % 2, 0:D], ALU.add).then_inc(s_bv, 1)
                if there(b):
                    wait(dve, s_belu, b + 1)
                    v.scalar_tensor_tensor(b_v[:, s, :], b_v[:, s, :], 0.0, b_e[:, s, :], ALU.max, ALU.add
                                           ).then_inc(s_bs, 1)
                if there(b - 1):
                    wait(dve, s_brstd, b)
                    wait(dve, s_bst[m], landed(b - 5, m, 2) if there(b - 5) else 0)
                    normalized(b_x1[:, m, 0:MUL], b_v[:, m, 0:MUL], m).then_inc(s_bx1, 1)
                if there(b):
                    wait(dve, s_bs, b + 1)
                    v.bn_stats(stat[:, s, :], b_v[:, s, :]).then_inc(s_bmv, 1)
                if there(b - 1):
                    normalized(b_x1[:, m, MUL:D].rearrange("p (d u) -> p d u", d=3),
                               b_v[:, m, MUL:D].rearrange("p (u d) -> p d u", d=3), m).then_inc(s_bx1, 1)
                if there(b):
                    mean_and_variance(s, b, s_bmv)
                    variance_plus_eps(s, b, s_bmv)

            steps(dve, NB, 1, 1, step_b)

            def step_c(u, s, there):
                m = (s - 2) % TURN
                if there(u):
                    wait(dve, s_csr, u + 1)
                    wait(dve, s_csl, u + 1)
                    wait(dve, s_cc, u - 3)
                    for k in range(PAIR):
                        v.scalar_tensor_tensor(same[:, s, k, :], PS[:, 2, k * P:(k + 1) * P],
                                               c_src[:, s, k:k + 1], lower_eq[:, :], ALU.is_equal, ALU.mult,
                                               accum_out=c_cnt[:, s, k:k + 1]).then_inc(s_csame, 1)
                    y = (c_y[:, s // 2, :, :] if s % 2 else PS[:, 0, :].rearrange("p (k d) -> p k d", k=PAIR)
                         ).rearrange("p k (d u) -> p k d u", d=4)
                    w = wt[:, s, :, 0:D].rearrange("p k (a b u) -> p k a b u", a=2, b=2)
                    sh1 = wt[:, s, :, D + 1:D + 4].rearrange("p k (d o) -> p k d o", o=1).to_broadcast([P, PAIR, 3, MUL])
                    q = mid[:, s % 2, :, 1, :]
                    if s % 2:
                        wait(dve, s_cyg[s // 2], landed(u, s, PAIR))
                    else:
                        wait(dve, s_cy, u + 2)
                    wait(dve, s_cw[s], landed(u, s, PAIR))
                    wait(dve, s_cmt, PAIR * (u - 1))

                    def spread(z):
                        return z.rearrange("p k (o u) -> p k o u", o=1).to_broadcast([P, PAIR, 3, MUL])

                    v.tensor_tensor(evs[:, :, :, :], y[:, :, 1:4, :], sh1, ALU.mult).then_inc(s_cpr, 1)
                    v.tensor_tensor(mid[:, s % 2, :, 0:2, :], w[:, :, :, 0, :],
                                    y[:, :, 0:1, :].to_broadcast([P, PAIR, 2, MUL]), ALU.mult).then_inc(s_cpr, 1)
                if there(u - 2):
                    v.tensor_scalar(c_d[:, m, :], c_src[:, m, :], -1.0, trash[:, 0:1], ALU.mult, ALU.add
                                    ).then_inc(s_cix, 1)
                if there(u):
                    wait(dve, s_cpr, 5 * u + 1)
                    v.tensor_tensor(evt[:, :, :], evs[:, :, 0, :], evs[:, :, 1, :], ALU.add).then_inc(s_cpr, 1)
                    wait(dve, s_cpr, 5 * u + 2)
                    v.tensor_tensor(mid[:, s % 2, :, 2:8:2, :], spread(q), sh1, ALU.mult).then_inc(s_cpr, 1)
                    v.tensor_tensor(mid[:, s % 2, :, 3:8:2, :], y[:, :, 1:4, :], spread(w[:, :, 0, 1, :]), ALU.mult)
                    wait(dve, s_cpr, 5 * u + 3)
                    v.tensor_tensor(evt[:, :, :], evt[:, :, :], evs[:, :, 2, :], ALU.add).then_inc(s_cpr, 1)
                if there(u - 2):
                    wait(dve, s_cix, 3 * u - 5)
                    wait(dve, s_csame, PAIR * (u - 1))
                    v.scalar_tensor_tensor(c_d[:, m, :], c_cnt[:, m, :], 1.5, c_d[:, m, :], ALU.is_gt, ALU.mult
                                           ).then_inc(s_cix, 1)
                if there(u):
                    wait(dve, s_cpr, 5 * u + 5)
                    v.tensor_tensor(q, evt[:, :, :], w[:, :, 1, 1, :], ALU.mult).then_inc(s_cmid, 1)
                if there(u - 2):
                    wait(dve, s_cix, 3 * u - 4)
                    for k in range(PAIR):
                        wait(dve, s_add[m % 2 * PAIR + k], 8 * (u - 6) + 16 - 8 * (m % 2) if there(u - 6) else 0)
                    v.tensor_tensor(c_idx[:, m, :], c_d[:, m, :], c_src[:, m, :], ALU.add).then_inc(s_cix, 1)

            steps(dve, NU, 0, 2, step_c)

            def step_d(b, s, there):
                n2, n, m = (s + 2) % TURN, (s + 1) % TURN, (s - 1) % TURN
                if there(b - 1):
                    wait(dve, s_drs, b)
                    v.scalar_tensor_tensor(d_z[:, m, 0:MUL], d_o[:, m, 0:MUL], d_n[:, m, 4:5], gfull[:, 0:MUL],
                                           ALU.mult, ALU.mult).then_inc(s_dn, 1)
                    v.scalar_tensor_tensor(d_z[:, m, MUL:D], d_o[:, m, MUL:D], d_n[:, m, 5:6], gfull[:, MUL:D],
                                           ALU.mult, ALU.mult).then_inc(s_dn, 1)
                if there(b + 1):
                    wait(dve, s_ddn, b + 2)
                    wait(dve, s_dx[n], landed(b + 1, n))
                    v.scalar_tensor_tensor(d_o[:, n, :], PS[:, n, 0:D], d_n[:, n, 1:2], d_x[:, n, D:], ALU.mult,
                                           ALU.add).then_inc(s_do, 1)
                if there(b):
                    wait(dve, s_dsq, b + 1)
                    v.tensor_scalar(d_n[:, s, 2:4], d_n[:, s, 6:8], EPS, None, ALU.add).then_inc(s_dms, 1)
                if there(b - 1):
                    wait(dve, s_dn, 2 * b)
                    v.tensor_tensor(d_z[:, m, :], d_z[:, m, :], d_x[:, m, 0:D], ALU.add).then_inc(s_dz, 1)
                if there(b + 2):
                    wait(dve, s_dsum, b + 3)
                    v.tensor_scalar(d_n[:, n2, 0:1], PS[:, n2, D:D + 1], 1.0, float(2 * MUL), ALU.max, ALU.mult
                                    ).then_inc(s_ddeg, 1)
                if there(b - 2):
                    wait(dve, s_drstd, b - 1)
                    wait(dve, s_dst[n2], landed(b - 6, n2) if there(b - 6) else 0)
                    normalized(d_out[:, n2, 0:MUL], d_z[:, n2, 0:MUL], n2).then_inc(s_dout, 1)
                if there(b - 1):
                    wait(dve, s_dz, b)
                    v.bn_stats(stat[:, m, :], d_z[:, m, :]).then_inc(s_dmv, 1)
                if there(b - 2):
                    normalized(d_out[:, n2, MUL:D].rearrange("p (u d) -> p d u", d=3),
                               d_z[:, n2, MUL:D].rearrange("p (d u) -> p d u", d=3), n2).then_inc(s_dout, 1)
                if there(b - 1):
                    mean_and_variance(m, b - 1, s_dmv)
                if there(b - 1):
                    variance_plus_eps(m, b - 1, s_dmv)

            steps(dve, NB, 2, 2, step_d)


_WEIGHTS = ["bias", "skip_W", "w1_s", "w1_v", "wsc_s", "wsc_v", "w2_s", "w2_v", "fc_w1", "fc_w2", "fc_w3", "g_s", "g_v"]


def kernel(**inputs):
    import concourse.bacc as bacc
    from concourse.bass_utils import run_bass_kernel_spmd

    a = {k: np.asarray(v) for k, v in inputs.items()}
    x, src, dst = a["x"], a["src"], a["dst"]
    n, e = x.shape[0], src.shape[0]
    nb, np_, ew, t = sizes(n, e)
    w = {k: a.get("L0_gnn_" + k, a.get("L1_gnn_" + k)) for k in _WEIGHTS}
    xp = np.zeros((np_, x.shape[1]), x.dtype)
    xp[:n] = x
    sd = np.zeros((2, ew * P), src.dtype)
    sd[1] = NO_NODE
    sd[0, :e], sd[1, :e] = src, dst
    sd = sd.reshape(2, ew, P)
    ea8 = np.zeros((t * P, a["edge_attr_8"].shape[1]), x.dtype)
    ea8[:e] = a["edge_attr_8"]
    ea4 = np.zeros((t * P, 4), x.dtype)
    ea4[:e] = a["edge_attr_4"]
    arrays = {
        "x": xp,
        "xT": np.ascontiguousarray(xp.T),
        "edges_sd": np.ascontiguousarray(sd.transpose(1, 0, 2)).reshape(ew, 2 * P),
        "window_ends": np.ascontiguousarray(sd[1][:, [0, P - 1]].T),
        "ea8": np.ascontiguousarray(ea8.reshape(t // 4, 2, 2 * P, -1).transpose(0, 1, 3, 2)).reshape(t // 4, -1, 2 * P),
        "ea4": np.ascontiguousarray(ea4.reshape(t, P, 4).transpose(1, 0, 2)),
        "W": a["L0_gnn_W"],
        "WT": np.ascontiguousarray(a["L0_gnn_W"].T),
        "att_src": a["L0_gnn_att_src"],
        "att_dst": a["L0_gnn_att_dst"],
        **w,
    }
    nc = bacc.Bacc("TRN2", target_bir_lowering=False, num_devices=1)
    aps = {k: nc.dram_tensor(f"in_{k}", v.shape, mybir.dt.from_np(v.dtype), kind="ExternalInput").ap()
           for k, v in arrays.items()}
    out = nc.dram_tensor("out", [np_, x.shape[1]], F32, kind="ExternalOutput").ap()
    bass_gat_equivariant_kernel(nc, out=out, n_nodes=n, n_edges=e, **aps)
    r = run_bass_kernel_spmd(nc, [{f"in_{k}": v for k, v in arrays.items()}], core_ids=[0])
    return r.results[0]["out"][:n]
```
